# Optimizing a Trainium2 kernel written in Bass

```python
import numpy as np
import jax
import jax.numpy as jnp

def _softmax(x, axis=-1):
    return jax.nn.softmax(x, axis=axis)

def _gelu(x):
    return jax.nn.gelu(x, approximate=True)

def _silu(x):
    return jax.nn.silu(x)

def _sigmoid(x):
    return jax.nn.sigmoid(x)

def _layernorm(x, axis=-1, eps=1e-05):
    m = jnp.mean(x, axis=axis, keepdims=True)
    v = jnp.var(x, axis=axis, keepdims=True)
    return (x - m) / jnp.sqrt(v + eps)

def _scatter_add(tgt, idx, src, axis=0):
    return tgt.at[idx].add(src)

def _segment_sum(src, seg, n):
    return jax.ops.segment_sum(src, seg, n)
kernel_name = 'mk_early_fusion_d2_tok_img512_r4_1bf166'

def setup_inputs(seed: int=0):
    np.random.seed(seed)
    _w = jnp.asarray

    def _rec_inputs():
        import jax
        import jax.numpy as jnp
        _rk = jax.random.key(seed)
        x = -0.000356955 + 1 * jax.random.normal(jax.random.fold_in(_rk, 1), (32, 3, 96, 96), jnp.float32)
        txt = -3.85354e-11 + 0.999983 * jax.random.normal(jax.random.fold_in(_rk, 2), (32, 77, 128), jnp.float32)
        return (x, txt)
    x, txt = _rec_inputs()

    def _L0_tok_setup():
        import jax, jax.numpy as jnp
        import numpy as np
        P = 16
        SHIFT = P // 2
        EPS = 1e-05

        def _shift2d(img, dy, dx):
            H, W = (img.shape[2], img.shape[3])
            pad = ((0, 0), (0, 0), (max(dy, 0), max(-dy, 0)), (max(dx, 0), max(-dx, 0)))
            z = jnp.pad(img, pad)
            return z[:, :, max(-dy, 0):max(-dy, 0) + H, max(-dx, 0):max(-dx, 0) + W]

        def _patchify(img):
            B, C, H, W = img.shape
            nH, nW = (H // P, W // P)
            t = img.reshape(B, C, nH, P, nW, P).transpose(0, 2, 4, 1, 3, 5)
            return t.reshape(B, nH * nW, C * P * P)
        key = jax.random.key(seed)
        ks = jax.random.split(key, 8)
        B, C, H, Wd = (128, 3, 224, 224)
        embed_dim = 128
        d_main = embed_dim // 2
        d_shift = embed_dim // 8
        fan_in = C * P * P
        std = 0.02
        x = jax.random.normal(ks[0], (B, C, H, Wd), dtype=jnp.float32)
        W_main = jax.random.normal(ks[1], (d_main, fan_in), dtype=jnp.float32) * std
        b_main = jnp.zeros((d_main,), dtype=jnp.float32)
        W_sx = jax.random.normal(ks[2], (d_shift, fan_in), dtype=jnp.float32) * std
        b_sx = jnp.zeros((d_shift,), dtype=jnp.float32)
        W_sy = jax.random.normal(ks[3], (d_shift, fan_in), dtype=jnp.float32) * std
        b_sy = jnp.zeros((d_shift,), dtype=jnp.float32)
        ln_g = jnp.ones((embed_dim,), dtype=jnp.float32)
        ln_b = jnp.zeros((embed_dim,), dtype=jnp.float32)
        return {'x': x, 'W_main': W_main, 'b_main': b_main, 'W_sx': W_sx, 'b_sx': b_sx, 'W_sy': W_sy, 'b_sy': b_sy, 'ln_g': ln_g, 'ln_b': ln_b}
    _L0_tok_all = _L0_tok_setup()
    _L0_tok_in = {k: v for k, v in _L0_tok_all.items() if k in ('W_main', 'b_main', 'W_sx', 'b_sx', 'W_sy', 'b_sy', 'ln_g', 'ln_b')}
    del _L0_tok_all

    def _L0_attn_setup():
        import math
        import jax, jax.numpy as jnp
        import numpy as np
        B, N, D = (2, 192, 128)
        H = 8
        DK = D // H
        BETA_NOT = 0.5
        EPS = 1e-06

        def _qkv(x, w):
            b, n, d = x.shape
            qkv = (x @ w).reshape(b, n, 3, H, DK).transpose(2, 0, 3, 1, 4)
            return (qkv[0], qkv[1], qkv[2])
        key = jax.random.key(seed)
        ks = jax.random.split(key, 8)
        s = 0.02
        return {'x': jax.random.normal(ks[0], (B, N, D), dtype=jnp.float32), 'qkv1_w': jax.random.normal(ks[1], (D, 3 * D), dtype=jnp.float32) * s, 'qkv2_w': jax.random.normal(ks[2], (D, 3 * D), dtype=jnp.float32) * s, 'proj_w': jax.random.normal(ks[3], (D, D), dtype=jnp.float32) * s, 'conv1_w': jax.random.normal(ks[4], (16, 6), dtype=jnp.float32) * 0.3, 'conv1_b': jax.random.normal(ks[5], (16,), dtype=jnp.float32) * 0.1, 'conv2_w': jax.random.normal(ks[6], (4, 16), dtype=jnp.float32) * 0.3, 'conv2_b': jnp.full((4,), -5.0, dtype=jnp.float32), 'chain_logit': jnp.asarray(-2.0, dtype=jnp.float32)}
    _L0_attn_all = _L0_attn_setup()
    _L0_attn_in = {k: v for k, v in _L0_attn_all.items() if k in ('qkv1_w', 'qkv2_w', 'proj_w', 'conv1_w', 'conv1_b', 'conv2_w', 'conv2_b', 'chain_logit')}
    del _L0_attn_all

    def _L0_ffn_setup():
        import jax, jax.numpy as jnp
        import numpy as np
        B, L, H, E, F, C = (8, 2048, 128, 8, 256, 2)
        key = jax.random.key(seed)
        ks = jax.random.split(key, 4)
        x = jax.random.normal(ks[0], (B, L, H), jnp.float32)
        Wg = jax.random.normal(ks[1], (H, E), jnp.float32) * H ** (-0.5)
        W1 = jax.random.normal(ks[2], (E, H, F), jnp.float32) * H ** (-0.5)
        b1 = jnp.zeros((E, F), jnp.float32)
        W2 = jax.random.normal(ks[3], (E, F, H), jnp.float32) * F ** (-0.5)
        b2 = jnp.zeros((E, H), jnp.float32)
        return {'x': x, 'Wg': Wg, 'W1': W1, 'b1': b1, 'W2': W2, 'b2': b2}
    _L0_ffn_all = _L0_ffn_setup()
    _L0_ffn_in = {k: v for k, v in _L0_ffn_all.items() if k in ('Wg', 'W1', 'b1', 'W2', 'b2')}
    del _L0_ffn_all

    def _L1_attn_setup():
        import jax, jax.numpy as jnp
        import numpy as np
        import math
        B, T, C = (8, 256, 128)
        H = 8
        HD = C // H
        MAX_REL = 64 + 4

        def _rel_index(t):
            r = jnp.arange(t)
            dist = jnp.clip(r[None, :] - r[:, None], -MAX_REL, MAX_REL)
            return dist + MAX_REL
        key = jax.random.key(seed)
        ks = jax.random.split(key, 12)
        xavier = lambda k, shape: jax.random.uniform(k, shape, jnp.float32, -1.0, 1.0) * math.sqrt(6.0 / (shape[0] + shape[1]))
        return {'x': jax.random.normal(ks[0], (B, T, C), jnp.float32), 'Wq': xavier(ks[1], (C, C)), 'bq': jnp.zeros((C,), jnp.float32), 'Wk': xavier(ks[2], (C, C)), 'bk': jnp.zeros((C,), jnp.float32), 'Wv': xavier(ks[3], (C, C)), 'bv': jnp.zeros((C,), jnp.float32), 'Wo': xavier(ks[4], (C, C)), 'bo': jnp.zeros((C,), jnp.float32), 'rel_k': xavier(ks[5], (2 * MAX_REL + 1, HD)), 'rel_v': xavier(ks[6], (2 * MAX_REL + 1, HD))}
    _L1_attn_all = _L1_attn_setup()
    _L1_attn_in = {k: v for k, v in _L1_attn_all.items() if k in ('Wq', 'bq', 'Wk', 'bk', 'Wv', 'bv', 'Wo', 'bo', 'rel_k', 'rel_v')}
    del _L1_attn_all

    def _L1_ffn_setup():
        import jax, jax.numpy as jnp
        import numpy as np
        S, B, I, O, H, E, K = (128, 32, 128, 128, 128, 8, 2)

        def _expert(x_seq, Wi, Wh, b, Wo, bo):
            Bsz = x_seq.shape[1]
            Hd = Wh.shape[0]

            def step(carry, xt):
                h, c = carry
                gates = xt @ Wi + h @ Wh + b
                i_, f_, g_, o_ = jnp.split(gates, 4, axis=-1)
                c = jax.nn.sigmoid(f_) * c + jax.nn.sigmoid(i_) * jnp.tanh(g_)
                h = jax.nn.sigmoid(o_) * jnp.tanh(c)
                return ((h, c), h @ Wo + bo)
            init = (jnp.zeros((Bsz, Hd), x_seq.dtype), jnp.zeros((Bsz, Hd), x_seq.dtype))
            _, ys = jax.lax.scan(step, init, x_seq)
            return ys
        key = jax.random.key(seed)
        ks = jax.random.split(key, 6)
        s = 0.02
        return {'x': jax.random.normal(ks[0], (S, B, I), dtype=jnp.float32), 'router_w': jax.random.normal(ks[1], (I, E), dtype=jnp.float32) * s, 'router_b': jnp.zeros((E,), dtype=jnp.float32), 'Wi': jax.random.normal(ks[2], (E, I, 4 * H), dtype=jnp.float32) * s, 'Wh': jax.random.normal(ks[3], (E, H, 4 * H), dtype=jnp.float32) * s, 'b': jnp.zeros((E, 4 * H), dtype=jnp.float32), 'Wo': jax.random.normal(ks[4], (E, H, O), dtype=jnp.float32) * s, 'bo': jnp.zeros((E, O), dtype=jnp.float32)}
    _L1_ffn_all = _L1_ffn_setup()
    _L1_ffn_in = {k: v for k, v in _L1_ffn_all.items() if k in ('router_w', 'router_b', 'Wi', 'Wh', 'b', 'Wo', 'bo')}
    del _L1_ffn_all
    return {'x': x, 'txt': txt, 'L0_tok_W_main': _L0_tok_in['W_main'], 'L0_tok_b_main': _L0_tok_in['b_main'], 'L0_tok_W_sx': _L0_tok_in['W_sx'], 'L0_tok_b_sx': _L0_tok_in['b_sx'], 'L0_tok_W_sy': _L0_tok_in['W_sy'], 'L0_tok_b_sy': _L0_tok_in['b_sy'], 'L0_tok_ln_g': _L0_tok_in['ln_g'], 'L0_tok_ln_b': _L0_tok_in['ln_b'], 'L0_attn_qkv1_w': _L0_attn_in['qkv1_w'], 'L0_attn_qkv2_w': _L0_attn_in['qkv2_w'], 'L0_attn_proj_w': _L0_attn_in['proj_w'], 'L0_attn_conv1_w': _L0_attn_in['conv1_w'], 'L0_attn_conv1_b': _L0_attn_in['conv1_b'], 'L0_attn_conv2_w': _L0_attn_in['conv2_w'], 'L0_attn_conv2_b': _L0_attn_in['conv2_b'], 'L0_attn_chain_logit': _L0_attn_in['chain_logit'], 'L0_ffn_Wg': _L0_ffn_in['Wg'], 'L0_ffn_W1': _L0_ffn_in['W1'], 'L0_ffn_b1': _L0_ffn_in['b1'], 'L0_ffn_W2': _L0_ffn_in['W2'], 'L0_ffn_b2': _L0_ffn_in['b2'], 'L1_attn_Wq': _L1_attn_in['Wq'], 'L1_attn_bq': _L1_attn_in['bq'], 'L1_attn_Wk': _L1_attn_in['Wk'], 'L1_attn_bk': _L1_attn_in['bk'], 'L1_attn_Wv': _L1_attn_in['Wv'], 'L1_attn_bv': _L1_attn_in['bv'], 'L1_attn_Wo': _L1_attn_in['Wo'], 'L1_attn_bo': _L1_attn_in['bo'], 'L1_attn_rel_k': _L1_attn_in['rel_k'], 'L1_attn_rel_v': _L1_attn_in['rel_v'], 'L1_ffn_router_w': _L1_ffn_in['router_w'], 'L1_ffn_router_b': _L1_ffn_in['router_b'], 'L1_ffn_Wi': _L1_ffn_in['Wi'], 'L1_ffn_Wh': _L1_ffn_in['Wh'], 'L1_ffn_b': _L1_ffn_in['b'], 'L1_ffn_Wo': _L1_ffn_in['Wo'], 'L1_ffn_bo': _L1_ffn_in['bo']}

def reference(x, txt, L0_tok_W_main, L0_tok_b_main, L0_tok_W_sx, L0_tok_b_sx, L0_tok_W_sy, L0_tok_b_sy, L0_tok_ln_g, L0_tok_ln_b, L0_attn_qkv1_w, L0_attn_qkv2_w, L0_attn_proj_w, L0_attn_conv1_w, L0_attn_conv1_b, L0_attn_conv2_w, L0_attn_conv2_b, L0_attn_chain_logit, L0_ffn_Wg, L0_ffn_W1, L0_ffn_b1, L0_ffn_W2, L0_ffn_b2, L1_attn_Wq, L1_attn_bq, L1_attn_Wk, L1_attn_bk, L1_attn_Wv, L1_attn_bv, L1_attn_Wo, L1_attn_bo, L1_attn_rel_k, L1_attn_rel_v, L1_ffn_router_w, L1_ffn_router_b, L1_ffn_Wi, L1_ffn_Wh, L1_ffn_b, L1_ffn_Wo, L1_ffn_bo):
    import jax
    import jax.numpy as jnp

    def _L0_tok_ref(x, W_main, b_main, W_sx, b_sx, W_sy, b_sy, ln_g, ln_b):
        import jax, jax.numpy as jnp
        import numpy as np
        P = 16
        SHIFT = P // 2
        EPS = 1e-05

        def _shift2d(img, dy, dx):
            H, W = (img.shape[2], img.shape[3])
            pad = ((0, 0), (0, 0), (max(dy, 0), max(-dy, 0)), (max(dx, 0), max(-dx, 0)))
            z = jnp.pad(img, pad)
            return z[:, :, max(-dy, 0):max(-dy, 0) + H, max(-dx, 0):max(-dx, 0) + W]

        def _patchify(img):
            B, C, H, W = img.shape
            nH, nW = (H // P, W // P)
            t = img.reshape(B, C, nH, P, nW, P).transpose(0, 2, 4, 1, 3, 5)
            return t.reshape(B, nH * nW, C * P * P)

        def proj(img, W, b):
            return jnp.einsum('bnf,of->bno', _patchify(img), W) + b
        main = proj(x, W_main, b_main)
        xl = proj(_shift2d(x, 0, -SHIFT), W_sx, b_sx)
        xr = proj(_shift2d(x, 0, SHIFT), W_sx, b_sx)
        yu = proj(_shift2d(x, -SHIFT, 0), W_sy, b_sy)
        yd = proj(_shift2d(x, SHIFT, 0), W_sy, b_sy)
        tok = jnp.concatenate([main, xl, xr, yu, yd], axis=-1)
        mu = jnp.mean(tok, axis=-1, keepdims=True)
        var = jnp.mean(jnp.square(tok - mu), axis=-1, keepdims=True)
        return (tok - mu) * jax.lax.rsqrt(var + EPS) * ln_g + ln_b

    def _L0_attn_ref(x, qkv1_w, qkv2_w, proj_w, conv1_w, conv1_b, conv2_w, conv2_b, chain_logit):
        import math
        import jax, jax.numpy as jnp
        import numpy as np
        B, N, D = (2, 192, 128)
        H = 8
        DK = D // H
        BETA_NOT = 0.5
        EPS = 1e-06

        def _qkv(x, w):
            b, n, d = x.shape
            qkv = (x @ w).reshape(b, n, 3, H, DK).transpose(2, 0, 3, 1, 4)
            return (qkv[0], qkv[1], qkv[2])
        scale = 1.0 / math.sqrt(DK)
        q1, k1, v1 = _qkv(x, qkv1_w)
        q2, k2, v2 = _qkv(x, qkv2_w)
        S1 = jnp.einsum('bhnd,bhmd->bhnm', q1, k1) * scale
        S2 = jnp.einsum('bhnd,bhmd->bhnm', q2, k2) * scale
        A1 = jax.nn.softmax(S1, axis=-1)
        A2 = jax.nn.softmax(S2, axis=-1)
        C_right = jnp.einsum('bhnk,bhkm->bhnm', A1, A2)
        C_left = jnp.einsum('bhnk,bhkm->bhnm', A2, A1)
        Cr = jnp.log(C_right + EPS)
        Cl = jnp.log(C_left + EPS)
        feat = jnp.stack([S1, S2, jnp.swapaxes(S1, -1, -2), jnp.swapaxes(S2, -1, -2), Cr, Cl], axis=2)
        hid = jnp.einsum('bhcnm,oc->bhonm', feat, conv1_w) + conv1_b[None, None, :, None, None]
        hid = jax.nn.gelu(hid, approximate=True)
        gates = jax.nn.sigmoid(jnp.einsum('bhcnm,oc->bhonm', hid, conv2_w) + conv2_b[None, None, :, None, None])
        g_and, g_or, g_not, g_chain = (gates[:, :, 0], gates[:, :, 1], gates[:, :, 2], gates[:, :, 3])
        Smix = S1 + g_and * S2 + g_or * (jnp.logaddexp(S1, S2) - S1) - g_not * (BETA_NOT * S2) + g_chain * Cr
        A = jax.nn.softmax(Smix, axis=-1)
        y_base = jnp.einsum('bhnm,bhmd->bhnd', A, v1)
        transport = jnp.einsum('bhnm,bhmd->bhnd', A2, v2)
        y_chain = jnp.einsum('bhnm,bhmd->bhnd', A1, transport)
        w = jax.nn.sigmoid(chain_logit)
        y = y_base + w * y_chain
        y = jnp.swapaxes(y, 1, 2).reshape(x.shape[0], x.shape[1], D)
        return y @ proj_w

    def _L0_ffn_ref(x, Wg, W1, b1, W2, b2):
        import jax, jax.numpy as jnp
        import numpy as np
        B, L, H, E, F, C = (8, 2048, 128, 8, 256, 2)
        b, l, h = x.shape
        e = Wg.shape[1]
        k = min(max(int(l * C / e), 1), l)
        S = jax.nn.softmax(x @ Wg, axis=-1)
        St = jnp.swapaxes(S, 1, 2)
        G, I = jax.lax.top_k(St, k)
        ex = jnp.take_along_axis(x[:, None], I[..., None], axis=2)
        hmid = jax.nn.gelu(jnp.einsum('bekh,ehf->bekf', ex, W1) + b1[None, :, None, :], approximate=False)
        out = jnp.einsum('bekf,efh->bekh', hmid, W2) + b2[None, :, None, :]
        vals = G[..., None] * out
        new_x = jnp.zeros_like(x).at[jnp.arange(b)[:, None, None], I].add(vals)
        return new_x

    def _L1_attn_ref(x, Wq, bq, Wk, bk, Wv, bv, Wo, bo, rel_k, rel_v):
        import jax, jax.numpy as jnp
        import numpy as np
        import math
        B, T, C = (8, 256, 128)
        H = 8
        HD = C // H
        MAX_REL = 64 + 4

        def _rel_index(t):
            r = jnp.arange(t)
            dist = jnp.clip(r[None, :] - r[:, None], -MAX_REL, MAX_REL)
            return dist + MAX_REL
        b, t, c = x.shape
        h, hd = (H, HD)
        q = x @ Wq + bq
        k = x @ Wk + bk
        v = x @ Wv + bv
        rq = q.reshape(b, t, h, hd).transpose(0, 2, 1, 3)
        rk = k.reshape(b, t, h, hd).transpose(0, 2, 1, 3)
        rv = v.reshape(b, t, h, hd).transpose(0, 2, 1, 3)
        idx = _rel_index(t)
        rk2 = rel_k[idx]
        rv2 = rel_v[idx]
        attn1 = jnp.einsum('bhqd,bhkd->bhqk', rq, rk)
        attn2 = jnp.einsum('bhqd,qkd->bhqk', rq, rk2)
        attn = jax.nn.softmax((attn1 + attn2) * (1.0 / math.sqrt(c)), axis=-1)
        w1 = jnp.einsum('bhqk,bhkd->bhqd', attn, rv)
        w2 = jnp.einsum('bhqk,qkd->bhqd', attn, rv2)
        out = (w1 + w2).transpose(0, 2, 1, 3).reshape(b, t, c)
        return out @ Wo + bo

    def _L1_ffn_ref(x, router_w, router_b, Wi, Wh, b, Wo, bo):
        import jax, jax.numpy as jnp
        import numpy as np
        S, B, I, O, H, E, K = (128, 32, 128, 128, 128, 8, 2)

        def _expert(x_seq, Wi, Wh, b, Wo, bo):
            Bsz = x_seq.shape[1]
            Hd = Wh.shape[0]

            def step(carry, xt):
                h, c = carry
                gates = xt @ Wi + h @ Wh + b
                i_, f_, g_, o_ = jnp.split(gates, 4, axis=-1)
                c = jax.nn.sigmoid(f_) * c + jax.nn.sigmoid(i_) * jnp.tanh(g_)
                h = jax.nn.sigmoid(o_) * jnp.tanh(c)
                return ((h, c), h @ Wo + bo)
            init = (jnp.zeros((Bsz, Hd), x_seq.dtype), jnp.zeros((Bsz, Hd), x_seq.dtype))
            _, ys = jax.lax.scan(step, init, x_seq)
            return ys
        S_, B_, I_ = x.shape
        N = S_ * B_
        flat_x = x.reshape(N, I_)
        logits = flat_x @ router_w + router_b
        top_vals, top_idx = jax.lax.top_k(logits, K)
        rw = jax.nn.softmax(top_vals, axis=1)
        mask = (top_idx.T[:, None, :] == jnp.arange(E)[None, :, None]).astype(x.dtype)
        expert_x = (mask[..., None] * flat_x[None, None]).reshape(K, E, S_, B_, I_)
        run_e = jax.vmap(_expert, in_axes=(0, 0, 0, 0, 0, 0))
        run_ke = jax.vmap(run_e, in_axes=(0, None, None, None, None, None))
        out = run_ke(expert_x, Wi, Wh, b, Wo, bo)
        out = out.reshape(K, E, N, -1)
        y = jnp.einsum('ken,nk,keno->no', mask, rw, out)
        return y.reshape(S_, B_, -1)
    h = _L0_tok_ref(x, L0_tok_W_main, L0_tok_b_main, L0_tok_W_sx, L0_tok_b_sx, L0_tok_W_sy, L0_tok_b_sy, L0_tok_ln_g, L0_tok_ln_b)
    h = jnp.concatenate([h, txt], axis=1)
    h = h + _L0_attn_ref(_layernorm(h, axis=-1), L0_attn_qkv1_w, L0_attn_qkv2_w, L0_attn_proj_w, L0_attn_conv1_w, L0_attn_conv1_b, L0_attn_conv2_w, L0_attn_conv2_b, L0_attn_chain_logit)
    h = h + _L0_ffn_ref(_layernorm(h, axis=-1), L0_ffn_Wg, L0_ffn_W1, L0_ffn_b1, L0_ffn_W2, L0_ffn_b2)
    h = h + _L1_attn_ref(_layernorm(h, axis=-1), L1_attn_Wq, L1_attn_bq, L1_attn_Wk, L1_attn_bk, L1_attn_Wv, L1_attn_bv, L1_attn_Wo, L1_attn_bo, L1_attn_rel_k, L1_attn_rel_v)
    h = h + _L1_ffn_ref(_layernorm(h, axis=-1), L1_ffn_router_w, L1_ffn_router_b, L1_ffn_Wi, L1_ffn_Wh, L1_ffn_b, L1_ffn_Wo, L1_ffn_bo)
    return h

_drawn_inputs = setup_inputs


def setup_inputs(seed=0):
    import zlib

    import numpy as np

    out = dict(_drawn_inputs(seed))
    spreads = {'L0_tok_b_main': (0.0, 0.1),
     'L0_tok_b_sx': (0.0, 0.1),
     'L0_tok_b_sy': (0.0, 0.1),
     'L0_tok_ln_g': (1.0, 0.2),
     'L0_tok_ln_b': (0.0, 0.1),
     'L0_attn_conv2_b': (-5.0, 0.6),
     'L0_ffn_b1': (0.0, 0.267),
     'L0_ffn_b2': (0.0, 0.1),
     'L1_attn_bq': (0.0, 0.8),
     'L1_attn_bk': (0.0, 0.8),
     'L1_attn_bv': (0.0, 0.1),
     'L1_attn_bo': (0.0, 0.1),
     'L1_ffn_router_b': (0.0, 0.1),
     'L1_ffn_b': (0.0, 0.8),
     'L1_ffn_bo': (0.0, 0.1)}
    factors = {'L0_attn_qkv1_w': 5.237,
     'L0_attn_qkv2_w': 8.0,
     'L0_attn_proj_w': 4.711,
     'L0_attn_conv1_w': 8.0,
     'L0_attn_conv1_b': 8.0,
     'L0_attn_conv2_w': 8.0,
     'L1_attn_rel_k': 8.0,
     'L1_ffn_Wi': 6.811,
     'L1_ffn_Wh': 8.0,
     'L1_ffn_Wo': 5.145}
    for name, (base, spread) in spreads.items():
        noise = np.random.default_rng([zlib.crc32(name.encode()), seed]).standard_normal(out[name].shape)
        drawn = base * np.exp(spread * noise) if base else spread * noise
        out[name] = jnp.asarray(drawn.astype(out[name].dtype))
    for name, factor in factors.items():
        out[name] = (out[name] * factor).astype(out[name].dtype)
    return out
```

```python
from contextlib import ExitStack, contextmanager

import numpy as np
import concourse.bass as bass
from concourse import mybir

F32 = mybir.dt.float32
ALU = mybir.AluOpType
ACT = mybir.ActivationFunctionType
AX_X = mybir.AxisListType.X

B = 32
NT = 36
TX = 77
N = NT + TX
D = 128
H = 8
DK = D // H
LN_EPS = 1e-5
BANK = 512
HB = 4


class Steps:

    def __init__(self, engine, sem, loop=0, per=0):
        self.engine, self.sem, self.base, self.per, self.n = engine, sem, loop * per, per, 0

    def done(self, instruction):
        instruction.then_inc(self.sem, 1)
        self.n += 1
        self.engine.wait_ge(self.sem, self.base + self.n)

    def close(self):
        assert self.n == self.per, (self.n, self.per)


class Phase:

    def __init__(self, nc, name):
        self.nc, self.name, self.ctx, self.sems = nc, name, ExitStack(), []

    def __enter__(self):
        return self

    def __exit__(self, *args):
        self.nc.clear_and_free_semaphores(self.sems)
        self.nc.all_engine_barrier()
        self.ctx.close()

    def sb(self, name, shape):
        return self.ctx.enter_context(self.nc.sbuf_tensor(f"{self.name}_{name}", shape, F32))

    def sem(self, name):
        self.sems.append(self.nc.alloc_semaphore(f"{self.name}_{name}"))
        return self.sems[-1]

    def block(self):
        return self.nc.Block()


def over_banks(ps, bank, banks, parts, width):
    return ps[0:parts, bank:bank + banks, 0:HB * width].rearrange("p k (h n) -> p k h n", h=HB)


def mean_and_rstd(ph, tag, parts):
    return dict(
        stats=ph.sb(f"{tag}_stats", [parts, B, 6]), mean=ph.sb(f"{tag}_mean", [parts, B]),
        diff=ph.sb(f"{tag}_diff", [parts, B]), var=ph.sb(f"{tag}_var", [parts, B]),
        std=ph.sb(f"{tag}_std", [parts, B]), rstd=ph.sb(f"{tag}_rstd", [parts, B]))


def ln_statistics(dve, steps, x, parts, t, var_ready, std_ready, stats_done):
    with dve.Fori(0, B) as b:
        dve.bn_stats(t["stats"][:, b, :], x[0:parts, b, :]).then_inc(stats_done, 1)
    dve.wait_ge(stats_done, B)
    st = t["stats"]
    steps.done(dve.tensor_tensor(t["mean"][:], st[:, :, 1], st[:, :, 4], ALU.add))
    steps.done(dve.tensor_tensor(t["diff"][:], st[:, :, 1], st[:, :, 4], ALU.subtract))
    steps.done(dve.tensor_tensor(t["var"][:], st[:, :, 2], st[:, :, 5], ALU.add))
    steps.done(dve.tensor_tensor(t["diff"][:], t["diff"][:], t["diff"][:], ALU.mult))
    steps.done(dve.tensor_scalar(t["mean"][:], t["mean"][:], 0.5, None, ALU.mult))
    steps.done(dve.tensor_scalar(t["var"][:], t["var"][:], 1.0 / D, None, ALU.mult))
    dve.scalar_tensor_tensor(t["var"][:], t["diff"][:], 0.25, t["var"][:], ALU.mult, ALU.add).then_inc(var_ready, 1)
    dve.wait_ge(std_ready, 1)
    steps.done(dve.reciprocal(t["rstd"][:], t["std"][:]))


def tokenize(nc, h, ps, ident, eps, dram):
    CW = 14
    with Phase(nc, "tok") as ph:
        xv = ph.sb("xv", [128, 3, B * 6, CW])
        xh = ph.sb("xh", [128, 3, B, CW, 6])
        wv = ph.sb("wv", [128, 4, 3, D])
        wh = ph.sb("wh", [128, 4, 3, D])
        bias = ph.sb("bias", [D, 1])
        gain = ph.sb("gain", [NT, D])
        shift = ph.sb("shift", [NT, D])
        tokT = ph.sb("tokT", [D, B * NT])
        tok = ph.sb("tok", [NT, B, D])
        t = mean_and_rstd(ph, "ln", NT)
        loads, txt_in, out_ready, tokT_ready, rows_ready = (ph.sem(s) for s in (
            "loads", "txt_in", "out_ready", "tokT_ready", "rows_ready"))
        var_ready, std_ready, stats_done, dve_step = (ph.sem(s) for s in (
            "var_ready", "std_ready", "stats_done", "dve_step"))
        weights_in = ph.sem("weights_in")
        IB = [11, 11, 10]

        with ph.block() as block:
            @block.sync
            def _(sp):
                sp.dma_start(wv[:], dram["tok_wv"]).then_inc(weights_in, 16)
                sp.dma_start(xv[:], dram["x_v"]).then_inc(loads, 16)
                sp.dma_start(wh[:], dram["tok_wh"]).then_inc(weights_in, 16)
                sp.dma_start(xh[:], dram["x_h"]).then_inc(loads, 16)
                sp.dma_start(bias[:], dram["tok_bias"]).then_inc(weights_in, 16)
                sp.dma_start(gain[:], dram["tok_gain"].partition_broadcast(NT)).then_inc(weights_in, 16)
                sp.dma_start(shift[:], dram["tok_shift"].partition_broadcast(NT)).then_inc(weights_in, 16)
                sp.dma_start(h[NT:N, :, :], dram["txt"].rearrange("b t d -> t b d")).then_inc(txt_in, 16)
                sp.wait_ge(txt_in, 16)

            @block.tensor
            def _(pe):
                pe.wait_ge(weights_in, 80)
                pe.wait_ge(loads, 32)
                b0 = 0
                for k, nb in enumerate(IB):
                    out = ps[:, k, 0:nb * NT]
                    for p in range(4):
                        for c in range(3):
                            pe.matmul(out, wv[:, p, c, :], xv[:, c, 6 * b0:6 * (b0 + nb), p:p + 11:2],
                                      start=(p == 0 and c == 0), stop=False)
                    for p in range(4):
                        for c in range(3):
                            last = pe.matmul(out, wh[:, p, c, :], xh[:, c, b0:b0 + nb, p:p + 11:2, :],
                                             start=False, stop=(p == 3 and c == 2))
                    last.then_inc(out_ready, 1)
                    b0 += nb
                pe.wait_ge(tokT_ready, 3)
                for b in range(B):
                    tr = pe.transpose(ps[0:NT, b // 4, (b % 4) * D:(b % 4 + 1) * D], tokT[:, b * NT:(b + 1) * NT], ident[:])
                    if b % 4 == 3:
                        tr.then_inc(rows_ready, 1)

            @block.scalar
            def _(act):
                b0 = 0
                for k, nb in enumerate(IB):
                    act.wait_ge(out_ready, k + 1)
                    act.activation(tokT[:, b0 * NT:(b0 + nb) * NT], ps[:, k, 0:nb * NT], ACT.Identity,
                                   bias=bias[:]).then_inc(tokT_ready, 1)
                    b0 += nb
                act.wait_ge(var_ready, 1)
                act.activation(t["std"][:], t["var"][:], ACT.Sqrt, bias=eps[0:NT]).then_inc(std_ready, 1)

            @block.vector
            def _(dve):
                steps = Steps(dve, dve_step)
                for k in range(8):
                    dve.wait_ge(rows_ready, k + 1)
                    steps.done(dve.tensor_copy(tok[:, 4 * k:4 * k + 4, :],
                                               ps[0:NT, k, :].rearrange("p (b d) -> p b d", d=D)))
                ln_statistics(dve, steps, tok, NT, t, var_ready, std_ready, stats_done)
                wide = [NT, B, D]
                steps.done(dve.tensor_tensor(tok[:], tok[:], t["mean"][:].unsqueeze(2).broadcast_to(wide), ALU.subtract))
                steps.done(dve.tensor_tensor(tok[:], tok[:], t["rstd"][:].unsqueeze(2).broadcast_to(wide), ALU.mult))
                steps.done(dve.tensor_tensor(tok[:], tok[:], gain[:].unsqueeze(1).broadcast_to(wide), ALU.mult))
                steps.done(dve.tensor_tensor(h[0:NT, :, :], tok[:], shift[:].unsqueeze(1).broadcast_to(wide), ALU.add))


def norm_and_turn(nc, name, h, hT, ps, ident, eps):
    with Phase(nc, name) as ph:
        hn = ph.sb("hn", [N, B, D])
        t = mean_and_rstd(ph, "ln", N)
        var_ready, std_ready, stats_done, dve_step, rows_ready, turned, moved = (ph.sem(s) for s in (
            "var_ready", "std_ready", "stats_done", "dve_step", "rows_ready", "turned", "moved"))
        with ph.block() as block:
            @block.vector
            def _(dve):
                steps = Steps(dve, dve_step)
                ln_statistics(dve, steps, h, N, t, var_ready, std_ready, stats_done)
                for b in range(B):
                    dve.tensor_scalar(hn[:, b, :], h[:, b, :], t["mean"][:, b:b + 1], t["rstd"][:, b:b + 1],
                                      ALU.subtract, ALU.mult).then_inc(rows_ready, 1)

            @block.tensor
            def _(pe):
                for b in range(B):
                    pe.wait_ge(rows_ready, b + 1)
                    tr = pe.transpose(ps[:, b // 4, (b % 4) * N:(b % 4 + 1) * N], hn[:, b, :], ident[0:N, 0:N])
                    if b % 4 == 3:
                        tr.then_inc(turned, 1)

            @block.scalar
            def _(act):
                act.wait_ge(var_ready, 1)
                act.activation(t["std"][:], t["var"][:], ACT.Sqrt, bias=eps[0:N]).then_inc(std_ready, 1)
                for k in range(B // 4):
                    act.wait_ge(turned, k + 1)
                    act.activation(hT[:, 4 * k:4 * k + 4, :], ps[:, k, 0:4 * N].rearrange("p (b n) -> p b n", n=N),
                                   ACT.Copy).then_inc(moved, 1)
                act.wait_ge(moved, B // 4)



def signal(engine, instruction, sem, count):
    instruction.then_inc(sem, 1)
    engine.wait_ge(sem, count)


def logic_attention(nc, h, hT, ps, ident, dram):
    W = H * N
    G = 8
    GROUPS = -(-N // G)
    MP = GROUPS * G
    CUT = 64
    LO = N - CUT
    UNITS = H * GROUPS // 8
    S_BANK, A1T_BANK, A2T_BANK = (2, 5), 0, 2
    T0_BANK, T1_BANK, CR_BANK = 4, 6, 0
    HID_BANK, GATE_BANK = (2, 4), (6, 7)

    ND = 19

    def made_by(u):
        return sum(1 for x in range(8 * (u + 1)) if x % GROUPS == GROUPS - 1 or x % 8 == 7)

    def head_marks(hd):
        return sum(1 for x in range(GROUPS * (hd + 1)) if x % GROUPS == GROUPS - 1 or x % 8 == 7)

    GATE_MARKS = made_by(UNITS - 1)
    with Phase(nc, "la") as ph:
        sb = ph.sb
        w_m, w_n = sb("w_m", [D, 4, 128]), sb("w_n", [D, 4, 128])
        w_v, w_out = sb("w_v", [D, 2 * D]), sb("w_out", [D, D])
        c_mask, q_mask = sb("c_mask", [128, 4]), sb("q_mask", [128, 2])
        w_exp, w_sel = sb("w_exp", [128, 16]), sb("w_sel", [128, 16])
        sel_hot, g_hot = sb("sel_hot", [128, GROUPS, G]), sb("g_hot", [128, G])
        w2_rows, b1 = sb("w2_rows", [128, 4]), sb("b1", [128, 1])
        b2, w_chain = sb("b2", [N, 4]), sb("w_chain", [N, 1])
        one, tiny = sb("one", [128, 1]), sb("tiny", [128, 1])
        sel = sb("sel", [128, GROUPS, G, 16])
        w2 = sb("w2", [128, G, 4])

        xT = sb("xT", [D, N])
        m_side = sb("m_side", [128, 4, N])
        n_side = sb("n_side", [128, 4, N])
        n_map = sb("n_map", [128, 2, 2, 4, N])
        n_head = sb("n_head", [128, 2, 4, N])
        V = sb("V", [N, 2 * D])
        m_exp = sb("m_exp", [128, 4, MP, 16])
        S = [sb(f"S{i}", [N, W]) for i in (1, 2)]
        P = [sb(f"P{i}", [N, W]) for i in (1, 2)]
        PT = [sb(f"PT{i}", [N, W]) for i in (1, 2)]
        top, total, inv = sb("top", [N, 3 * H]), sb("total", [N, 3 * H]), sb("inv", [N, 3 * H])
        T0, T1, Cr = sb("T0", [128, W]), sb("T1", [128, W]), sb("Cr", [N, W])
        soft, absd = sb("soft", [N, W]), sb("absd", [N, W])
        hid = sb("hid", [128, 2, 8, N])
        gate = sb("gate", [N, W, 4])
        mixA, mixB, mixC = sb("mixA", [N, W]), sb("mixB", [N, W]), sb("mixC", [N, W])
        ET, transport, chain = sb("ET", [N, W]), sb("transport", [N, D]), sb("chain", [N, D])
        y, yT = sb("y", [N, D]), sb("yT", [D, N])

        names = ("consts_in setup xT_ready mn_made m_ready n_ready v_made V_ready n_map_ready exp_ready "
                 "S1_made S2_made S1_ready S2_ready shifted raised P_ready PT_made PT1_ready PT2_ready "
                 "T0_made T1_made Cr_made T0_ready T1_ready Cr_ready transport_made transport_ready "
                 "chain_made chain_ready diff_ready abs_ready soft_ready hid_made hid_ready gate_made gate_in "
                 "gate_ready mix_shifted mix_raised mix_T_made ET_ready base_made y_ready yT_made yT_ready "
                 "out_made dve_step act_step pool_step act_setup").split()
        s = {n: ph.sem(n) for n in names}
        loads = [(w_m, "la_w_m"), (w_n, "la_w_n"), (w_v, "la_w_v"), (w_out, "la_w_out"), (c_mask, "la_c_mask"),
                 (q_mask, "la_q_mask"), (w_exp, "la_w_exp"), (w_sel, "la_w_sel"), (sel_hot, "la_sel_hot"),
                 (g_hot, "la_g_hot"), (w2_rows, "la_w2_rows"), (b1, "la_b1")]

        def col(i, h0=0):
            return slice((h0 + i) * N, (h0 + i + 1) * N)

        def heads(bank, parts=N):
            return ps[0:parts, bank:bank + 2, 0:HB * N]

        def two(tile, parts=N):
            return tile[0:parts, :].rearrange("p (k c) -> p k c", k=2)

        with ph.block() as block:
            @block.sync
            def _(sp):
                for tile, name in loads:
                    sp.dma_start(tile[:], dram[name]).then_inc(s["consts_in"], 16)
                sp.dma_start(b2[:], dram["la_b2"].partition_broadcast(N)).then_inc(s["consts_in"], 16)
                sp.dma_start(w_chain[:], dram["la_chain"].partition_broadcast(N)).then_inc(s["consts_in"], 16)
                sp.wait_ge(s["consts_in"], 16 * (len(loads) + 2))

            @block.gpsimd
            def _(pool):
                pool.memset(m_exp[:, :, N:MP, :], 0.0).then_inc(s["pool_step"], 1)
                pool.wait_ge(s["pool_step"], 1)
                pool.wait_ge(s["setup"], 4)

                def image(b, first):
                    if not first:
                        pool.wait_ge(s["v_made"], b)
                    pool.tensor_copy(xT[:], hT[:, b, :]).then_inc(s["xT_ready"], 1)
                    pool.wait_ge(s["m_ready"], b + 1)
                    if not first:
                        pool.wait_ge(s["hid_made"], b * UNITS)
                    for p in range(4):
                        wide = [128, N, 16]
                        pool.tensor_tensor(m_exp[:, p, 0:N, :], m_side[:, p, :].unsqueeze(2).broadcast_to(wide),
                                           w_exp[:].unsqueeze(1).broadcast_to(wide), ALU.mult).then_inc(s["exp_ready"], 1)

                image(0, True)
                with pool.Fori(1, B) as b:
                    image(b, False)

            @block.tensor
            def _(pe):
                pe.wait_ge(s["setup"], 4)
                pe.wait_ge(s["consts_in"], 16 * (len(loads) + 2))
                with pe.Fori(0, B) as b:
                    for bank, w in ((0, w_m), (1, w_n)):
                        for p in range(4):
                            mm = pe.matmul(ps[:, bank, col(p)], w[:, p, :], hT[:, b, :], start=True, stop=True)
                    mm.then_inc(s["mn_made"], 1)
                    pe.wait_ge(s["xT_ready"], b + 1)
                    pe.wait_ge(s["dve_step"], ND * b + 4)
                    pe.matmul(ps[0:N, 4, 0:2 * D], xT[:], w_v[:], start=True, stop=True).then_inc(s["v_made"], 1)
                    pe.wait_ge(s["n_map_ready"], 6 * b + 4)
                    pe.wait_ge(s["m_ready"], b + 1)
                    for i in range(2):
                        for hd in range(H):
                            p, q = hd // 2, hd % 2
                            mm = pe.matmul(ps[0:N, S_BANK[i] + hd // HB, col(hd % HB)], n_map[:, i, q, p, :],
                                           m_side[:, p, :], start=True, stop=True)
                        mm.then_inc(s[f"S{i + 1}_made"], 1)
                    for i, bank in ((0, A1T_BANK), (1, A2T_BANK)):
                        pe.wait_ge(s["P_ready"], 2 * b + i + 1)
                        for hd in range(H):
                            tr = pe.transpose(ps[0:N, bank + hd // HB, col(hd % HB)], P[i][:, col(hd)], ident[0:N, 0:N])
                        tr.then_inc(s["PT_made"], 1)
                    pe.wait_ge(s["PT1_ready"], b + 1)
                    pe.wait_ge(s["PT2_ready"], b + 1)
                    pe.wait_ge(s["V_ready"], b + 1)
                    pe.wait_ge(s["S2_ready"], b + 1)
                    for bank, lo, sem in ((T0_BANK, 0, "T0_made"), (T1_BANK, LO, "T1_made")):
                        for hd in range(H):
                            keys = slice(hd * N + lo, hd * N + lo + CUT)
                            pe.matmul(ps[0:CUT, bank + hd // HB, col(hd % HB)], P[1][:, keys], PT[0][:, col(hd)],
                                      start=True, stop=True)
                            mm = pe.matmul(ps[CUT:128, bank + hd // HB, col(hd % HB)], P[0][:, keys], PT[1][:, col(hd)],
                                           start=True, stop=True)
                        mm.then_inc(s[sem], 1)
                    for hd in range(H):
                        mm = pe.matmul(ps[0:N, CR_BANK + hd // HB, col(hd % HB)], PT[0][:, col(hd)], P[1][:, col(hd)],
                                       start=True, stop=True)
                    mm.then_inc(s["Cr_made"], 1)
                    for hd in range(H):
                        mm = pe.matmul(ps[0:N, 2, hd * DK:(hd + 1) * DK], PT[1][:, col(hd)],
                                       V[:, D + hd * DK:D + (hd + 1) * DK], start=True, stop=True)
                    mm.then_inc(s["transport_made"], 1)
                    pe.wait_ge(s["transport_ready"], b + 1)
                    for hd in range(H):
                        mm = pe.matmul(ps[0:N, 3, hd * DK:(hd + 1) * DK], PT[0][:, col(hd)],
                                       transport[:, hd * DK:(hd + 1) * DK], start=True, stop=True)
                    mm.then_inc(s["chain_made"], 1)
                    pe.wait_ge(s["chain_ready"], b + 1)
                    pe.wait_ge(s["T0_ready"], b + 1)
                    pe.wait_ge(s["T1_ready"], b + 1)

                    def second(u):
                        pe.wait_ge(s["hid_ready"], UNITS * b + u + 1)
                        for k in range(8):
                            hd, g = divmod(8 * u + k, GROUPS)
                            if g == 0 and hd >= 2:
                                pe.wait_ge(s["gate_in"], H * b + hd - 1)
                            mm = pe.matmul(ps[0:N, GATE_BANK[hd % 2], g * 32:g * 32 + 32], hid[:, u % 2, k, :],
                                           w2[:].rearrange("p g c -> p (g c)"), start=True, stop=True)
                            if g == GROUPS - 1 or k == 7:
                                mm.then_inc(s["gate_made"], 1)

                    for u in range(UNITS):
                        if u >= 2:
                            pe.wait_ge(s["hid_ready"], UNITS * b + u - 1)
                        for k in range(8):
                            hd, g = divmod(8 * u + k, GROUPS)
                            p, q = hd // 2, hd % 2
                            if g == 0:
                                pe.wait_ge(s["exp_ready"], 4 * b + p + 1)
                            out = ps[:, HID_BANK[u % 2] + k // 4, col(k % 4)]
                            pe.matmul(out, m_exp[:, p, 8 * g:8 * g + 8, :].rearrange("p g o -> p (g o)"),
                                      n_head[:, q, p, :], start=True, stop=False)
                            mm = pe.matmul(out, sel[:, g, :, :].rearrange("p g o -> p (g o)"),
                                           (T0 if g < 8 else T1)[:, col(hd)], start=False, stop=True)
                        mm.then_inc(s["hid_made"], 1)
                        if u:
                            second(u - 1)
                    second(UNITS - 1)
                    pe.wait_ge(s["mix_raised"], b + 1)
                    for hd in range(H):
                        tr = pe.transpose(ps[0:N, hd // HB, col(hd % HB)], mixB[:, col(hd)], ident[0:N, 0:N])
                    tr.then_inc(s["mix_T_made"], 1)
                    pe.wait_ge(s["ET_ready"], b + 1)
                    for hd in range(H):
                        mm = pe.matmul(ps[0:N, 2, hd * DK:(hd + 1) * DK], ET[:, col(hd)],
                                       V[:, hd * DK:(hd + 1) * DK], start=True, stop=True)
                    mm.then_inc(s["base_made"], 1)
                    pe.wait_ge(s["y_ready"], b + 1)
                    pe.transpose(ps[0:D, 3, 0:N], y[:], ident[0:N, 0:N]).then_inc(s["yT_made"], 1)
                    pe.wait_ge(s["yT_ready"], b + 1)
                    pe.matmul(ps[0:N, 4, 0:D], yT[:], w_out[:], start=True, stop=True).then_inc(s["out_made"], 1)

            @block.scalar
            def _(act):
                act.wait_ge(s["consts_in"], 16 * (len(loads) + 2))
                signal(act, act.activation(w_chain[:], w_chain[:], ACT.Tanh, scale=0.5), s["act_setup"], 1)
                act.wait_ge(s["setup"], 4)
                with act.Fori(0, B) as b:
                    act.wait_ge(s["mn_made"], b + 1)
                    act.activation(m_side[:], ps[:, 0, 0:4 * N].rearrange("p (k n) -> p k n", k=4), ACT.Copy).then_inc(s["m_ready"], 1)
                    act.wait_ge(s["v_made"], b + 1)
                    act.activation(V[:], ps[0:N, 4, 0:2 * D], ACT.Copy).then_inc(s["V_ready"], 1)
                    for i in range(2):
                        act.wait_ge(s[f"S{i + 1}_made"], b + 1)
                        act.activation(two(S[i]), heads(S_BANK[i]), ACT.Copy).then_inc(s[f"S{i + 1}_ready"], 1)
                    for i in range(2):
                        act.wait_ge(s["shifted"], 2 * b + i + 1)
                        act.activation(P[i][:], P[i][:], ACT.Exp).then_inc(s["raised"], 1)
                    act.wait_ge(s["diff_ready"], b + 1)
                    signal(act, act.activation(absd[:], soft[:], ACT.Abs), s["act_step"], 3 * b + 1)
                    signal(act, act.activation(absd[:], absd[:], ACT.Exp, scale=-1.0), s["act_step"], 3 * b + 2)
                    act.activation(absd[:], absd[:], ACT.Ln, bias=one[0:N]).then_inc(s["abs_ready"], 1)
                    act.wait_ge(s["PT_made"], 2 * b + 1)
                    act.activation(two(PT[0]), heads(A1T_BANK), ACT.Copy).then_inc(s["PT1_ready"], 1)
                    for made, ready, tile, bank, parts in (("T0_made", "T0_ready", T0, T0_BANK, 128),
                                                           ("T1_made", "T1_ready", T1, T1_BANK, 128),
                                                           ("Cr_made", "Cr_ready", Cr, CR_BANK, N)):
                        act.wait_ge(s[made], b + 1)
                        act.activation(two(tile, parts), heads(bank, parts), ACT.Ln, bias=tiny[0:parts]).then_inc(s[ready], 1)
                    for u in range(UNITS):
                        act.wait_ge(s["hid_made"], UNITS * b + u + 1)
                        if u >= 2:
                            act.wait_ge(s["gate_made"], made_by(u - 2) + GATE_MARKS * b)
                        act.activation(hid[:, u % 2, :, :].rearrange("p (k c) n -> p k (c n)", k=2), heads(HID_BANK[u % 2], 128),
                                       ACT.Gelu_apprx_tanh, bias=b1[:]).then_inc(s["hid_ready"], 1)
                    act.wait_ge(s["gate_in"], H * b + H)
                    act.activation(gate[:], gate[:], ACT.Tanh, scale=0.5).then_inc(s["gate_ready"], 1)
                    act.wait_ge(s["mix_shifted"], b + 1)
                    act.activation(mixB[:], mixA[:], ACT.Exp).then_inc(s["mix_raised"], 1)
                    act.wait_ge(s["mix_T_made"], b + 1)
                    act.activation(two(ET), heads(0), ACT.Copy).then_inc(s["ET_ready"], 1)
                    act.wait_ge(s["yT_made"], b + 1)
                    act.activation(yT[:], ps[0:D, 3, 0:N], ACT.Copy).then_inc(s["yT_ready"], 1)
                    signal(act, act.activation(absd[:, 0:1], one[0:N], ACT.Copy), s["act_step"], 3 * b + 3)

            @block.vector
            def _(dve):
                dve.memset(one[:], 1.0).then_inc(s["setup"], 1)
                dve.memset(tiny[:], 1e-6).then_inc(s["setup"], 1)
                dve.wait_ge(s["consts_in"], 16 * (len(loads) + 2))
                wide = [128, GROUPS * G, 16]
                dve.tensor_tensor(sel[:].rearrange("p a g o -> p (a g) o"),
                                  sel_hot[:].rearrange("p a g -> p (a g)").unsqueeze(2).broadcast_to(wide),
                                  w_sel[:].unsqueeze(1).broadcast_to(wide), ALU.mult).then_inc(s["dve_step"], 1)
                wide = [128, G, 4]
                dve.tensor_tensor(w2[:], g_hot[:].unsqueeze(2).broadcast_to(wide), w2_rows[:].unsqueeze(1).broadcast_to(wide),
                                  ALU.mult).then_inc(s["dve_step"], 1)
                dve.tensor_scalar(w_exp[:], w_exp[:], DK ** -0.5, None, ALU.mult).then_inc(s["dve_step"], 1)
                dve.wait_ge(s["act_setup"], 1)
                dve.tensor_scalar(w_chain[:], w_chain[:], 0.5, 0.5, ALU.mult, ALU.add).then_inc(s["dve_step"], 1)
                dve.wait_ge(s["dve_step"], 4)
                signal(dve, dve.memset(top[:], 0.0), s["setup"], 3)
                signal(dve, dve.memset(total[:], 0.0), s["setup"], 4)
                with dve.Fori(0, B) as b:
                    k = [4]

                    def step(instruction):
                        k[0] += 1
                        signal(dve, instruction, s["dve_step"], ND * b + k[0])

                    def softmax_top(x, out, i, ready, count):
                        t = top[:, H * i:H * i + H]
                        step(dve.tensor_reduce(t, x.rearrange("p (h n) -> p h n", h=H), AX_X, ALU.max))
                        signal(dve, dve.tensor_tensor(out.rearrange("p (h n) -> p h n", h=H), x.rearrange("p (h n) -> p h n", h=H),
                                                      t.unsqueeze(2).broadcast_to([N, H, N]), ALU.subtract), s[ready], count)

                    def softmax_inverse(x, i):
                        t = total[:, H * i:H * i + H]
                        step(dve.tensor_reduce(t, x.rearrange("p (h n) -> p h n", h=H), AX_X, ALU.add))
                        step(dve.reciprocal(inv[:, H * i:H * i + H], t))

                    dve.wait_ge(s["mn_made"], b + 1)
                    step(dve.tensor_copy(n_side[:], ps[:, 1, 0:4 * N].rearrange("p (k n) -> p k n", k=4)))
                    for i in range(2):
                        for q in range(2):
                            dve.tensor_scalar(n_map[:, i, q], n_side[:], c_mask[:, 2 * i + q:2 * i + q + 1], None,
                                              ALU.mult).then_inc(s["n_map_ready"], 1)
                    for q in range(2):
                        dve.tensor_scalar(n_head[:, q], n_side[:], q_mask[:, q:q + 1], None, ALU.mult).then_inc(s["n_map_ready"], 1)
                    for i in range(2):
                        dve.wait_ge(s[f"S{i + 1}_ready"], b + 1)
                        softmax_top(S[i][:], P[i][:], i, "shifted", 2 * b + i + 1)
                    signal(dve, dve.tensor_tensor(soft[:], S[1][:], S[0][:], ALU.subtract), s["diff_ready"], b + 1)
                    for i in range(2):
                        dve.wait_ge(s["raised"], 2 * b + i + 1)
                        softmax_inverse(P[i][:], i)
                        p3 = P[i][:].rearrange("p (h n) -> p h n", h=H)
                        signal(dve, dve.tensor_tensor(p3, p3, inv[:, H * i:H * i + H].unsqueeze(2).broadcast_to([N, H, N]),
                                                      ALU.mult), s["P_ready"], 2 * b + i + 1)
                    dve.wait_ge(s["PT_made"], 2 * b + 2)
                    dve.tensor_copy(two(PT[1]), heads(A2T_BANK)).then_inc(s["PT2_ready"], 1)
                    dve.wait_ge(s["abs_ready"], b + 1)
                    signal(dve, dve.scalar_tensor_tensor(soft[:], soft[:], 0.0, absd[:], ALU.max, ALU.add), s["soft_ready"], b + 1)
                    dve.wait_ge(s["transport_made"], b + 1)
                    dve.tensor_copy(transport[:], ps[0:N, 2, 0:D]).then_inc(s["transport_ready"], 1)
                    dve.wait_ge(s["chain_made"], b + 1)
                    dve.tensor_scalar(chain[:], ps[0:N, 3, 0:D], w_chain[:], None, ALU.mult).then_inc(s["chain_ready"], 1)
                    for hd in range(H):
                        dve.wait_ge(s["gate_made"], GATE_MARKS * b + head_marks(hd))
                        dve.tensor_tensor(gate[:, col(hd), :], ps[0:N, GATE_BANK[hd % 2], 0:4 * N].rearrange("p (m c) -> p m c", c=4),
                                          b2[:].unsqueeze(1).broadcast_to([N, N, 4]), ALU.add).then_inc(s["gate_in"], 1)
                    dve.wait_ge(s["gate_ready"], b + 1)
                    t_and, t_or, t_not, t_chain = (gate[:, :, c] for c in range(4))
                    step(dve.scalar_tensor_tensor(mixA[:], t_not, -0.5, t_and, ALU.mult, ALU.add))
                    step(dve.scalar_tensor_tensor(mixA[:], mixA[:], 0.5, S[1][:], ALU.add, ALU.mult))
                    step(dve.scalar_tensor_tensor(mixB[:], t_or, 1.0, soft[:], ALU.add, ALU.mult))
                    dve.wait_ge(s["Cr_ready"], b + 1)
                    step(dve.scalar_tensor_tensor(mixC[:], t_chain, 1.0, Cr[:], ALU.add, ALU.mult))
                    step(dve.tensor_tensor(mixA[:], mixA[:], mixB[:], ALU.add))
                    step(dve.tensor_tensor(mixA[:], mixA[:], mixC[:], ALU.add))
                    step(dve.scalar_tensor_tensor(mixA[:], mixA[:], 0.5, S[0][:], ALU.mult, ALU.add))
                    softmax_top(mixA[:], mixA[:], 2, "mix_shifted", b + 1)
                    dve.wait_ge(s["mix_raised"], b + 1)
                    softmax_inverse(mixB[:], 2)
                    dve.wait_ge(s["base_made"], b + 1)
                    y3 = y[:].rearrange("p (h d) -> p h d", h=H)
                    step(dve.tensor_tensor(y3, ps[0:N, 2, 0:D].rearrange("p (h d) -> p h d", h=H),
                                           inv[:, 2 * H:3 * H].unsqueeze(2).broadcast_to([N, H, DK]), ALU.mult))
                    dve.tensor_tensor(y[:], y[:], chain[:], ALU.add).then_inc(s["y_ready"], 1)
                    dve.wait_ge(s["out_made"], b + 1)
                    step(dve.tensor_tensor(h[:, b, :], ps[0:N, 4, 0:D], h[:, b, :], ALU.add))
                    assert k[0] == ND + 4, k


def expert_choice(nc, h, hT, ps, ident, dram):
    E, F, TOP = 8, 256, 2 * N // 8
    HALF = B // 2
    Q = 4
    with Phase(nc, "ec") as ph:
        sb = ph.sb
        w_gate = sb("w_gate", [D, E])
        w1, b1 = sb("w1", [D, E, F]), sb("b1", [128, E, 2])
        w2 = sb("w2", [128, E, 2, D])
        b2 = sb("b2", [128, HALF, D])
        gate = sb("gate", [N, B, E])
        peak, total, inv = sb("peak", [N, B]), sb("total", [N, B]), sb("inv", [N, B])
        rows = sb("rows", [128, 2, N])
        left, best = sb("left", [128, 2, N]), sb("best", [128, 2, 4, 8])
        above, equal, rank = sb("above", [128, 2, N]), sb("equal", [128, 2, N]), sb("rank", [128, 2, N])
        room, ones = sb("room", [128, 2]), sb("ones", [128, N])
        hid = sb("hid", [128, 2, 2, Q * N])
        names = ("consts_in scores_made shifted raised gate_ready rows_made rows_ready chosen turned_back "
                 "bias_made hid_made hid_ready out_made added dve_step").split()
        s = {n: ph.sem(n) for n in names}
        wide = [N, B, E]

        with ph.block() as block:
            @block.sync
            def _(sp):
                for tile, name in ((w_gate, "ec_w_gate"), (w1, "ec_w1"), (b1, "ec_b1"), (w2, "ec_w2"), (b2, "ec_b2")):
                    sp.dma_start(tile[:], dram[name]).then_inc(s["consts_in"], 16)

            @block.tensor
            def _(pe):
                pe.wait_ge(s["consts_in"], 80)
                for b in range(B):
                    mm = pe.matmul(ps[0:N, 0, b * E:(b + 1) * E], hT[:, b, :], w_gate[:], start=True, stop=True)
                mm.then_inc(s["scores_made"], 1)
                pe.wait_ge(s["gate_ready"], 1)
                for k in range(2):
                    tr = pe.transpose(ps[:, 1, k * N:(k + 1) * N], gate[:, k * HALF:(k + 1) * HALF, :].rearrange("p b e -> p (b e)"),
                                      ident[0:N, 0:N])
                tr.then_inc(s["rows_made"], 1)
                pe.wait_ge(s["chosen"], 1)
                for k in range(2):
                    tr = pe.transpose(ps[0:N, 0, k * 128:(k + 1) * 128], rows[:, k, :], ident[:])
                tr.then_inc(s["turned_back"], 1)
                for j in range(8):
                    lo = j % 4 * Q
                    if j >= 4:
                        pe.wait_ge(s["added"], j - 3)
                    pe.matmul(ps[0:N, 1 + j % 4, :], rows[:, j // 4, :], b2[:, lo:lo + Q, :].rearrange("p b d -> p (b d)"),
                              start=True, stop=True).then_inc(s["bias_made"], 1)
                pe.wait_ge(s["added"], 8)
                with pe.Fori(0, B // Q) as g:
                    def second(e):
                        pe.wait_ge(s["hid_ready"], 2 * E * g + 2 * e + 2)
                        pe.wait_ge(s["added"], 8 + E * g + e - 1)
                        for i in range(Q):
                            for c in range(2):
                                mm = pe.matmul(ps[0:N, 6 + e % 2, i * D:(i + 1) * D], hid[:, e % 2, c, i * N:(i + 1) * N],
                                               w2[:, e, c, :], start=(c == 0), stop=(c == 1))
                        mm.then_inc(s["out_made"], 1)

                    for e in range(E):
                        for c in range(2):
                            if e >= 2:
                                pe.wait_ge(s["hid_ready"], 2 * E * g + 2 * e + c - 3)
                            pe.matmul(ps[:, 2 + (2 * e + c) % 4, 0:Q * N], w1[:, e, c * 128:(c + 1) * 128],
                                      hT[:, bass.ds(g * Q, Q), :].rearrange("p b n -> p (b n)"),
                                      start=True, stop=True).then_inc(s["hid_made"], 1)
                        if e:
                            second(e - 1)
                    second(E - 1)

            @block.scalar
            def _(act):
                act.wait_ge(s["shifted"], 1)
                act.activation(gate[:], gate[:], ACT.Exp).then_inc(s["raised"], 1)
                with act.Fori(0, B // Q) as g:
                    for e in range(E):
                        for c in range(2):
                            act.wait_ge(s["hid_made"], 2 * E * g + 2 * e + c + 1)
                            if e >= 2:
                                act.wait_ge(s["out_made"], E * g + e - 1)
                            act.activation(hid[:, e % 2, c, :], ps[:, 2 + (2 * e + c) % 4, 0:Q * N], ACT.Gelu,
                                           bias=b1[:, e, c:c + 1]).then_inc(s["hid_ready"], 1)

            @block.vector
            def _(dve):
                steps = Steps(dve, s["dve_step"])
                steps.done(dve.memset(ones[:], 1.0))
                dve.wait_ge(s["scores_made"], 1)
                scores = ps[0:N, 0, 0:B * E].rearrange("p (b e) -> p b e", e=E)
                steps.done(dve.tensor_reduce(peak[:], scores, AX_X, ALU.max))
                dve.tensor_tensor(gate[:], scores, peak[:].unsqueeze(2).broadcast_to(wide), ALU.subtract).then_inc(s["shifted"], 1)
                dve.wait_ge(s["raised"], 1)
                steps.done(dve.tensor_reduce(total[:], gate[:], AX_X, ALU.add))
                steps.done(dve.reciprocal(inv[:], total[:]))
                dve.tensor_tensor(gate[:], gate[:], inv[:].unsqueeze(2).broadcast_to(wide), ALU.mult).then_inc(s["gate_ready"], 1)
                dve.wait_ge(s["rows_made"], 1)
                steps.done(dve.tensor_copy(rows[:], ps[:, 1, 0:2 * N].rearrange("p (k n) -> p k n", k=2)))
                steps.done(dve.tensor_copy(left[:], rows[:]))
                for k in range(2):
                    for r in range(TOP // 8):
                        steps.done(dve.max(best[:, k, r, :], left[:, k, :]))
                        steps.done(dve.match_replace(left[:, k, :], best[:, k, r, :], left[:, k, :], -1.0))
                    steps.done(dve.max(best[:, k, TOP // 8, :], left[:, k, :]))
                    last = best[:, k, TOP // 8, TOP % 8 - 1:TOP % 8]
                    steps.done(dve.tensor_scalar(above[:, k, :], rows[:, k, :], last, None, ALU.is_gt))
                    steps.done(dve.tensor_scalar(equal[:, k, :], rows[:, k, :], last, None, ALU.is_equal))
                    steps.done(dve.tensor_reduce(room[:, k:k + 1], above[:, k, :], AX_X, ALU.add))
                    steps.done(dve.tensor_scalar(room[:, k:k + 1], room[:, k:k + 1], -1.0, float(TOP), ALU.mult, ALU.add))
                    steps.done(dve.tensor_tensor_scan(rank[:, k, :], ones[:], equal[:, k, :], 0.0, ALU.mult, ALU.add))
                    steps.done(dve.scalar_tensor_tensor(equal[:, k, :], rank[:, k, :], room[:, k:k + 1], equal[:, k, :],
                                                        ALU.is_le, ALU.mult))
                    steps.done(dve.tensor_tensor(above[:, k, :], above[:, k, :], equal[:, k, :], ALU.add))
                dve.tensor_tensor(rows[:], rows[:], above[:], ALU.mult).then_inc(s["chosen"], 1)
                dve.wait_ge(s["turned_back"], 1)
                steps.done(dve.tensor_copy(gate[:], ps[0:N, 0, 0:B * E].rearrange("p (b e) -> p b e", e=E)))
                for j in range(8):
                    dve.wait_ge(s["bias_made"], j + 1)
                    part = h[:, Q * j:Q * j + Q, :]
                    signal(dve, dve.tensor_tensor(part, ps[0:N, 1 + j % 4, :].rearrange("p (b d) -> p b d", d=D), part,
                                                  ALU.add), s["added"], j + 1)
                with dve.Fori(0, B // Q) as g:
                    for e in range(E):
                        dve.wait_ge(s["out_made"], E * g + e + 1)
                        for i in range(Q):
                            row = h[:, g * Q + i, :]
                            one = dve.scalar_tensor_tensor(row, ps[0:N, 6 + e % 2, i * D:(i + 1) * D], gate[:, g * Q + i, e:e + 1],
                                                           row, ALU.mult, ALU.add)
                        signal(dve, one, s["added"], 8 + E * g + e + 1)


def relative_attention(nc, h, hT, ps, ident, dram):
    J = 2 * N - 1
    W = H * N
    SCALE = D ** -0.5
    r_dram = nc.dram_tensor("ra_shift_scores", (B, N, H * J), F32, kind="Internal").ap()
    e_dram = nc.dram_tensor("ra_shift_probs", (2, N, H * J), F32, kind="Internal").ap()

    def skewed(dram_ap, i):
        return bass.AP(dram_ap.tensor, i * (N * H * J) + N - 1, [[H * J - 1, N], [J, H], [1, N]])

    with Phase(nc, "ra") as outer:
        scores = outer.sb("scores", [N, B, W])
        V = outer.sb("V", [N, B, D])
        with Phase(nc, "rp") as ph:
            sb = ph.sb
            w_q, w_k, w_v = sb("w_q", [D, D]), sb("w_k", [D, D]), sb("w_v", [D, D])
            b_q, b_k, b_v = sb("b_q", [D, 1]), sb("b_k", [D, 1]), sb("b_v", [N, D])
            rel_k, head_mask = sb("rel_k", [D, J]), sb("head_mask", [D, H])
            b_out = sb("b_out", [N, D])
            xT, qT, kT = sb("xT", [D, N]), sb("qT", [D, N]), sb("kT", [D, N])
            q_head = sb("q_head", [D, H, N])
            shift = sb("shift", [N, 2, 4, 2 * J])
            names = ("consts_in xT_ready q_made k_made qT_ready kT_ready q_head_ready V_ready scores_made "
                     "scores_ready shift_made shift_dve shift_act shift_out0 shift_out1 bias_added").split()
            s = {n: ph.sem(n) for n in names}
            shift_out = (s["shift_out0"], s["shift_out1"])
            loads = [(w_q, "ra_w_q"), (w_k, "ra_w_k"), (w_v, "ra_w_v"), (b_q, "ra_b_q"), (b_k, "ra_b_k"),
                     (rel_k, "ra_rel_k"), (head_mask, "ra_head_mask")]
            rows = [(b_v, "ra_b_v"), (b_out, "ra_b_out")]
            ALL_IN = 16 * (len(loads) + len(rows))
            with ph.block() as block:
                @block.sync
                def _(sp):
                    for tile, name in loads:
                        sp.dma_start(tile[:], dram[name]).then_inc(s["consts_in"], 16)
                    for tile, name in rows:
                        sp.dma_start(tile[:], dram[name].partition_broadcast(N)).then_inc(s["consts_in"], 16)
                    for k in range(2):
                        sp.wait_ge(shift_out[k], 16 * (B // 2))

                @block.gpsimd
                def _(pool):
                    pool.wait_ge(s["consts_in"], ALL_IN)
                    pool.tensor_tensor(h[:], h[:], b_out[:].unsqueeze(1).broadcast_to([N, B, D]), ALU.add).then_inc(s["bias_added"], 1)
                    pool.tensor_copy(xT[:], hT[:, 0, :]).then_inc(s["xT_ready"], 1)
                    with pool.Fori(1, B) as b:
                        pool.wait_ge(s["q_made"], b)
                        pool.tensor_copy(xT[:], hT[:, b, :]).then_inc(s["xT_ready"], 1)

                @block.tensor
                def _(pe):
                    def image(b, first):
                        if not first:
                            pe.wait_ge(s["kT_ready"], b)
                            pe.wait_ge(s["V_ready"], b)
                        pe.matmul(ps[:, 7, 0:N], w_k[:], hT[:, b, :], start=True, stop=True).then_inc(s["k_made"], 1)
                        pe.matmul(ps[:, 0, 0:N], w_q[:], hT[:, b, :], start=True, stop=True)
                        pe.wait_ge(s["xT_ready"], b + 1)
                        pe.matmul(ps[0:N, 0, 128:128 + D], xT[:], w_v[:], start=True, stop=True).then_inc(s["q_made"], 1)
                        pe.wait_ge(s["kT_ready"], b + 1)
                        pe.wait_ge(s["q_head_ready"], b + 1)
                        if not first:
                            pe.wait_ge(s["scores_ready"], b)
                        for hd in range(H):
                            mm = pe.matmul(ps[0:N, 1 + hd // HB, hd % HB * N:(hd % HB + 1) * N], q_head[:, hd, :], kT[:],
                                           start=True, stop=True)
                        mm.then_inc(s["scores_made"], 1)
                        if not first:
                            pe.wait_ge(s["shift_dve"], b)
                            pe.wait_ge(s["shift_act"], b)
                        for hd in range(H):
                            mm = pe.matmul(ps[0:N, 3 + hd // 2, hd % 2 * J:(hd % 2 + 1) * J], q_head[:, hd, :], rel_k[:],
                                           start=True, stop=True)
                            if hd % 4 == 3:
                                mm.then_inc(s["shift_made"], 1)

                    pe.wait_ge(s["consts_in"], ALL_IN)
                    image(0, True)
                    with pe.Fori(1, B) as b:
                        image(b, False)

                @block.scalar
                def _(act):
                    def image(b, k, early):
                        act.wait_ge(s["k_made"], b + 1)
                        if not early or k:
                            act.wait_ge(s["shift_made"], 2 * b)
                        act.activation(kT[:], ps[:, 7, 0:N], ACT.Identity, bias=b_k[:]).then_inc(s["kT_ready"], 1)
                        act.wait_ge(s["scores_made"], b + 1)
                        act.activation(scores[:, b, :].rearrange("p (k c) -> p k c", k=2), ps[0:N, 1:3, 0:HB * N],
                                       ACT.Copy).then_inc(s["scores_ready"], 1)
                        act.wait_ge(s["shift_made"], 2 * b + 2)
                        if not early:
                            act.wait_ge(shift_out[k], 8 * b - 8 * k)
                        act.activation(shift[:, k, 2:4, :], ps[0:N, 5:7, 0:2 * J], ACT.Copy).then_inc(s["shift_act"], 1)
                        act.wait_ge(s["shift_dve"], b + 1)
                        act.wait_ge(s["shift_act"], b + 1)
                        act.dma_start(r_dram[b, :, :], shift[:, k].rearrange("p a c -> p (a c)")).then_inc(shift_out[k], 16)

                    act.wait_ge(s["consts_in"], ALL_IN)
                    image(0, 0, True)
                    image(1, 1, True)
                    with act.Fori(2, B - 1, 2) as b:
                        image(b, 0, False)
                        image(b + 1, 1, False)

                @block.vector
                def _(dve):
                    def image(b, k, early):
                        dve.wait_ge(s["q_made"], b + 1)
                        signal(dve, dve.tensor_scalar(qT[:], ps[:, 0, 0:N], b_q[:], SCALE, ALU.add, ALU.mult), s["qT_ready"], b + 1)
                        if not early or k:
                            dve.wait_ge(s["shift_made"], 2 * b)
                        dve.tensor_tensor(q_head[:], qT[:].unsqueeze(1).broadcast_to([D, H, N]),
                                          head_mask[:].unsqueeze(2).broadcast_to([D, H, N]), ALU.mult).then_inc(s["q_head_ready"], 1)
                        dve.tensor_tensor(V[:, b, :], ps[0:N, 0, 128:128 + D], b_v[:], ALU.add).then_inc(s["V_ready"], 1)
                        dve.wait_ge(s["shift_made"], 2 * b + 1)
                        if not early:
                            dve.wait_ge(shift_out[k], 8 * b - 8 * k)
                        dve.tensor_copy(shift[:, k, 0:2, :], ps[0:N, 3:5, 0:2 * J]).then_inc(s["shift_dve"], 1)

                    dve.wait_ge(s["consts_in"], ALL_IN)
                    image(0, 0, True)
                    image(1, 1, True)
                    with dve.Fori(2, B - 1, 2) as b:
                        image(b, 0, False)
                        image(b + 1, 1, False)

        with Phase(nc, "rv") as ph:
            sb = ph.sb
            w_out, rel_v = sb("w_out", [D, D]), sb("rel_v", [N, 2, DK])
            zero = hT[0:N].rearrange("p b n -> p (b n)")[:, 0:H * J]
            bent = sb("bent", [N, 2, W])
            z = sb("z", [N, W])
            E = sb("E", [N, 2, W])
            Ej = sb("Ej", [N, 2, H * J])
            top, total, inv = sb("top", [N, H]), sb("total", [N, H]), sb("inv", [N, 2, H])
            ET, EjT = sb("ET", [N, W]), sb("EjT", [N, 2, W])
            y, yT = sb("y", [N, D]), sb("yT", [D, N])
            names = ("consts_in zeroed bent_in0 bent_in1 summed shifted raised inv_ready E_out0 E_out1 Ej_in0 Ej_in1 "
                     "ET_made ET_ready EjT_made0 EjT_made1 EjT_ready0 EjT_ready1 y_made y_ready yT_made yT_ready out_made "
                     "added zero_set dve_step").split()
            s = {n: ph.sem(n) for n in names}
            bent_in, E_out, Ej_in = ([s[f"{n}{k}"] for k in range(2)] for n in ("bent_in", "E_out", "Ej_in"))

            def lagged(engine, front, back):
                front(0, 0, True)
                front(1, 1, True)
                back(0, 0, True)
                front(2, 0, False)
                back(1, 1, True)
                with engine.Fori(3, B - 4, 2) as b:
                    front(b, 1, False)
                    back(b - 1, 0, False)
                    front(b + 1, 0, False)
                    back(b, 1, False)
                for b in (B - 3, B - 2, B - 1):
                    front(b, b % 2, False)
                    back(b - 1, 1 - b % 2, False)
                back(B - 1, 1, False)

            def turn(b, k):
                return 8 * b - 8 * k + 16

            with ph.block() as block:
                @block.sync
                def _(sp):
                    sp.dma_start(w_out[:], dram["ra_w_out"]).then_inc(s["consts_in"], 16)
                    sp.dma_start(rel_v[:], dram["ra_rel_v"]).then_inc(s["consts_in"], 16)
                    sp.wait_ge(s["zero_set"], 1)
                    for k in range(2):
                        sp.dma_start(e_dram[k, :, :], zero).then_inc(s["zeroed"], 16)
                    sp.wait_ge(s["zeroed"], 32)

                    def store_and_reload(b, k, early):
                        sp.wait_ge(s["raised"], b + 1)
                        if not early:
                            sp.wait_ge(Ej_in[k], turn(b, k) - 16)
                        sp.dma_start(skewed(e_dram, k), E[:, k, :].rearrange("p (h n) -> p h n", h=H)).then_inc(E_out[k], 16)
                        sp.wait_ge(E_out[k], turn(b, k))
                        if not early:
                            sp.wait_ge(s["EjT_made1"], b - 1)
                        sp.dma_start(Ej[:, k, :], e_dram[k, :, :]).then_inc(Ej_in[k], 16)

                    for b in range(B):
                        store_and_reload(b, b % 2, b < 2)

                @block.tensor
                def _(pe):
                    pe.wait_ge(s["consts_in"], 32)

                    def image(b, k, first):
                        pe.wait_ge(s["raised"], b + 1)
                        for hd in range(H):
                            tr = pe.transpose(ps[0:N, hd // HB, hd % HB * N:(hd % HB + 1) * N], E[:, k, hd * N:(hd + 1) * N],
                                              ident[0:N, 0:N])
                        tr.then_inc(s["ET_made"], 1)
                        pe.wait_ge(Ej_in[k], turn(b, k))
                        for c, lo, hi in ((0, 0, N), (1, N, J)):
                            for hd in range(H):
                                tr = pe.transpose(ps[0:hi - lo, 3 + 2 * c + hd // HB, hd % HB * N:(hd % HB + 1) * N],
                                                  Ej[:, k, hd * J + lo:hd * J + hi], ident[0:N, 0:N])
                            tr.then_inc(s[f"EjT_made{c}"], 1)
                        pe.wait_ge(s["ET_ready"], b + 1)
                        pe.wait_ge(s["EjT_ready0"], b + 1)
                        pe.wait_ge(s["EjT_ready1"], b + 1)
                        for hd in range(H):
                            out = ps[0:N, 2, hd * DK:(hd + 1) * DK]
                            c = slice(hd * N, (hd + 1) * N)
                            pe.matmul(out, ET[:, c], V[:, b, hd * DK:(hd + 1) * DK], start=True, stop=False)
                            pe.matmul(out, EjT[:, 0, c], rel_v[:, 0, :], start=False, stop=False)
                            mm = pe.matmul(out, EjT[0:J - N, 1, c], rel_v[0:J - N, 1, :], start=False, stop=True)
                        mm.then_inc(s["y_made"], 1)
                        pe.wait_ge(s["y_ready"], b + 1)
                        pe.transpose(ps[0:D, 7, 0:N], y[:], ident[0:N, 0:N]).then_inc(s["yT_made"], 1)
                        pe.wait_ge(s["yT_ready"], b + 1)
                        pe.matmul(ps[0:N, 7, 128:128 + D], yT[:], w_out[:], start=True, stop=True).then_inc(s["out_made"], 1)

                    image(0, 0, True)
                    image(1, 1, False)
                    with pe.Fori(2, B - 1, 2) as b:
                        image(b, 0, False)
                        image(b + 1, 1, False)

                @block.scalar
                def _(act):
                    def load_bent(b, k):
                        act.dma_start(bent[:, k, :].rearrange("p (h n) -> p h n", h=H), skewed(r_dram, b)).then_inc(bent_in[k], 16)

                    def front(b, k, early):
                        act.wait_ge(s["shifted"], b + 1)
                        if not early:
                            act.wait_ge(s["ET_made"], b - 1)
                            act.wait_ge(E_out[k], turn(b, k) - 16)
                        act.activation(E[:, k, :], z[:], ACT.Exp).then_inc(s["raised"], 1)
                        if not isinstance(b, int) or b + 2 < B:
                            load_bent(b + 2, k)

                    def back(b, k, early):
                        act.wait_ge(s["ET_made"], b + 1)
                        act.activation(ET[:].rearrange("p (k c) -> p k c", k=2), ps[0:N, 0:2, 0:HB * N], ACT.Copy).then_inc(s["ET_ready"], 1)
                        act.wait_ge(s["EjT_made1"], b + 1)
                        act.activation(EjT[0:J - N, 1, :].rearrange("p (k c) -> p k c", k=2), ps[0:J - N, 5:7, 0:HB * N],
                                       ACT.Copy).then_inc(s["EjT_ready1"], 1)
                        act.wait_ge(s["yT_made"], b + 1)
                        act.activation(yT[:], ps[0:D, 7, 0:N], ACT.Copy).then_inc(s["yT_ready"], 1)

                    load_bent(0, 0)
                    load_bent(1, 1)
                    lagged(act, front, back)

                @block.vector
                def _(dve):
                    dve.memset(zero, 0.0).then_inc(s["zero_set"], 1)

                    def front(b, k, early):
                        def chain(i, instruction):
                            signal(dve, instruction, s["dve_step"], 3 * b + i)

                        z3 = z[:].rearrange("p (h n) -> p h n", h=H)
                        dve.wait_ge(bent_in[k], turn(b, k))
                        if not (early and k == 0):
                            dve.wait_ge(s["raised"], b)
                        signal(dve, dve.tensor_tensor(z[:], scores[:, b, :], bent[:, k, :], ALU.add), s["summed"], b + 1)
                        chain(1, dve.tensor_reduce(top[:], z3, AX_X, ALU.max))
                        dve.tensor_tensor(z3, z3, top[:].unsqueeze(2).broadcast_to([N, H, N]), ALU.subtract).then_inc(s["shifted"], 1)
                        dve.wait_ge(s["raised"], b + 1)
                        chain(2, dve.tensor_reduce(total[:], E[:, k, :].rearrange("p (h n) -> p h n", h=H), AX_X, ALU.add))
                        chain(3, dve.reciprocal(inv[:, k, :], total[:]))

                    def back(b, k, early):
                        dve.wait_ge(s["EjT_made0"], b + 1)
                        dve.tensor_copy(EjT[:, 0, :].rearrange("p (k c) -> p k c", k=2), ps[0:N, 3:5, 0:HB * N]).then_inc(s["EjT_ready0"], 1)
                        dve.wait_ge(s["y_made"], b + 1)
                        dve.tensor_tensor(y[:].rearrange("p (h d) -> p h d", h=H), ps[0:N, 2, 0:D].rearrange("p (h d) -> p h d", h=H),
                                          inv[:, k, :].unsqueeze(2).broadcast_to([N, H, DK]), ALU.mult).then_inc(s["y_ready"], 1)
                        dve.wait_ge(s["out_made"], b + 1)
                        signal(dve, dve.tensor_tensor(h[:, b, :], ps[0:N, 7, 128:128 + D], h[:, b, :], ALU.add), s["added"], b + 1)

                    lagged(dve, front, back)


def lstm_experts(nc, h, hT, ps, ident, dram):
    E, K, T = 8, 2, B
    C = K * N
    m_dram = nc.dram_tensor("ls_masks", (T * E * K, N), F32, kind="Internal").ap()
    w_dram = nc.dram_tensor("ls_weights", (T * E * K, N), F32, kind="Internal").ap()

    with Phase(nc, "lr") as ph:
        sb = ph.sb
        w_route, b_route, order = sb("w_route", [D, E]), sb("b_route", [N, E]), sb("order", [N, E])
        logit, pick = sb("logit", [N, T, E]), sb("pick", [N, T, E])
        best, late = sb("best", [N, K, T]), sb("late", [N, T])
        ratio, weight = sb("ratio", [N, T]), sb("weight", [N, K, T])
        mask, wmask = sb("mask", [N, T, E, K]), sb("wmask", [N, T, E, K])
        turned = sb("turned", [128, 2, 4, N])
        names = "consts_in logits_made gap_ready ratio_ready masks_ready turned_made turned_ready stored dve_step".split()
        s = {n: ph.sem(n) for n in names}
        wide = [N, T, E]
        with ph.block() as block:
            @block.sync
            def _(sp):
                sp.dma_start(w_route[:], dram["ls_w_route"]).then_inc(s["consts_in"], 16)
                sp.dma_start(b_route[:], dram["ls_b_route"].partition_broadcast(N)).then_inc(s["consts_in"], 16)
                sp.dma_start(order[:], dram["ls_order"].partition_broadcast(N)).then_inc(s["consts_in"], 16)
                for i, out in enumerate((m_dram, w_dram)):
                    sp.wait_ge(s["turned_ready"], i + 1)
                    sp.dma_start(out.rearrange("(k p) n -> p k n", p=128), turned[:, i]).then_inc(s["stored"], 16)
                sp.wait_ge(s["stored"], 32)

            @block.tensor
            def _(pe):
                pe.wait_ge(s["consts_in"], 48)
                for b in range(T):
                    mm = pe.matmul(ps[0:N, 0, b * E:(b + 1) * E], hT[:, b, :], w_route[:], start=True, stop=True)
                mm.then_inc(s["logits_made"], 1)
                for i, m in enumerate((mask, wmask)):
                    pe.wait_ge(s["masks_ready"], i + 1)
                    for k in range(4):
                        tr = pe.transpose(ps[:, 1 + i, k * N:(k + 1) * N], m[:, 8 * k:8 * k + 8].rearrange("p t e k -> p (t e k)"),
                                          ident[0:N, 0:N])
                    tr.then_inc(s["turned_made"], 1)

            @block.scalar
            def _(act):
                act.wait_ge(s["gap_ready"], 1)
                act.activation(ratio[:], ratio[:], ACT.Exp).then_inc(s["ratio_ready"], 1)
                for i in range(2):
                    act.wait_ge(s["turned_made"], i + 1)
                    act.activation(turned[:, i], ps[:, 1 + i, 0:4 * N].rearrange("p (k n) -> p k n", k=4), ACT.Copy).then_inc(s["turned_ready"], 1)

            @block.vector
            def _(dve):
                steps = Steps(dve, s["dve_step"])
                dve.wait_ge(s["consts_in"], 48)
                dve.wait_ge(s["logits_made"], 1)
                steps.done(dve.tensor_tensor(logit[:], ps[0:N, 0, 0:T * E].rearrange("p (t e) -> p t e", e=E),
                                             b_route[:].unsqueeze(1).broadcast_to(wide), ALU.add))
                for k in range(K):
                    chosen = mask[:, :, :, k]
                    steps.done(dve.tensor_reduce(best[:, k, :], logit[:], AX_X, ALU.max))
                    steps.done(dve.tensor_tensor(pick[:], logit[:], best[:, k, :].unsqueeze(2).broadcast_to(wide), ALU.is_equal))
                    steps.done(dve.tensor_tensor(pick[:], pick[:], order[:].unsqueeze(1).broadcast_to(wide), ALU.mult))
                    steps.done(dve.tensor_reduce(late[:], pick[:], AX_X, ALU.max))
                    steps.done(dve.tensor_tensor(chosen, pick[:], late[:].unsqueeze(2).broadcast_to(wide), ALU.is_equal))
                    if k == 0:
                        steps.done(dve.tensor_scalar(pick[:], chosen, -1e38, None, ALU.mult))
                        steps.done(dve.tensor_tensor(logit[:], logit[:], pick[:], ALU.add))
                dve.tensor_tensor(ratio[:], best[:, 1, :], best[:, 0, :], ALU.subtract).then_inc(s["gap_ready"], 1)
                dve.wait_ge(s["ratio_ready"], 1)
                steps.done(dve.tensor_scalar(late[:], ratio[:], 1.0, None, ALU.add))
                steps.done(dve.reciprocal(weight[:, 0, :], late[:]))
                signal(dve, dve.tensor_tensor(weight[:, 1, :], ratio[:], weight[:, 0, :], ALU.mult), s["masks_ready"], 1)
                for k in range(K):
                    w = dve.tensor_tensor(wmask[:, :, :, k], mask[:, :, :, k], weight[:, k, :].unsqueeze(2).broadcast_to(wide), ALU.mult)
                    if k == 1:
                        w.then_inc(s["masks_ready"], 1)

    with Phase(nc, "ls") as ph:
        sb = ph.sb
        w_in, w_rec = sb("w_in", [D, E, 4, D]), sb("w_rec", [D, E, 4, D])
        bias = sb("bias", [D, E, 4])
        w_out, b_out = sb("w_out", [D, E, D]), sb("b_out", [E * K, D])
        m_all, w_all = sb("m_all", [D, 2, E, C]), sb("w_all", [D, 2, E, C])
        w_row = sb("w_row", [E * K, 2, N])
        xm = sb("xm", [D, 2, E, C])
        state, cell = sb("state", [D, E, C]), sb("cell", [D, E, C])
        gates = sb("gates", [D, 4, 4, C])
        part, fresh, tc = sb("part", [D, C]), sb("fresh", [D, C]), sb("tc", [D, 2, C])
        wh, hc = sb("wh", [D, 2, C]), sb("hc", [D, E, N])
        names = ("consts_in masks_in0 masks_in1 zero_set xm_ready gates_made gates_ready cell_ready tc_ready "
                 "state_ready hc_ready y_made y_added dve_step pool_step").split()
        s = {n: ph.sem(n) for n in names}
        masks_in = (s["masks_in0"], s["masks_in1"])

        def steps_of(engine, step):
            step(0, 0)
            step(1, 1)
            with engine.Fori(2, T - 1, 2) as t:
                step(t, 0)
                step(t + 1, 1)

        def since(t, n):
            return not isinstance(t, int) or t >= n

        with ph.block() as block:
            @block.sync
            def _(sp):
                for tile, name in ((w_in, "ls_w_in"), (w_rec, "ls_w_rec"), (bias, "ls_bias"), (w_out, "ls_w_out"), (b_out, "ls_b_out")):
                    sp.dma_start(tile[:], dram[name]).then_inc(s["consts_in"], 16)
                for t in range(T):
                    k = t % 2
                    if t >= 2:
                        sp.wait_ge(s["xm_ready"], t - 1)
                        sp.wait_ge(s["hc_ready"], E * (t - 1))
                        sp.wait_ge(s["y_made"], t - 1)
                    rows = slice(t * E * K, (t + 1) * E * K)
                    sp.dma_start(m_all[:, k].rearrange("p e c -> p (e c)"),
                                 m_dram[rows, :].rearrange("r n -> (r n)").partition_broadcast(D)).then_inc(masks_in[k], 16)
                    sp.dma_start(w_all[:, k].rearrange("p e c -> p (e c)"),
                                 w_dram[rows, :].rearrange("r n -> (r n)").partition_broadcast(D)).then_inc(masks_in[k], 16)
                    sp.dma_start(w_row[:, k], w_dram[rows, :]).then_inc(masks_in[k], 16)

            @block.gpsimd
            def _(pool):
                def mask_inputs(t, k):
                    pool.wait_ge(masks_in[k], 24 * t - 24 * k + 48)
                    if since(t, 2):
                        pool.wait_ge(s["gates_made"], E * t - E)
                    pool.tensor_tensor(xm[:, k].rearrange("p e (k n) -> p (e k) n", k=K),
                                       hT[:, t, :].unsqueeze(1).broadcast_to([D, E * K, N]),
                                       m_all[:, k].rearrange("p e (k n) -> p (e k) n", k=K), ALU.mult).then_inc(s["xm_ready"], 1)

                def combine(t, k):
                    if since(t, 1):
                        pool.wait_ge(s["y_made"], t)
                    for e in range(E):
                        pool.wait_ge(s["state_ready"], E * t + e + 1)
                        signal(pool, pool.tensor_tensor(wh[:, e % 2], state[:, e], w_all[:, k, e], ALU.mult), s["pool_step"], E * t + e + 1)
                        pool.tensor_tensor(hc[:, e], wh[:, e % 2, 0:N], wh[:, e % 2, N:C], ALU.add).then_inc(s["hc_ready"], 1)

                mask_inputs(0, 0)
                mask_inputs(1, 1)
                combine(0, 0)
                with pool.Fori(1, T - 2, 2) as t:
                    mask_inputs(t + 1, 0)
                    combine(t, 1)
                    mask_inputs(t + 2, 1)
                    combine(t + 1, 0)
                combine(T - 1, 1)

            @block.tensor
            def _(pe):
                def outputs(t, k):
                    pe.wait_ge(s["hc_ready"], E * t + E)
                    if since(t, 1):
                        pe.wait_ge(s["y_added"], t)
                    for e in range(E):
                        pe.matmul(ps[0:N, 7, 0:D], hc[:, e], w_out[:, e, :], start=(e == 0), stop=False)
                    pe.matmul(ps[0:N, 7, 0:D], w_row[:, k], b_out[:], start=False, stop=True).then_inc(s["y_made"], 1)

                def step(t, k):
                    pe.wait_ge(s["xm_ready"], t + 1)
                    for e in range(E):
                        if e >= 3:
                            pe.wait_ge(s["gates_ready"], E * t + e - 2)
                        elif since(t, 1):
                            pe.wait_ge(s["gates_ready"], E * t if e < 2 else E * t - 2)
                        if since(t, 1):
                            pe.wait_ge(s["state_ready"], E * t - E + e + 1)
                        bank = e % 3 * 2
                        for j in range(4):
                            out = ps[:, bank + j // 2, j % 2 * 256:j % 2 * 256 + C]
                            pe.matmul(out, w_in[:, e, j, :], xm[:, k, e], start=True, stop=False)
                            mm = pe.matmul(out, w_rec[:, e, j, :], state[:, e], start=False, stop=True)
                        mm.then_inc(s["gates_made"], 1)
                        if e == 3 and since(t, 1):
                            outputs(t - 1, 1 - k)

                pe.wait_ge(s["consts_in"], 80)
                pe.wait_ge(s["zero_set"], 2)
                steps_of(pe, step)
                outputs(T - 1, 1)

            @block.scalar
            def _(act):
                def cell_tanh(t, e):
                    act.wait_ge(s["cell_ready"], E * t + e + 1)
                    act.activation(tc[:, e % 2], cell[:, e], ACT.Tanh).then_inc(s["tc_ready"], 1)

                def step(t, k):
                    for e in range(E):
                        act.wait_ge(s["gates_made"], E * t + e + 1)
                        if e >= 4 or since(t, 1):
                            act.wait_ge(s["state_ready"], E * t + e - 3)
                        bank = e % 3 * 2
                        view = ps[:, bank:bank + 2, :].rearrange("p k (j c) -> p (k j) c", j=2)
                        for j in range(4):
                            g = act.activation(gates[:, e % 4, j], view[:, j, 0:C], ACT.Tanh if j == 3 else ACT.Sigmoid,
                                               bias=bias[:, e, j:j + 1])
                        g.then_inc(s["gates_ready"], 1)
                        if e:
                            cell_tanh(t, e - 1)
                    cell_tanh(t, E - 1)

                act.wait_ge(s["consts_in"], 80)
                steps_of(act, step)

            @block.vector
            def _(dve):
                def new_state(t, e):
                    dve.wait_ge(s["tc_ready"], E * t + e + 1)
                    if since(t, 1):
                        dve.wait_ge(s["hc_ready"], E * t - E + e + 1)
                    dve.tensor_tensor(state[:, e], gates[:, e % 4, 2], tc[:, e % 2], ALU.mult).then_inc(s["state_ready"], 1)

                def add_outputs(t):
                    dve.wait_ge(s["y_made"], t + 1)
                    dve.tensor_tensor(h[:, t, :], ps[0:N, 7, 0:D], h[:, t, :], ALU.add).then_inc(s["y_added"], 1)

                def step(t, k):
                    for e in range(E):
                        n = 2 * E * t + 2 * e
                        dve.wait_ge(s["gates_ready"], E * t + e + 1)
                        g = gates[:, e % 4]
                        signal(dve, dve.tensor_tensor(part[:], g[:, 1], cell[:, e], ALU.mult), s["dve_step"], n + 1)
                        signal(dve, dve.tensor_tensor(fresh[:], g[:, 0], g[:, 3], ALU.mult), s["dve_step"], n + 2)
                        signal(dve, dve.tensor_tensor(cell[:, e], part[:], fresh[:], ALU.add), s["cell_ready"], E * t + e + 1)
                        if e:
                            new_state(t, e - 1)
                        if e == 5 and since(t, 1):
                            add_outputs(t - 1)
                    new_state(t, E - 1)

                signal(dve, dve.memset(state[:], 0.0), s["zero_set"], 1)
                signal(dve, dve.memset(cell[:], 0.0), s["zero_set"], 2)
                steps_of(dve, step)
                add_outputs(T - 1)



def build(nc, dram, out):
    with ExitStack() as ctx:
        def sb(name, shape):
            return ctx.enter_context(nc.sbuf_tensor(name, shape, F32))

        h = sb("h", [N, B, D])
        hT = sb("hT", [D, B, N])
        ident = sb("ident", [128, 128])
        eps = sb("eps", [128, 1])
        ps = ctx.enter_context(nc.psum_tensor("ps", [128, 8, BANK], F32))
        const_in = ctx.enter_context(nc.semaphore("const_in"))
        eps_set = ctx.enter_context(nc.semaphore("eps_set"))
        with nc.Block() as block:
            @block.sync
            def _(sp):
                sp.dma_start(ident[:], dram["ident"]).then_inc(const_in, 16)
                sp.wait_ge(const_in, 16)

            @block.vector
            def _(dve):
                dve.memset(eps[:], LN_EPS).then_inc(eps_set, 1)
                dve.wait_ge(eps_set, 1)

        tokenize(nc, h, ps, ident, eps, dram)
        norm_and_turn(nc, "la_norm", h, hT, ps, ident, eps)
        logic_attention(nc, h, hT, ps, ident, dram)
        norm_and_turn(nc, "ec_norm", h, hT, ps, ident, eps)
        expert_choice(nc, h, hT, ps, ident, dram)
        norm_and_turn(nc, "ra_norm", h, hT, ps, ident, eps)
        relative_attention(nc, h, hT, ps, ident, dram)
        norm_and_turn(nc, "ls_norm", h, hT, ps, ident, eps)
        lstm_experts(nc, h, hT, ps, ident, dram)
        out_done = ctx.enter_context(nc.semaphore("out_done"))
        with nc.Block() as block:
            @block.sync
            def _(sp):
                sp.dma_start(out.rearrange("b t d -> t b d"), h[:]).then_inc(out_done, 16)
                sp.wait_ge(out_done, 16)


def host_layout(a):
    P = {}
    x = a["x"]
    cells = x.reshape(B, 3, 6, 2, 8, 12, 8)
    v = cells.transpose(3, 4, 6, 1, 0, 2, 5).reshape(128, 3, B * 6, 12)
    P["x_v"] = np.pad(v, ((0, 0), (0, 0), (0, 0), (1, 1)))
    cells = x.reshape(B, 3, 12, 8, 6, 2, 8)
    v = cells.transpose(5, 3, 6, 1, 0, 2, 4).reshape(128, 3, B, 12, 6)
    P["x_h"] = np.pad(v, ((0, 0), (0, 0), (0, 0), (1, 1), (0, 0)))
    wm = a["L0_tok_W_main"].reshape(64, 3, 2, 8, 2, 8)
    wx = a["L0_tok_W_sx"].reshape(16, 3, 2, 8, 2, 8)
    wy = a["L0_tok_W_sy"].reshape(16, 3, 2, 8, 2, 8)
    wv = np.zeros((128, 4, 3, D), np.float32)
    wh = np.zeros((128, 4, 3, D), np.float32)
    for half in range(2):
        vert = lambda w: w[:, :, :, :, half, :].transpose(2, 3, 4, 1, 0).reshape(128, 3, -1)
        horz = lambda w: w[:, :, half].transpose(3, 2, 4, 1, 0).reshape(128, 3, -1)
        wv[:, 1 + half, :, 0:64] = vert(wm)
        wv[:, 2 + half, :, 64:80] = vert(wx)
        wv[:, 0 + half, :, 80:96] = vert(wx)
        wh[:, 2 + half, :, 96:112] = horz(wy)
        wh[:, 0 + half, :, 112:128] = horz(wy)
    P["tok_wv"], P["tok_wh"] = wv, wh
    bx, by = a["L0_tok_b_sx"], a["L0_tok_b_sy"]
    P["tok_bias"] = np.concatenate([a["L0_tok_b_main"], bx, bx, by, by]).reshape(D, 1)
    P["tok_gain"], P["tok_shift"] = a["L0_tok_ln_g"], a["L0_tok_ln_b"]
    P["txt"] = a["txt"]
    P["ident"] = np.eye(128, dtype=np.float32)
    q1, k1, v1 = np.split(a["L0_attn_qkv1_w"], 3, axis=1)
    q2, k2, v2 = np.split(a["L0_attn_qkv2_w"], 3, axis=1)
    stack = lambda *w: np.stack([m.reshape(D, 4, 2, DK) for m in w], axis=3).reshape(D, 4, 128)
    P["la_w_m"], P["la_w_n"] = stack(k1, k2, q1, q2), stack(q1, q2, k1, k2)
    P["la_w_v"] = np.concatenate([v1, v2], axis=1)
    P["la_w_out"] = a["L0_attn_proj_w"]
    row = np.arange(128)
    which, parity = row % 64 // DK, row // 64
    P["la_c_mask"] = np.stack([(which == i) & (parity == q) for i in range(2) for q in range(2)], 1) * np.float32(DK ** -0.5)
    P["la_q_mask"] = np.stack([parity == 0, parity == 1], 1).astype(np.float32)
    conv1 = a["L0_attn_conv1_w"]
    P["la_w_exp"] = conv1.T[which]
    P["la_w_sel"] = conv1.T[4 + parity]
    key = np.arange(15)[:, None] * 8 + np.arange(8)[None, :]
    own = np.where(np.arange(15)[:, None] < 8, key, key - (N - 64))
    P["la_sel_hot"] = ((row % 64)[:, None, None] == own[None]).astype(np.float32)
    P["la_g_hot"] = (row[:, None] // 16 == np.arange(8)).astype(np.float32)
    P["la_w2_rows"] = a["L0_attn_conv2_w"].T[row % 16]
    P["la_b1"] = a["L0_attn_conv1_b"][row % 16].reshape(128, 1)
    P["la_b2"] = a["L0_attn_conv2_b"]
    P["la_chain"] = a["L0_attn_chain_logit"].reshape(1)
    P["ec_w_gate"] = a["L0_ffn_Wg"]
    P["ec_w1"] = a["L0_ffn_W1"].transpose(1, 0, 2)
    P["ec_b1"] = a["L0_ffn_b1"].reshape(8, 2, 128).transpose(2, 0, 1)
    P["ec_w2"] = a["L0_ffn_W2"].reshape(8, 2, 128, D).transpose(2, 0, 1, 3)
    b2 = np.zeros((16, 8, 16, D), np.float32)
    b2[np.arange(16), :, np.arange(16), :] = a["L0_ffn_b2"]
    P["ec_b2"] = b2.reshape(128, 16, D)
    for n, w in (("q", "Wq"), ("k", "Wk"), ("v", "Wv"), ("out", "Wo")):
        P["ra_w_" + n] = a["L1_attn_" + w]
    P["ra_b_q"], P["ra_b_k"] = a["L1_attn_bq"].reshape(D, 1), a["L1_attn_bk"].reshape(D, 1)
    P["ra_b_v"], P["ra_b_out"] = a["L1_attn_bv"], a["L1_attn_bo"]
    far = a["L1_attn_rel_k"].shape[0] // 2
    place = np.clip(np.arange(2 * N - 1) - (N - 1), -far, far) + far
    P["ra_rel_k"] = np.tile(a["L1_attn_rel_k"][place].T, (H, 1))
    rel_v = np.zeros((2 * N, DK), np.float32)
    rel_v[:2 * N - 1] = a["L1_attn_rel_v"][place]
    P["ra_rel_v"] = rel_v.reshape(2, N, DK).transpose(1, 0, 2)
    P["ra_head_mask"] = (np.arange(D)[:, None] // DK == np.arange(H)).astype(np.float32)
    P["ls_w_route"], P["ls_b_route"] = a["L1_ffn_router_w"], a["L1_ffn_router_b"]
    P["ls_order"] = np.arange(8, 0, -1).astype(np.float32)
    gate = [0, 1, 3, 2]
    for n, w in (("in", "Wi"), ("rec", "Wh")):
        P["ls_w_" + n] = a["L1_ffn_" + w].reshape(8, D, 4, D)[:, :, gate].transpose(1, 0, 2, 3)
    P["ls_bias"] = a["L1_ffn_b"].reshape(8, 4, D)[:, gate].transpose(2, 0, 1)
    P["ls_w_out"] = a["L1_ffn_Wo"].transpose(1, 0, 2)
    P["ls_b_out"] = np.repeat(a["L1_ffn_bo"], 2, axis=0)
    return {k: np.ascontiguousarray(v) for k, v in P.items()}


def kernel(**inputs):
    import concourse.bacc as bacc
    from concourse.bass_utils import run_bass_kernel_spmd

    nc = bacc.Bacc("TRN2", target_bir_lowering=False, num_devices=1)
    arrays = host_layout({k: np.asarray(v) for k, v in inputs.items()})
    dram = {k: nc.dram_tensor("in_" + k, v.shape, F32, kind="ExternalInput").ap() for k, v in arrays.items()}
    out = nc.dram_tensor("out_dram", (B, N, D), F32, kind="ExternalOutput").ap()
    build(nc, dram, out)
    r = run_bass_kernel_spmd(nc, [{"in_" + k: v for k, v in arrays.items()}], core_ids=[0])
    return r.results[0]["out_dram"]
```

```python
from contextlib import ExitStack, contextmanager

import numpy as np
import concourse.bass as bass
from concourse import mybir

F32 = mybir.dt.float32
F16 = mybir.dt.float16
ALU = mybir.AluOpType
ACT = mybir.ActivationFunctionType
AX_X = mybir.AxisListType.X

B = 32
NT = 36
TX = 77
N = NT + TX
D = 128
H = 8
DK = D // H
LN_EPS = 1e-5
BANK = 512
HB = 4


class Steps:

    def __init__(self, engine, sem, loop=0, per=0):
        self.engine, self.sem, self.base, self.per, self.n = engine, sem, loop * per, per, 0

    def done(self, instruction):
        instruction.then_inc(self.sem, 1)
        self.n += 1
        self.engine.wait_ge(self.sem, self.base + self.n)

    def close(self):
        assert self.n == self.per, (self.n, self.per)


class Phase:

    def __init__(self, nc, name):
        self.nc, self.name, self.ctx, self.sems = nc, name, ExitStack(), []

    def __enter__(self):
        return self

    def __exit__(self, *args):
        self.nc.clear_and_free_semaphores(self.sems)
        self.nc.all_engine_barrier()
        self.ctx.close()

    def sb(self, name, shape, dtype=F32):
        return self.ctx.enter_context(self.nc.sbuf_tensor(f"{self.name}_{name}", shape, dtype))

    def sem(self, name):
        self.sems.append(self.nc.alloc_semaphore(f"{self.name}_{name}"))
        return self.sems[-1]

    def block(self):
        return self.nc.Block()


def over_banks(ps, bank, banks, parts, width):
    return ps[0:parts, bank:bank + banks, 0:HB * width].rearrange("p k (h n) -> p k h n", h=HB)


def mean_and_rstd(ph, tag, parts):
    return dict(
        stats=ph.sb(f"{tag}_stats", [parts, B, 6]), mean=ph.sb(f"{tag}_mean", [parts, B]),
        diff=ph.sb(f"{tag}_diff", [parts, B]), var=ph.sb(f"{tag}_var", [parts, B]),
        std=ph.sb(f"{tag}_std", [parts, B]), rstd=ph.sb(f"{tag}_rstd", [parts, B]))


def ln_statistics(dve, steps, x, parts, t, var_ready, std_ready, stats_done):
    with dve.Fori(0, B) as b:
        dve.bn_stats(t["stats"][:, b, :], x[0:parts, b, :]).then_inc(stats_done, 1)
    dve.wait_ge(stats_done, B)
    st = t["stats"]
    steps.done(dve.tensor_tensor(t["mean"][:], st[:, :, 1], st[:, :, 4], ALU.add))
    steps.done(dve.tensor_tensor(t["diff"][:], st[:, :, 1], st[:, :, 4], ALU.subtract))
    steps.done(dve.tensor_tensor(t["var"][:], st[:, :, 2], st[:, :, 5], ALU.add))
    steps.done(dve.tensor_tensor(t["diff"][:], t["diff"][:], t["diff"][:], ALU.mult))
    steps.done(dve.tensor_scalar(t["mean"][:], t["mean"][:], 0.5, None, ALU.mult))
    steps.done(dve.tensor_scalar(t["var"][:], t["var"][:], 1.0 / D, None, ALU.mult))
    dve.scalar_tensor_tensor(t["var"][:], t["diff"][:], 0.25, t["var"][:], ALU.mult, ALU.add).then_inc(var_ready, 1)
    dve.wait_ge(std_ready, 1)
    steps.done(dve.reciprocal(t["rstd"][:], t["std"][:]))


def tokenize(nc, h, ps, ident, eps, dram):
    CW = 14
    with Phase(nc, "tok") as ph:
        xv = ph.sb("xv", [128, 3, B * 6, CW])
        xh = ph.sb("xh", [128, 3, B, CW, 6])
        wv = ph.sb("wv", [128, 4, 3, D])
        wh = ph.sb("wh", [128, 4, 3, D])
        bias = ph.sb("bias", [D, 1])
        gain = ph.sb("gain", [NT, D])
        shift = ph.sb("shift", [NT, D])
        tokT = ph.sb("tokT", [D, B * NT])
        tok = ph.sb("tok", [NT, B, D])
        t = mean_and_rstd(ph, "ln", NT)
        loads, txt_in, out_ready, tokT_ready, rows_ready = (ph.sem(s) for s in (
            "loads", "txt_in", "out_ready", "tokT_ready", "rows_ready"))
        var_ready, std_ready, stats_done, dve_step = (ph.sem(s) for s in (
            "var_ready", "std_ready", "stats_done", "dve_step"))
        weights_in = ph.sem("weights_in")
        IB = [11, 11, 10]

        with ph.block() as block:
            @block.sync
            def _(sp):
                sp.dma_start(wv[:], dram["tok_wv"]).then_inc(weights_in, 16)
                sp.dma_start(xv[:], dram["x_v"]).then_inc(loads, 16)
                sp.dma_start(wh[:], dram["tok_wh"]).then_inc(weights_in, 16)
                sp.dma_start(xh[:], dram["x_h"]).then_inc(loads, 16)
                sp.dma_start(bias[:], dram["tok_bias"]).then_inc(weights_in, 16)
                sp.dma_start(gain[:], dram["tok_gain"].partition_broadcast(NT)).then_inc(weights_in, 16)
                sp.dma_start(shift[:], dram["tok_shift"].partition_broadcast(NT)).then_inc(weights_in, 16)
                sp.dma_start(h[NT:N, :, :], dram["txt"].rearrange("b t d -> t b d")).then_inc(txt_in, 16)
                sp.wait_ge(txt_in, 16)

            @block.tensor
            def _(pe):
                pe.wait_ge(weights_in, 80)
                pe.wait_ge(loads, 32)
                b0 = 0
                for k, nb in enumerate(IB):
                    out = ps[:, k, 0:nb * NT]
                    for p in range(4):
                        for c in range(3):
                            pe.matmul(out, wv[:, p, c, :], xv[:, c, 6 * b0:6 * (b0 + nb), p:p + 11:2],
                                      start=(p == 0 and c == 0), stop=False)
                    for p in range(4):
                        for c in range(3):
                            last = pe.matmul(out, wh[:, p, c, :], xh[:, c, b0:b0 + nb, p:p + 11:2, :],
                                             start=False, stop=(p == 3 and c == 2))
                    last.then_inc(out_ready, 1)
                    b0 += nb
                pe.wait_ge(tokT_ready, 3)
                for b in range(B):
                    tr = pe.transpose(ps[0:NT, b // 4, (b % 4) * D:(b % 4 + 1) * D], tokT[:, b * NT:(b + 1) * NT], ident[:])
                    if b % 4 == 3:
                        tr.then_inc(rows_ready, 1)

            @block.scalar
            def _(act):
                b0 = 0
                for k, nb in enumerate(IB):
                    act.wait_ge(out_ready, k + 1)
                    act.activation(tokT[:, b0 * NT:(b0 + nb) * NT], ps[:, k, 0:nb * NT], ACT.Identity,
                                   bias=bias[:]).then_inc(tokT_ready, 1)
                    b0 += nb
                act.wait_ge(var_ready, 1)
                act.activation(t["std"][:], t["var"][:], ACT.Sqrt, bias=eps[0:NT]).then_inc(std_ready, 1)

            @block.vector
            def _(dve):
                steps = Steps(dve, dve_step)
                for k in range(8):
                    dve.wait_ge(rows_ready, k + 1)
                    steps.done(dve.tensor_copy(tok[:, 4 * k:4 * k + 4, :],
                                               ps[0:NT, k, :].rearrange("p (b d) -> p b d", d=D)))
                ln_statistics(dve, steps, tok, NT, t, var_ready, std_ready, stats_done)
                wide = [NT, B, D]
                steps.done(dve.tensor_tensor(tok[:], tok[:], t["mean"][:].unsqueeze(2).broadcast_to(wide), ALU.subtract))
                steps.done(dve.tensor_tensor(tok[:], tok[:], t["rstd"][:].unsqueeze(2).broadcast_to(wide), ALU.mult))
                steps.done(dve.tensor_tensor(tok[:], tok[:], gain[:].unsqueeze(1).broadcast_to(wide), ALU.mult))
                steps.done(dve.tensor_tensor(h[0:NT, :, :], tok[:], shift[:].unsqueeze(1).broadcast_to(wide), ALU.add))


def norm_and_turn(nc, name, h, hT, ps, ident, eps):
    with Phase(nc, name) as ph:
        hn = ph.sb("hn", [N, B, D])
        t = mean_and_rstd(ph, "ln", N)
        var_ready, std_ready, stats_done, dve_step, rows_ready, turned, moved = (ph.sem(s) for s in (
            "var_ready", "std_ready", "stats_done", "dve_step", "rows_ready", "turned", "moved"))
        with ph.block() as block:
            @block.vector
            def _(dve):
                steps = Steps(dve, dve_step)
                ln_statistics(dve, steps, h, N, t, var_ready, std_ready, stats_done)
                for b in range(B):
                    dve.tensor_scalar(hn[:, b, :], h[:, b, :], t["mean"][:, b:b + 1], t["rstd"][:, b:b + 1],
                                      ALU.subtract, ALU.mult).then_inc(rows_ready, 1)

            @block.tensor
            def _(pe):
                for b in range(B):
                    pe.wait_ge(rows_ready, b + 1)
                    tr = pe.transpose(ps[:, b // 4, (b % 4) * N:(b % 4 + 1) * N], hn[:, b, :], ident[0:N, 0:N])
                    if b % 4 == 3:
                        tr.then_inc(turned, 1)

            @block.scalar
            def _(act):
                act.wait_ge(var_ready, 1)
                act.activation(t["std"][:], t["var"][:], ACT.Sqrt, bias=eps[0:N]).then_inc(std_ready, 1)
                for k in range(B // 4):
                    act.wait_ge(turned, k + 1)
                    act.activation(hT[:, 4 * k:4 * k + 4, :], ps[:, k, 0:4 * N].rearrange("p (b n) -> p b n", n=N),
                                   ACT.Copy).then_inc(moved, 1)
                act.wait_ge(moved, B // 4)



def signal(engine, instruction, sem, count):
    instruction.then_inc(sem, 1)
    engine.wait_ge(sem, count)


def logic_attention(nc, h, hT, ps, ident, dram):
    W = H * N
    G = 8
    GROUPS = -(-N // G)
    MP = GROUPS * G
    MAPS, UNITS_H = 6, 16
    ROWS = 2 * MAPS * G
    EVACS = -(-GROUPS // 2)
    HT = 4

    with Phase(nc, "la") as ph:
        sb = ph.sb
        w_m, w_n = sb("w_m", [D, 2, 128]), sb("w_n", [D, 2, 128])
        w_v, w_out = sb("w_v", [D, 2 * D]), sb("w_out", [D, D])
        n_mask = sb("n_mask", [128, 2 * HT])
        key_hot, w1_rows = sb("key_hot", [ROWS, G]), sb("w1_rows", [ROWS, UNITS_H])
        g_hot, w2_rows, b1 = sb("g_hot", [128, G]), sb("w2_rows", [128, 4]), sb("b1", [128, 1])
        b2, w_chain = sb("b2", [N, 2, 4]), sb("w_chain", [N, 1])
        one, tiny, zero = (sb(n, [128, 1]) for n in ("one", "tiny", "zero"))
        w1_full = sb("w1_full", [ROWS, G, UNITS_H])
        w1 = sb("w1", [ROWS, 2, G * UNITS_H], F16)
        w2 = sb("w2", [128, G, 4])

        xT = sb("xT", [D, N])
        m_side = sb("m_side", [128, 2, N])
        n_side = sb("n_side", [128, 2, N])
        n_map = sb("n_map", [128, 2, HT, 2, N])
        V = sb("V", [N, 2, 2 * D])
        S = [sb(f"S{i}", [N, 2, W]) for i in (1, 2)]
        P = [sb(f"P{i}", [N, W]) for i in (1, 2)]
        PT = [sb(f"PT{i}", [N, W]) for i in (1, 2)]
        top, total, inv = sb("top", [N, 3 * H]), sb("total", [N, 3 * H]), sb("inv", [N, 3 * H])
        logT = [sb(f"logT{i}", [N, W]) for i in range(2)]
        Cr, soft = sb("Cr", [N, 2, W]), sb("soft", [N, 2, W])
        absd = sb("absd", [N, W])
        maps = sb("maps", [MP, MAPS, 2, W], F16)
        pairs_in = sb("pairs_in", [ROWS, GROUPS, W], F16)
        hid = sb("hid", [128, 2, H, N])
        gate = sb("gate", [N, H, MP, 4])
        mixA, mixB, mixC = sb("mixA", [N, W]), sb("mixB", [N, W]), sb("mixC", [N, W])
        ET, transport, chain = mixC, sb("transport", [N, D]), sb("chain", [N, 2, D])
        y, yT = sb("y", [N, D]), sb("yT", [D, N])

        names = ("consts_in setup act_setup dve_setup xT_ready mn_made m_ready n_ready n_map_ready S1_made S2_made "
                 "S1_ready S2_ready v_made V_ready top_step shifted diff_ready raised norm_step P_ready ST_made "
                 "ST_high PT_made PT1_ready PT2_ready CrT_made ClT_made Cr_made logT_ready Cr_ready log_step abs_step "
                 "abs_ready soft_ready pool_step transport_made transport_ready chain_made chain_ready pairs_in "
                 "hid_made hid_ready gate_made gate_in gate_ready mix_step mix_shifted mix_raised mixT_made ET_ready "
                 "inv_step base_made y_step y_ready yT_made yT_ready out_made added").split()
        s = {n: ph.sem(n) for n in names}
        map_ready = [ph.sem(f"map{c}_ready") for c in range(MAPS)]
        loads = [(w_m, "la_w_m"), (w_n, "la_w_n"), (w_v, "la_w_v"), (w_out, "la_w_out"), (n_mask, "la_n_mask"),
                 (key_hot, "la_key_hot"), (w1_rows, "la_w1_rows"), (g_hot, "la_g_hot"), (w2_rows, "la_w2_rows"),
                 (b1, "la_b1")]
        ALL_IN = 16 * (len(loads) + 2)

        def col(i):
            return slice(i * N, (i + 1) * N)

        def banks(bank, parts=N):
            return ps[0:parts, bank:bank + 2, 0:HB * N]

        def at(bank, hd):
            return ps[0:N, bank + hd // HB, col(hd % HB)]

        def two(tile):
            return tile.rearrange("p (k c) -> p k c", k=2)

        def by_head(tile):
            return tile.rearrange("p (h n) -> p h n", h=H)

        def per_head(stat, width=N):
            return stat.unsqueeze(2).broadcast_to([N, H, width])

        def since(b, n):
            return not isinstance(b, int) or b >= n

        def pipeline(engine, scores, products, pairs, output):
            scores(0, 0)
            products(0, 0)
            pairs(0, 0, True)
            with engine.Fori(1, B - 2, 2) as b:
                for i, k in ((0, 1), (1, 0)):
                    products(b + i, k)
                    output(b + i - 1, 1 - k)
                    pairs(b + i, k, True)
            products(B - 1, 1)
            output(B - 2, 0)
            pairs(B - 1, 1, False)
            output(B - 1, 1)

        def gates_of(j, n):
            return ps[0:N, 4 + j % 2, 0:H * G * n * 4].rearrange("p (h m g c) -> p h m g c", h=H, m=G, g=n)

        with ph.block() as block:
            @block.sync
            def _(sp):
                for tile, name in loads:
                    sp.dma_start(tile[:], dram[name]).then_inc(s["consts_in"], 16)
                sp.dma_start(b2[:], dram["la_b2"].partition_broadcast(N)).then_inc(s["consts_in"], 16)
                sp.dma_start(w_chain[:], dram["la_chain"].partition_broadcast(N)).then_inc(s["consts_in"], 16)

                def products(b, k):
                    if since(b, 1):
                        sp.wait_ge(s["hid_made"], GROUPS * b)
                    for c in (2, 3, 0, 1, 4, 5):
                        sp.wait_ge(map_ready[c], b + 1)
                        for part in range(2):
                            row = (part * MAPS + c) * G
                            sp.dma_start(pairs_in[row:row + G, :, :], maps[:, c, part, :]).then_inc(s["pairs_in"], 16)

                for b in range(B):
                    products(b, b % 2)

            @block.gpsimd
            def _(pool):
                pool.memset(zero[:], 0.0).then_inc(s["setup"], 1)
                pool.memset(maps[:], 0.0).then_inc(s["setup"], 1)
                pool.wait_ge(s["setup"], 2)
                pool.wait_ge(s["consts_in"], ALL_IN)

                def copy(out, x):
                    rows, cols = x.shape
                    return pool.tensor_tensor(out, x, zero[0:rows].broadcast_to([rows, cols]), ALU.add)

                def split(b, k):
                    for i in range(2):
                        pool.wait_ge(s[f"S{i + 1}_ready"], b + 1)
                        signal(pool, copy(maps[0:N, 2 + i, 0, :], S[i][:, k, :]), s["pool_step"], 2 * b + i + 1)
                        pool.tensor_tensor(maps[0:N, 2 + i, 1, :], S[i][:, k, :], maps[0:N, 2 + i, 0, :],
                                           ALU.subtract).then_inc(map_ready[2 + i], 1)

                def scores(b, k):
                    if since(b, 1):
                        pool.wait_ge(s["v_made"], b)
                    copy(xT[:], hT[:, b, :]).then_inc(s["xT_ready"], 1)
                    pool.wait_ge(s["n_ready"], b + 1)
                    wide = [128, 2 * HT, 2 * N]
                    pool.tensor_tensor(n_map[:].rearrange("p i q t n -> p (i q) (t n)"),
                                       n_side[:].rearrange("p t n -> p (t n)").unsqueeze(1).broadcast_to(wide),
                                       n_mask[:].unsqueeze(2).broadcast_to(wide), ALU.mult).then_inc(s["n_map_ready"], 1)
                    if since(b, 1):
                        pool.wait_ge(s["pairs_in"], 2 * MAPS * 16 * b)
                    split(b, k)

                scores(0, 0)
                with pool.Fori(1, B - 2, 2) as b:
                    scores(b, 1)
                    scores(b + 1, 0)
                scores(B - 1, 1)

            @block.tensor
            def _(pe):
                def project(b):
                    if since(b, 2):
                        pe.wait_ge(s["added"], b - 1)
                    if since(b, 1):
                        pe.wait_ge(s["chain_ready"], b)
                    for bank, w in ((6, w_m), (7, w_n)):
                        for t in range(2):
                            mm = pe.matmul(ps[:, bank, col(t)], w[:, t, :], hT[:, b, :], start=True, stop=True)
                    mm.then_inc(s["mn_made"], 1)

                def score(b, i):
                    if i == 0:
                        pe.wait_ge(s["m_ready"], b + 1)
                        pe.wait_ge(s["n_map_ready"], b + 1)
                    else:
                        pe.wait_ge(s["S1_ready"], b + 1)
                    for hd in range(H):
                        mm = pe.matmul(at(6, hd), n_map[:, i, hd % HT, hd // HT, :], m_side[:, hd // HT, :], start=True, stop=True)
                    mm.then_inc(s[f"S{i + 1}_made"], 1)

                def values(b):
                    pe.wait_ge(s["S2_ready"], b + 1)
                    pe.wait_ge(s["xT_ready"], b + 1)
                    pe.matmul(ps[0:N, 6, 0:2 * D], xT[:], w_v[:], start=True, stop=True).then_inc(s["v_made"], 1)

                def scores(b, k):
                    project(b)
                    score(b, 0)
                    score(b, 1)
                    values(b)

                def products(b, k):
                    if since(b, 1):
                        pe.wait_ge(s["hid_ready"], GROUPS * b)
                    for i in range(2):
                        pe.wait_ge(s[f"S{i + 1}_ready"], b + 1)
                        for hd in range(H):
                            tr = pe.transpose(at(2 * i, hd), S[i][:, k, col(hd)], ident[0:N, 0:N])
                        tr.then_inc(s["ST_made"], 1)
                    pe.wait_ge(s["V_ready"], b + 1)
                    if since(b, 1):
                        pe.wait_ge(s["gate_in"], EVACS * b)
                    for i in range(2):
                        pe.wait_ge(s["P_ready"], 2 * b + i + 1)
                        for hd in range(H):
                            tr = pe.transpose(at(4 + 2 * i, hd), P[i][:, col(hd)], ident[0:N, 0:N])
                        tr.then_inc(s["PT_made"], 1)
                    pe.wait_ge(s["PT1_ready"], b + 1)
                    pe.wait_ge(map_ready[0], b + 1)
                    for hd in range(H):
                        mm = pe.matmul(at(0, hd), P[1][:, col(hd)], PT[0][:, col(hd)], start=True, stop=True)
                    mm.then_inc(s["CrT_made"], 1)
                    pe.wait_ge(s["PT2_ready"], b + 1)
                    pe.wait_ge(map_ready[1], b + 1)
                    for hd in range(H):
                        mm = pe.matmul(at(2, hd), P[0][:, col(hd)], PT[1][:, col(hd)], start=True, stop=True)
                    mm.then_inc(s["ClT_made"], 1)
                    for hd in range(H):
                        mm = pe.matmul(at(4, hd), PT[0][:, col(hd)], P[1][:, col(hd)], start=True, stop=True)
                    mm.then_inc(s["Cr_made"], 1)
                    for hd in range(H):
                        mm = pe.matmul(ps[0:N, 6, hd * DK:(hd + 1) * DK], PT[1][:, col(hd)],
                                       V[:, k, D + hd * DK:D + (hd + 1) * DK], start=True, stop=True)
                    mm.then_inc(s["transport_made"], 1)
                    pe.wait_ge(s["transport_ready"], b + 1)
                    for hd in range(H):
                        mm = pe.matmul(ps[0:N, 7, hd * DK:(hd + 1) * DK], PT[0][:, col(hd)],
                                       transport[:, hd * DK:(hd + 1) * DK], start=True, stop=True)
                    mm.then_inc(s["chain_made"], 1)

                def output(b, k):
                    pe.wait_ge(s["mix_raised"], b + 1)
                    if isinstance(b, int) and b == B - 1:
                        pe.wait_ge(s["hid_ready"], GROUPS * B)
                    else:
                        pe.wait_ge(s["logT_ready"], 2 * b + 3)
                    for hd in range(H):
                        tr = pe.transpose(at(0, hd), mixB[:, col(hd)], ident[0:N, 0:N])
                    tr.then_inc(s["mixT_made"], 1)
                    pe.wait_ge(s["ET_ready"], b + 1)
                    if not (isinstance(b, int) and b == B - 1):
                        pe.wait_ge(s["chain_ready"], b + 2)
                    for hd in range(H):
                        mm = pe.matmul(ps[0:N, 7, 128 + hd * DK:128 + (hd + 1) * DK], ET[:, col(hd)],
                                       V[:, k, hd * DK:(hd + 1) * DK], start=True, stop=True)
                    mm.then_inc(s["base_made"], 1)
                    pe.wait_ge(s["y_ready"], b + 1)
                    pe.transpose(ps[0:D, 6, 128:128 + N], y[:], ident[0:N, 0:N]).then_inc(s["yT_made"], 1)
                    pe.wait_ge(s["yT_ready"], b + 1)
                    pe.matmul(ps[0:N, 7, 256:256 + D], yT[:], w_out[:], start=True, stop=True).then_inc(s["out_made"], 1)

                def pairs(b, k, more):
                    pe.wait_ge(s["pairs_in"], 2 * MAPS * 16 * (b + 1))
                    pe.wait_ge(s["logT_ready"], 2 * b + 2)
                    pe.wait_ge(s["Cr_ready"], b + 1)
                    if since(b, 1):
                        pe.wait_ge(s["ET_ready"], b)

                    def second(g):
                        pe.wait_ge(s["hid_ready"], GROUPS * b + g + 1)
                        j = g // 2
                        n = min(2, GROUPS - 2 * j)
                        if g % 2 == 0 and j >= 2:
                            pe.wait_ge(s["gate_in"], EVACS * b + j - 1)
                        for hd in range(H):
                            mm = pe.matmul(gates_of(j, n)[:, hd, :, g % 2, :], hid[:, g % 2, hd, :], w2[:], start=True, stop=True)
                        mm.then_inc(s["gate_made"], 1)

                    for g in range(GROUPS):
                        if g >= 2:
                            pe.wait_ge(s["hid_ready"], GROUPS * b + g - 1)
                        for half in range(2):
                            for part in range(2):
                                mm = pe.matmul(ps[:, g % 2 * 2 + half, 0:HB * N], w1[:, part, :],
                                               pairs_in[:, g, half * HB * N:(half + 1) * HB * N],
                                               start=(part == 0), stop=(part == 1))
                        mm.then_inc(s["hid_made"], 1)
                        if g:
                            second(g - 1)
                        if more:
                            if g == 1:
                                project(b + 1)
                            if g == 4:
                                score(b + 1, 0)
                            if g == 8:
                                score(b + 1, 1)
                            if g == 12:
                                values(b + 1)
                    second(GROUPS - 1)

                pe.wait_ge(s["consts_in"], ALL_IN)
                pe.wait_ge(s["dve_setup"], 8)
                pipeline(pe, scores, products, pairs, output)

            @block.scalar
            def _(act):
                def keys_side(b):
                    act.wait_ge(s["mn_made"], b + 1)
                    act.activation(m_side[:], ps[:, 6, 0:2 * N].rearrange("p (k n) -> p k n", k=2), ACT.Copy).then_inc(s["m_ready"], 1)

                def score(b, k, i):
                    act.wait_ge(s[f"S{i + 1}_made"], b + 1)
                    act.activation(two(S[i][:, k]), banks(6), ACT.Copy).then_inc(s[f"S{i + 1}_ready"], 1)

                def values(b, k):
                    act.wait_ge(s["v_made"], b + 1)
                    act.activation(V[:, k], ps[0:N, 6, 0:2 * D], ACT.Copy).then_inc(s["V_ready"], 1)

                def scores(b, k):
                    keys_side(b)
                    score(b, k, 0)
                    score(b, k, 1)
                    values(b, k)

                def products(b, k):
                    for i in range(2):
                        act.wait_ge(s["shifted"], 2 * b + i + 1)
                        act.activation(P[i][:], P[i][:], ACT.Exp).then_inc(s["raised"], 1)
                    if since(b, 1):
                        act.wait_ge(s["pairs_in"], 2 * MAPS * 16 * b)
                    for i in range(2):
                        act.wait_ge(s["ST_made"], 2 * b + i + 1)
                        act.activation(two(maps[0:N, i, 0, :]), banks(2 * i), ACT.Copy).then_inc(s["ST_high"], 1)
                    act.wait_ge(s["PT_made"], 2 * b + 1)
                    act.activation(two(PT[0][:]), banks(4), ACT.Copy).then_inc(s["PT1_ready"], 1)
                    act.wait_ge(s["diff_ready"], b + 1)
                    signal(act, act.activation(absd[:], soft[:, k], ACT.Abs), s["abs_step"], 2 * b + 1)
                    signal(act, act.activation(absd[:], absd[:], ACT.Exp, scale=-1.0), s["abs_step"], 2 * b + 2)
                    act.activation(absd[:], absd[:], ACT.Ln, bias=one[0:N]).then_inc(s["abs_ready"], 1)
                    for i, made in enumerate(("CrT_made", "ClT_made")):
                        act.wait_ge(s[made], b + 1)
                        act.activation(two(logT[i][:]), banks(2 * i), ACT.Ln, bias=tiny[0:N]).then_inc(s["logT_ready"], 1)
                    act.wait_ge(s["Cr_made"], b + 1)
                    act.activation(two(Cr[:, k]), banks(4), ACT.Ln, bias=tiny[0:N]).then_inc(s["Cr_ready"], 1)

                def output(b, k):
                    act.wait_ge(s["mix_shifted"], b + 1)
                    act.activation(mixB[:], mixA[:], ACT.Exp).then_inc(s["mix_raised"], 1)
                    act.wait_ge(s["mixT_made"], b + 1)
                    act.activation(two(ET[:]), banks(0), ACT.Copy).then_inc(s["ET_ready"], 1)
                    act.wait_ge(s["yT_made"], b + 1)
                    act.activation(yT[:], ps[0:D, 6, 128:128 + N], ACT.Copy).then_inc(s["yT_ready"], 1)

                def pairs(b, k, more):
                    for g in range(GROUPS):
                        act.wait_ge(s["hid_made"], GROUPS * b + g + 1)
                        if g >= 2:
                            act.wait_ge(s["gate_made"], GROUPS * b + g - 1)
                        act.activation(hid[:, g % 2].rearrange("p (k h) n -> p k (h n)", k=2), banks(g % 2 * 2, 128),
                                       ACT.Gelu_apprx_tanh, bias=b1[:]).then_inc(s["hid_ready"], 1)
                        if more:
                            if g == 2:
                                keys_side(b + 1)
                            if g == 5:
                                score(b + 1, 1 - k, 0)
                            if g == 9:
                                score(b + 1, 1 - k, 1)
                            if g == 13:
                                values(b + 1, 1 - k)
                    act.wait_ge(s["gate_in"], EVACS * (b + 1))
                    act.activation(gate[:], gate[:], ACT.Tanh, scale=0.5).then_inc(s["gate_ready"], 1)

                act.wait_ge(s["consts_in"], ALL_IN)
                signal(act, act.activation(w_chain[:], w_chain[:], ACT.Tanh, scale=0.5), s["act_setup"], 1)
                act.wait_ge(s["dve_setup"], 8)
                pipeline(act, scores, products, pairs, output)

            @block.vector
            def _(dve):
                def queries_side(b):
                    dve.wait_ge(s["mn_made"], b + 1)
                    if since(b, 1):
                        dve.wait_ge(s["n_map_ready"], b)
                    dve.tensor_copy(n_side[:], ps[:, 7, 0:2 * N].rearrange("p (k n) -> p k n", k=2)).then_inc(s["n_ready"], 1)

                def largest(x, i):
                    return dve.tensor_reduce(top[:, H * i:H * i + H], by_head(x), AX_X, ALU.max)

                def shift(x, out, i):
                    return dve.tensor_tensor(by_head(out), by_head(x), per_head(top[:, H * i:H * i + H]), ALU.subtract)

                def score(b, k, i):
                    dve.wait_ge(s[f"S{i + 1}_ready"], b + 1)
                    signal(dve, largest(S[i][:, k], i), s["top_step"], 2 * b + i + 1)
                    shift(S[i][:, k], P[i][:], i).then_inc(s["shifted"], 1)
                    if i == 1:
                        dve.tensor_tensor(soft[:, k], S[1][:, k], S[0][:, k], ALU.subtract).then_inc(s["diff_ready"], 1)

                def scores(b, k):
                    queries_side(b)
                    score(b, k, 0)
                    score(b, k, 1)

                def products(b, k):
                    for i in range(2):
                        dve.wait_ge(s["raised"], 2 * b + i + 1)
                        stat = slice(H * i, H * i + H)
                        signal(dve, dve.tensor_reduce(total[:, stat], by_head(P[i][:]), AX_X, ALU.add), s["norm_step"], 4 * b + 2 * i + 1)
                        signal(dve, dve.reciprocal(inv[:, stat], total[:, stat]), s["norm_step"], 4 * b + 2 * i + 2)
                        dve.tensor_tensor(by_head(P[i][:]), by_head(P[i][:]), per_head(inv[:, stat]), ALU.mult).then_inc(s["P_ready"], 1)
                    for i in range(2):
                        dve.wait_ge(s["ST_high"], 2 * b + i + 1)
                        dve.tensor_tensor(two(maps[0:N, i, 1, :]), banks(2 * i), two(maps[0:N, i, 0, :]),
                                          ALU.subtract).then_inc(map_ready[i], 1)
                    dve.wait_ge(s["PT_made"], 2 * b + 2)
                    dve.tensor_copy(two(PT[1][:]), banks(6)).then_inc(s["PT2_ready"], 1)
                    if since(b, 1):
                        mix_gates(b - 1, 1 - k)
                    dve.wait_ge(s["abs_ready"], b + 1)
                    dve.wait_ge(s["diff_ready"], b + 1)
                    dve.scalar_tensor_tensor(soft[:, k], soft[:, k], 0.0, absd[:], ALU.max, ALU.add).then_inc(s["soft_ready"], 1)
                    for i in range(2):
                        dve.wait_ge(s["logT_ready"], 2 * b + i + 1)
                        signal(dve, dve.tensor_copy(maps[0:N, 4 + i, 0, :], logT[i][:]), s["log_step"], 2 * b + i + 1)
                        dve.tensor_tensor(maps[0:N, 4 + i, 1, :], logT[i][:], maps[0:N, 4 + i, 0, :], ALU.subtract)\
                           .then_inc(map_ready[4 + i], 1)
                    dve.wait_ge(s["transport_made"], b + 1)
                    dve.tensor_copy(transport[:], ps[0:N, 6, 0:D]).then_inc(s["transport_ready"], 1)
                    dve.wait_ge(s["chain_made"], b + 1)
                    dve.tensor_scalar(chain[:, k], ps[0:N, 7, 0:D], w_chain[:], None, ALU.mult).then_inc(s["chain_ready"], 1)

                def mix_gates(b, k):
                    def step(i, instruction):
                        signal(dve, instruction, s["mix_step"], 7 * b + i)

                    t_and, t_or, t_not, t_chain = (gate[:, :, 0:N, c] for c in range(4))
                    A, Bm, C = (by_head(x[:]) for x in (mixA, mixB, mixC))
                    dve.wait_ge(s["gate_ready"], b + 1)
                    step(1, dve.scalar_tensor_tensor(A, t_not, -0.5, t_and, ALU.mult, ALU.add))
                    step(2, dve.scalar_tensor_tensor(A, A, 0.5, by_head(S[1][:, k]), ALU.add, ALU.mult))
                    dve.wait_ge(s["soft_ready"], b + 1)
                    step(3, dve.scalar_tensor_tensor(Bm, t_or, 1.0, by_head(soft[:, k]), ALU.add, ALU.mult))
                    dve.wait_ge(s["Cr_ready"], b + 1)
                    step(4, dve.scalar_tensor_tensor(C, t_chain, 1.0, by_head(Cr[:, k]), ALU.add, ALU.mult))

                def output(b, k):
                    def step(i, instruction):
                        signal(dve, instruction, s["mix_step"], 7 * b + i)

                    if isinstance(b, int) and b == B - 1:
                        mix_gates(b, k)
                    step(5, dve.tensor_tensor(mixA[:], mixA[:], mixB[:], ALU.add))
                    step(6, dve.tensor_tensor(mixA[:], mixA[:], mixC[:], ALU.add))
                    step(7, dve.scalar_tensor_tensor(mixA[:], mixA[:], 0.5, S[0][:, k], ALU.mult, ALU.add))
                    stat = slice(2 * H, 3 * H)
                    signal(dve, largest(mixA[:], 2), s["inv_step"], 3 * b + 1)
                    shift(mixA[:], mixA[:], 2).then_inc(s["mix_shifted"], 1)
                    dve.wait_ge(s["mix_raised"], b + 1)
                    signal(dve, dve.tensor_reduce(total[:, stat], by_head(mixB[:]), AX_X, ALU.add), s["inv_step"], 3 * b + 2)
                    signal(dve, dve.reciprocal(inv[:, stat], total[:, stat]), s["inv_step"], 3 * b + 3)
                    dve.wait_ge(s["base_made"], b + 1)
                    signal(dve, dve.tensor_tensor(y[:].rearrange("p (h d) -> p h d", h=H),
                                                  ps[0:N, 7, 128:128 + D].rearrange("p (h d) -> p h d", h=H),
                                                  per_head(inv[:, stat], DK), ALU.mult), s["y_step"], b + 1)
                    dve.tensor_tensor(y[:], y[:], chain[:, k], ALU.add).then_inc(s["y_ready"], 1)
                    dve.wait_ge(s["out_made"], b + 1)
                    dve.tensor_tensor(h[:, b, :], ps[0:N, 7, 256:256 + D], h[:, b, :], ALU.add).then_inc(s["added"], 1)

                def pairs(b, k, more):
                    for j in range(EVACS):
                        n = min(2, GROUPS - 2 * j)
                        dve.wait_ge(s["gate_made"], GROUPS * b + 2 * j + n)
                        wide = [N, H, G, 4 * n]
                        dve.tensor_tensor(gate[:].rearrange("p h (m g) c -> p h m (g c)", m=G)[:, :, :, 8 * j:8 * j + 4 * n],
                                          gates_of(j, n).rearrange("p h m g c -> p h m (g c)"),
                                          b2[:, 0:n].rearrange("p g c -> p (g c)").unsqueeze(1).unsqueeze(1).broadcast_to(wide),
                                          ALU.add).then_inc(s["gate_in"], 1)
                        if more:
                            if j == 0:
                                queries_side(b + 1)
                            if j == 2:
                                score(b + 1, 1 - k, 0)
                            if j == 4:
                                score(b + 1, 1 - k, 1)

                def setup(i, instruction):
                    signal(dve, instruction, s["dve_setup"], i)

                setup(1, dve.memset(one[:], 1.0))
                setup(2, dve.memset(tiny[:], 1e-6))
                dve.wait_ge(s["setup"], 2)
                dve.wait_ge(s["consts_in"], ALL_IN)
                wide = [ROWS, G, UNITS_H]
                setup(3, dve.tensor_tensor(w1_full[:], key_hot[:].unsqueeze(2).broadcast_to(wide),
                                           w1_rows[:].unsqueeze(1).broadcast_to(wide), ALU.mult))
                flat = w1_full[:].rearrange("p g o -> p (g o)")
                setup(4, dve.tensor_copy(w1[:, 0, :], flat))
                setup(5, dve.tensor_tensor(w1[:, 1, :], flat, w1[:, 0, :], ALU.subtract))
                wide = [128, G, 4]
                setup(6, dve.tensor_tensor(w2[:], g_hot[:].unsqueeze(2).broadcast_to(wide),
                                           w2_rows[:].unsqueeze(1).broadcast_to(wide), ALU.mult))
                dve.wait_ge(s["act_setup"], 1)
                setup(7, dve.tensor_scalar(w_chain[:], w_chain[:], 0.5, 0.5, ALU.mult, ALU.add))
                setup(8, dve.memset(top[:], 0.0))
                pipeline(dve, scores, products, pairs, output)


def expert_choice(nc, h, hT, ps, ident, dram):
    E, F, TOP = 8, 256, 2 * N // 8
    HALF = B // 2
    Q = 4
    with Phase(nc, "ec") as ph:
        sb = ph.sb
        w_gate = sb("w_gate", [D, E])
        w1, b1 = sb("w1", [D, E, F]), sb("b1", [128, E, 2])
        w2 = sb("w2", [128, E, 2, D])
        b2 = sb("b2", [128, HALF, D])
        gate = sb("gate", [N, B, E])
        peak, total, inv = sb("peak", [N, B]), sb("total", [N, B]), sb("inv", [N, B])
        rows = sb("rows", [128, 2, N])
        left, best = sb("left", [128, 2, N]), sb("best", [128, 2, 4, 8])
        above, equal, rank = sb("above", [128, 2, N]), sb("equal", [128, 2, N]), sb("rank", [128, 2, N])
        room, ones = sb("room", [128, 2]), sb("ones", [128, N])
        hid = sb("hid", [128, 2, 2, Q * N])
        names = ("consts_in scores_made shifted raised gate_ready rows_made rows_ready chosen turned_back "
                 "bias_made hid_made hid_ready out_made added dve_step").split()
        s = {n: ph.sem(n) for n in names}
        wide = [N, B, E]

        with ph.block() as block:
            @block.sync
            def _(sp):
                for tile, name in ((w_gate, "ec_w_gate"), (w1, "ec_w1"), (b1, "ec_b1"), (w2, "ec_w2"), (b2, "ec_b2")):
                    sp.dma_start(tile[:], dram[name]).then_inc(s["consts_in"], 16)

            @block.tensor
            def _(pe):
                pe.wait_ge(s["consts_in"], 80)
                for b in range(B):
                    mm = pe.matmul(ps[0:N, 0, b * E:(b + 1) * E], hT[:, b, :], w_gate[:], start=True, stop=True)
                mm.then_inc(s["scores_made"], 1)
                pe.wait_ge(s["gate_ready"], 1)
                for k in range(2):
                    tr = pe.transpose(ps[:, 1, k * N:(k + 1) * N], gate[:, k * HALF:(k + 1) * HALF, :].rearrange("p b e -> p (b e)"),
                                      ident[0:N, 0:N])
                tr.then_inc(s["rows_made"], 1)
                pe.wait_ge(s["chosen"], 1)
                for k in range(2):
                    tr = pe.transpose(ps[0:N, 0, k * 128:(k + 1) * 128], rows[:, k, :], ident[:])
                tr.then_inc(s["turned_back"], 1)
                for j in range(8):
                    lo = j % 4 * Q
                    if j >= 4:
                        pe.wait_ge(s["added"], j - 3)
                    pe.matmul(ps[0:N, 1 + j % 4, :], rows[:, j // 4, :], b2[:, lo:lo + Q, :].rearrange("p b d -> p (b d)"),
                              start=True, stop=True).then_inc(s["bias_made"], 1)
                pe.wait_ge(s["added"], 8)
                with pe.Fori(0, B // Q) as g:
                    def second(e):
                        pe.wait_ge(s["hid_ready"], 2 * E * g + 2 * e + 2)
                        pe.wait_ge(s["added"], 8 + E * g + e - 1)
                        for i in range(Q):
                            for c in range(2):
                                mm = pe.matmul(ps[0:N, 6 + e % 2, i * D:(i + 1) * D], hid[:, e % 2, c, i * N:(i + 1) * N],
                                               w2[:, e, c, :], start=(c == 0), stop=(c == 1))
                        mm.then_inc(s["out_made"], 1)

                    for e in range(E):
                        for c in range(2):
                            if e >= 2:
                                pe.wait_ge(s["hid_ready"], 2 * E * g + 2 * e + c - 3)
                            pe.matmul(ps[:, 2 + (2 * e + c) % 4, 0:Q * N], w1[:, e, c * 128:(c + 1) * 128],
                                      hT[:, bass.ds(g * Q, Q), :].rearrange("p b n -> p (b n)"),
                                      start=True, stop=True).then_inc(s["hid_made"], 1)
                        if e:
                            second(e - 1)
                    second(E - 1)

            @block.scalar
            def _(act):
                act.wait_ge(s["shifted"], 1)
                act.activation(gate[:], gate[:], ACT.Exp).then_inc(s["raised"], 1)
                with act.Fori(0, B // Q) as g:
                    for e in range(E):
                        for c in range(2):
                            act.wait_ge(s["hid_made"], 2 * E * g + 2 * e + c + 1)
                            if e >= 2:
                                act.wait_ge(s["out_made"], E * g + e - 1)
                            act.activation(hid[:, e % 2, c, :], ps[:, 2 + (2 * e + c) % 4, 0:Q * N], ACT.Gelu,
                                           bias=b1[:, e, c:c + 1]).then_inc(s["hid_ready"], 1)

            @block.vector
            def _(dve):
                steps = Steps(dve, s["dve_step"])
                steps.done(dve.memset(ones[:], 1.0))
                dve.wait_ge(s["scores_made"], 1)
                scores = ps[0:N, 0, 0:B * E].rearrange("p (b e) -> p b e", e=E)
                steps.done(dve.tensor_reduce(peak[:], scores, AX_X, ALU.max))
                dve.tensor_tensor(gate[:], scores, peak[:].unsqueeze(2).broadcast_to(wide), ALU.subtract).then_inc(s["shifted"], 1)
                dve.wait_ge(s["raised"], 1)
                steps.done(dve.tensor_reduce(total[:], gate[:], AX_X, ALU.add))
                steps.done(dve.reciprocal(inv[:], total[:]))
                dve.tensor_tensor(gate[:], gate[:], inv[:].unsqueeze(2).broadcast_to(wide), ALU.mult).then_inc(s["gate_ready"], 1)
                dve.wait_ge(s["rows_made"], 1)
                steps.done(dve.tensor_copy(rows[:], ps[:, 1, 0:2 * N].rearrange("p (k n) -> p k n", k=2)))
                steps.done(dve.tensor_copy(left[:], rows[:]))
                for k in range(2):
                    for r in range(TOP // 8):
                        steps.done(dve.max(best[:, k, r, :], left[:, k, :]))
                        steps.done(dve.match_replace(left[:, k, :], best[:, k, r, :], left[:, k, :], -1.0))
                    steps.done(dve.max(best[:, k, TOP // 8, :], left[:, k, :]))
                    last = best[:, k, TOP // 8, TOP % 8 - 1:TOP % 8]
                    steps.done(dve.tensor_scalar(above[:, k, :], rows[:, k, :], last, None, ALU.is_gt))
                    steps.done(dve.tensor_scalar(equal[:, k, :], rows[:, k, :], last, None, ALU.is_equal))
                    steps.done(dve.tensor_reduce(room[:, k:k + 1], above[:, k, :], AX_X, ALU.add))
                    steps.done(dve.tensor_scalar(room[:, k:k + 1], room[:, k:k + 1], -1.0, float(TOP), ALU.mult, ALU.add))
                    steps.done(dve.tensor_tensor_scan(rank[:, k, :], ones[:], equal[:, k, :], 0.0, ALU.mult, ALU.add))
                    steps.done(dve.scalar_tensor_tensor(equal[:, k, :], rank[:, k, :], room[:, k:k + 1], equal[:, k, :],
                                                        ALU.is_le, ALU.mult))
                    steps.done(dve.tensor_tensor(above[:, k, :], above[:, k, :], equal[:, k, :], ALU.add))
                dve.tensor_tensor(rows[:], rows[:], above[:], ALU.mult).then_inc(s["chosen"], 1)
                dve.wait_ge(s["turned_back"], 1)
                steps.done(dve.tensor_copy(gate[:], ps[0:N, 0, 0:B * E].rearrange("p (b e) -> p b e", e=E)))
                for j in range(8):
                    dve.wait_ge(s["bias_made"], j + 1)
                    part = h[:, Q * j:Q * j + Q, :]
                    signal(dve, dve.tensor_tensor(part, ps[0:N, 1 + j % 4, :].rearrange("p (b d) -> p b d", d=D), part,
                                                  ALU.add), s["added"], j + 1)
                with dve.Fori(0, B // Q) as g:
                    for e in range(E):
                        dve.wait_ge(s["out_made"], E * g + e + 1)
                        for i in range(Q):
                            row = h[:, g * Q + i, :]
                            one = dve.scalar_tensor_tensor(row, ps[0:N, 6 + e % 2, i * D:(i + 1) * D], gate[:, g * Q + i, e:e + 1],
                                                           row, ALU.mult, ALU.add)
                        signal(dve, one, s["added"], 8 + E * g + e + 1)


def relative_attention(nc, h, hT, ps, ident, dram):
    J = 2 * N - 1
    W = H * N
    SCALE = D ** -0.5
    r_dram = nc.dram_tensor("ra_shift_scores", (B, N, H * J), F32, kind="Internal").ap()
    e_dram = nc.dram_tensor("ra_shift_probs", (2, N, H * J), F32, kind="Internal").ap()

    def skewed(dram_ap, i):
        return bass.AP(dram_ap.tensor, i * (N * H * J) + N - 1, [[H * J - 1, N], [J, H], [1, N]])

    with Phase(nc, "ra") as outer:
        scores = outer.sb("scores", [N, B, W])
        V = outer.sb("V", [N, B, D])
        with Phase(nc, "rp") as ph:
            sb = ph.sb
            w_q, w_k, w_v = sb("w_q", [D, D]), sb("w_k", [D, D]), sb("w_v", [D, D])
            b_q, b_k, b_v = sb("b_q", [D, 1]), sb("b_k", [D, 1]), sb("b_v", [N, D])
            rel_k, head_mask = sb("rel_k", [D, J]), sb("head_mask", [D, H])
            b_out = sb("b_out", [N, D])
            xT, qT, kT = sb("xT", [D, N]), sb("qT", [D, N]), sb("kT", [D, N])
            q_head = sb("q_head", [D, H, N])
            shift = sb("shift", [N, 2, 4, 2 * J])
            names = ("consts_in xT_ready q_made k_made qT_ready kT_ready q_head_ready V_ready scores_made "
                     "scores_ready shift_made shift_dve shift_act shift_out0 shift_out1 bias_added").split()
            s = {n: ph.sem(n) for n in names}
            shift_out = (s["shift_out0"], s["shift_out1"])
            loads = [(w_q, "ra_w_q"), (w_k, "ra_w_k"), (w_v, "ra_w_v"), (b_q, "ra_b_q"), (b_k, "ra_b_k"),
                     (rel_k, "ra_rel_k"), (head_mask, "ra_head_mask")]
            rows = [(b_v, "ra_b_v"), (b_out, "ra_b_out")]
            ALL_IN = 16 * (len(loads) + len(rows))
            with ph.block() as block:
                @block.sync
                def _(sp):
                    for tile, name in loads:
                        sp.dma_start(tile[:], dram[name]).then_inc(s["consts_in"], 16)
                    for tile, name in rows:
                        sp.dma_start(tile[:], dram[name].partition_broadcast(N)).then_inc(s["consts_in"], 16)
                    for k in range(2):
                        sp.wait_ge(shift_out[k], 16 * (B // 2))

                @block.gpsimd
                def _(pool):
                    pool.wait_ge(s["consts_in"], ALL_IN)
                    pool.tensor_tensor(h[:], h[:], b_out[:].unsqueeze(1).broadcast_to([N, B, D]), ALU.add).then_inc(s["bias_added"], 1)
                    pool.tensor_copy(xT[:], hT[:, 0, :]).then_inc(s["xT_ready"], 1)
                    with pool.Fori(1, B) as b:
                        pool.wait_ge(s["q_made"], b)
                        pool.tensor_copy(xT[:], hT[:, b, :]).then_inc(s["xT_ready"], 1)

                @block.tensor
                def _(pe):
                    def image(b, first):
                        if not first:
                            pe.wait_ge(s["kT_ready"], b)
                            pe.wait_ge(s["V_ready"], b)
                        pe.matmul(ps[:, 7, 0:N], w_k[:], hT[:, b, :], start=True, stop=True).then_inc(s["k_made"], 1)
                        pe.matmul(ps[:, 0, 0:N], w_q[:], hT[:, b, :], start=True, stop=True)
                        pe.wait_ge(s["xT_ready"], b + 1)
                        pe.matmul(ps[0:N, 0, 128:128 + D], xT[:], w_v[:], start=True, stop=True).then_inc(s["q_made"], 1)
                        pe.wait_ge(s["kT_ready"], b + 1)
                        pe.wait_ge(s["q_head_ready"], b + 1)
                        if not first:
                            pe.wait_ge(s["scores_ready"], b)
                        for hd in range(H):
                            mm = pe.matmul(ps[0:N, 1 + hd // HB, hd % HB * N:(hd % HB + 1) * N], q_head[:, hd, :], kT[:],
                                           start=True, stop=True)
                        mm.then_inc(s["scores_made"], 1)
                        if not first:
                            pe.wait_ge(s["shift_dve"], b)
                            pe.wait_ge(s["shift_act"], b)
                        for hd in range(H):
                            mm = pe.matmul(ps[0:N, 3 + hd // 2, hd % 2 * J:(hd % 2 + 1) * J], q_head[:, hd, :], rel_k[:],
                                           start=True, stop=True)
                            if hd % 4 == 3:
                                mm.then_inc(s["shift_made"], 1)

                    pe.wait_ge(s["consts_in"], ALL_IN)
                    image(0, True)
                    with pe.Fori(1, B) as b:
                        image(b, False)

                @block.scalar
                def _(act):
                    def image(b, k, early):
                        act.wait_ge(s["k_made"], b + 1)
                        if not early or k:
                            act.wait_ge(s["shift_made"], 2 * b)
                        act.activation(kT[:], ps[:, 7, 0:N], ACT.Identity, bias=b_k[:]).then_inc(s["kT_ready"], 1)
                        act.wait_ge(s["scores_made"], b + 1)
                        act.activation(scores[:, b, :].rearrange("p (k c) -> p k c", k=2), ps[0:N, 1:3, 0:HB * N],
                                       ACT.Copy).then_inc(s["scores_ready"], 1)
                        act.wait_ge(s["shift_made"], 2 * b + 2)
                        if not early:
                            act.wait_ge(shift_out[k], 8 * b - 8 * k)
                        act.activation(shift[:, k, 2:4, :], ps[0:N, 5:7, 0:2 * J], ACT.Copy).then_inc(s["shift_act"], 1)
                        act.wait_ge(s["shift_dve"], b + 1)
                        act.wait_ge(s["shift_act"], b + 1)
                        act.dma_start(r_dram[b, :, :], shift[:, k].rearrange("p a c -> p (a c)")).then_inc(shift_out[k], 16)

                    act.wait_ge(s["consts_in"], ALL_IN)
                    image(0, 0, True)
                    image(1, 1, True)
                    with act.Fori(2, B - 1, 2) as b:
                        image(b, 0, False)
                        image(b + 1, 1, False)

                @block.vector
                def _(dve):
                    def image(b, k, early):
                        dve.wait_ge(s["q_made"], b + 1)
                        signal(dve, dve.tensor_scalar(qT[:], ps[:, 0, 0:N], b_q[:], SCALE, ALU.add, ALU.mult), s["qT_ready"], b + 1)
                        if not early or k:
                            dve.wait_ge(s["shift_made"], 2 * b)
                        dve.tensor_tensor(q_head[:], qT[:].unsqueeze(1).broadcast_to([D, H, N]),
                                          head_mask[:].unsqueeze(2).broadcast_to([D, H, N]), ALU.mult).then_inc(s["q_head_ready"], 1)
                        dve.tensor_tensor(V[:, b, :], ps[0:N, 0, 128:128 + D], b_v[:], ALU.add).then_inc(s["V_ready"], 1)
                        dve.wait_ge(s["shift_made"], 2 * b + 1)
                        if not early:
                            dve.wait_ge(shift_out[k], 8 * b - 8 * k)
                        dve.tensor_copy(shift[:, k, 0:2, :], ps[0:N, 3:5, 0:2 * J]).then_inc(s["shift_dve"], 1)

                    dve.wait_ge(s["consts_in"], ALL_IN)
                    image(0, 0, True)
                    image(1, 1, True)
                    with dve.Fori(2, B - 1, 2) as b:
                        image(b, 0, False)
                        image(b + 1, 1, False)

        with Phase(nc, "rv") as ph:
            sb = ph.sb
            w_out, rel_v = sb("w_out", [D, D]), sb("rel_v", [N, 2, DK])
            zero = hT[0:N].rearrange("p b n -> p (b n)")[:, 0:H * J]
            bent = sb("bent", [N, 2, W])
            z = sb("z", [N, W])
            E = sb("E", [N, 2, W])
            Ej = sb("Ej", [N, 2, H * J])
            top, total, inv = sb("top", [N, H]), sb("total", [N, H]), sb("inv", [N, 2, H])
            ET, EjT = sb("ET", [N, W]), sb("EjT", [N, 2, W])
            y, yT = sb("y", [N, D]), sb("yT", [D, N])
            names = ("consts_in zeroed bent_in0 bent_in1 summed shifted raised inv_ready E_out0 E_out1 Ej_in0 Ej_in1 "
                     "ET_made ET_ready EjT_made0 EjT_made1 EjT_ready0 EjT_ready1 y_made y_ready yT_made yT_ready out_made "
                     "added zero_set dve_step").split()
            s = {n: ph.sem(n) for n in names}
            bent_in, E_out, Ej_in = ([s[f"{n}{k}"] for k in range(2)] for n in ("bent_in", "E_out", "Ej_in"))

            def lagged(engine, front, back):
                front(0, 0, True)
                front(1, 1, True)
                back(0, 0, True)
                front(2, 0, False)
                back(1, 1, True)
                with engine.Fori(3, B - 4, 2) as b:
                    front(b, 1, False)
                    back(b - 1, 0, False)
                    front(b + 1, 0, False)
                    back(b, 1, False)
                for b in (B - 3, B - 2, B - 1):
                    front(b, b % 2, False)
                    back(b - 1, 1 - b % 2, False)
                back(B - 1, 1, False)

            def turn(b, k):
                return 8 * b - 8 * k + 16

            with ph.block() as block:
                @block.sync
                def _(sp):
                    sp.dma_start(w_out[:], dram["ra_w_out"]).then_inc(s["consts_in"], 16)
                    sp.dma_start(rel_v[:], dram["ra_rel_v"]).then_inc(s["consts_in"], 16)
                    sp.wait_ge(s["zero_set"], 1)
                    for k in range(2):
                        sp.dma_start(e_dram[k, :, :], zero).then_inc(s["zeroed"], 16)
                    sp.wait_ge(s["zeroed"], 32)

                    def store_and_reload(b, k, early):
                        sp.wait_ge(s["raised"], b + 1)
                        if not early:
                            sp.wait_ge(Ej_in[k], turn(b, k) - 16)
                        sp.dma_start(skewed(e_dram, k), E[:, k, :].rearrange("p (h n) -> p h n", h=H)).then_inc(E_out[k], 16)
                        sp.wait_ge(E_out[k], turn(b, k))
                        if not early:
                            sp.wait_ge(s["EjT_made1"], b - 1)
                        sp.dma_start(Ej[:, k, :], e_dram[k, :, :]).then_inc(Ej_in[k], 16)

                    for b in range(B):
                        store_and_reload(b, b % 2, b < 2)

                @block.tensor
                def _(pe):
                    pe.wait_ge(s["consts_in"], 32)

                    def image(b, k, first):
                        pe.wait_ge(s["raised"], b + 1)
                        for hd in range(H):
                            tr = pe.transpose(ps[0:N, hd // HB, hd % HB * N:(hd % HB + 1) * N], E[:, k, hd * N:(hd + 1) * N],
                                              ident[0:N, 0:N])
                        tr.then_inc(s["ET_made"], 1)
                        pe.wait_ge(Ej_in[k], turn(b, k))
                        for c, lo, hi in ((0, 0, N), (1, N, J)):
                            for hd in range(H):
                                tr = pe.transpose(ps[0:hi - lo, 3 + 2 * c + hd // HB, hd % HB * N:(hd % HB + 1) * N],
                                                  Ej[:, k, hd * J + lo:hd * J + hi], ident[0:N, 0:N])
                            tr.then_inc(s[f"EjT_made{c}"], 1)
                        pe.wait_ge(s["ET_ready"], b + 1)
                        pe.wait_ge(s["EjT_ready0"], b + 1)
                        pe.wait_ge(s["EjT_ready1"], b + 1)
                        for hd in range(H):
                            out = ps[0:N, 2, hd * DK:(hd + 1) * DK]
                            c = slice(hd * N, (hd + 1) * N)
                            pe.matmul(out, ET[:, c], V[:, b, hd * DK:(hd + 1) * DK], start=True, stop=False)
                            pe.matmul(out, EjT[:, 0, c], rel_v[:, 0, :], start=False, stop=False)
                            mm = pe.matmul(out, EjT[0:J - N, 1, c], rel_v[0:J - N, 1, :], start=False, stop=True)
                        mm.then_inc(s["y_made"], 1)
                        pe.wait_ge(s["y_ready"], b + 1)
                        pe.transpose(ps[0:D, 7, 0:N], y[:], ident[0:N, 0:N]).then_inc(s["yT_made"], 1)
                        pe.wait_ge(s["yT_ready"], b + 1)
                        pe.matmul(ps[0:N, 7, 128:128 + D], yT[:], w_out[:], start=True, stop=True).then_inc(s["out_made"], 1)

                    image(0, 0, True)
                    image(1, 1, False)
                    with pe.Fori(2, B - 1, 2) as b:
                        image(b, 0, False)
                        image(b + 1, 1, False)

                @block.scalar
                def _(act):
                    def load_bent(b, k):
                        act.dma_start(bent[:, k, :].rearrange("p (h n) -> p h n", h=H), skewed(r_dram, b)).then_inc(bent_in[k], 16)

                    def front(b, k, early):
                        act.wait_ge(s["shifted"], b + 1)
                        if not early:
                            act.wait_ge(s["ET_made"], b - 1)
                            act.wait_ge(E_out[k], turn(b, k) - 16)
                        act.activation(E[:, k, :], z[:], ACT.Exp).then_inc(s["raised"], 1)
                        if not isinstance(b, int) or b + 2 < B:
                            load_bent(b + 2, k)

                    def back(b, k, early):
                        act.wait_ge(s["ET_made"], b + 1)
                        act.activation(ET[:].rearrange("p (k c) -> p k c", k=2), ps[0:N, 0:2, 0:HB * N], ACT.Copy).then_inc(s["ET_ready"], 1)
                        act.wait_ge(s["EjT_made1"], b + 1)
                        act.activation(EjT[0:J - N, 1, :].rearrange("p (k c) -> p k c", k=2), ps[0:J - N, 5:7, 0:HB * N],
                                       ACT.Copy).then_inc(s["EjT_ready1"], 1)
                        act.wait_ge(s["yT_made"], b + 1)
                        act.activation(yT[:], ps[0:D, 7, 0:N], ACT.Copy).then_inc(s["yT_ready"], 1)

                    load_bent(0, 0)
                    load_bent(1, 1)
                    lagged(act, front, back)

                @block.vector
                def _(dve):
                    dve.memset(zero, 0.0).then_inc(s["zero_set"], 1)

                    def front(b, k, early):
                        def chain(i, instruction):
                            signal(dve, instruction, s["dve_step"], 3 * b + i)

                        z3 = z[:].rearrange("p (h n) -> p h n", h=H)
                        dve.wait_ge(bent_in[k], turn(b, k))
                        if not (early and k == 0):
                            dve.wait_ge(s["raised"], b)
                        signal(dve, dve.tensor_tensor(z[:], scores[:, b, :], bent[:, k, :], ALU.add), s["summed"], b + 1)
                        chain(1, dve.tensor_reduce(top[:], z3, AX_X, ALU.max))
                        dve.tensor_tensor(z3, z3, top[:].unsqueeze(2).broadcast_to([N, H, N]), ALU.subtract).then_inc(s["shifted"], 1)
                        dve.wait_ge(s["raised"], b + 1)
                        chain(2, dve.tensor_reduce(total[:], E[:, k, :].rearrange("p (h n) -> p h n", h=H), AX_X, ALU.add))
                        chain(3, dve.reciprocal(inv[:, k, :], total[:]))

                    def back(b, k, early):
                        dve.wait_ge(s["EjT_made0"], b + 1)
                        dve.tensor_copy(EjT[:, 0, :].rearrange("p (k c) -> p k c", k=2), ps[0:N, 3:5, 0:HB * N]).then_inc(s["EjT_ready0"], 1)
                        dve.wait_ge(s["y_made"], b + 1)
                        dve.tensor_tensor(y[:].rearrange("p (h d) -> p h d", h=H), ps[0:N, 2, 0:D].rearrange("p (h d) -> p h d", h=H),
                                          inv[:, k, :].unsqueeze(2).broadcast_to([N, H, DK]), ALU.mult).then_inc(s["y_ready"], 1)
                        dve.wait_ge(s["out_made"], b + 1)
                        signal(dve, dve.tensor_tensor(h[:, b, :], ps[0:N, 7, 128:128 + D], h[:, b, :], ALU.add), s["added"], b + 1)

                    lagged(dve, front, back)


def lstm_experts(nc, h, hT, ps, ident, dram):
    E, K, T = 8, 2, B
    C = K * N
    m_dram = nc.dram_tensor("ls_masks", (T * E * K, N), F32, kind="Internal").ap()
    w_dram = nc.dram_tensor("ls_weights", (T * E * K, N), F32, kind="Internal").ap()

    with Phase(nc, "lr") as ph:
        sb = ph.sb
        w_route, b_route, order = sb("w_route", [D, E]), sb("b_route", [N, E]), sb("order", [N, E])
        logit, pick = sb("logit", [N, T, E]), sb("pick", [N, T, E])
        best, late = sb("best", [N, K, T]), sb("late", [N, T])
        ratio, weight = sb("ratio", [N, T]), sb("weight", [N, K, T])
        mask, wmask = sb("mask", [N, T, E, K]), sb("wmask", [N, T, E, K])
        turned = sb("turned", [128, 2, 4, N])
        names = "consts_in logits_made gap_ready ratio_ready masks_ready turned_made turned_ready stored dve_step".split()
        s = {n: ph.sem(n) for n in names}
        wide = [N, T, E]
        with ph.block() as block:
            @block.sync
            def _(sp):
                sp.dma_start(w_route[:], dram["ls_w_route"]).then_inc(s["consts_in"], 16)
                sp.dma_start(b_route[:], dram["ls_b_route"].partition_broadcast(N)).then_inc(s["consts_in"], 16)
                sp.dma_start(order[:], dram["ls_order"].partition_broadcast(N)).then_inc(s["consts_in"], 16)
                for i, out in enumerate((m_dram, w_dram)):
                    sp.wait_ge(s["turned_ready"], i + 1)
                    sp.dma_start(out.rearrange("(k p) n -> p k n", p=128), turned[:, i]).then_inc(s["stored"], 16)
                sp.wait_ge(s["stored"], 32)

            @block.tensor
            def _(pe):
                pe.wait_ge(s["consts_in"], 48)
                for b in range(T):
                    mm = pe.matmul(ps[0:N, 0, b * E:(b + 1) * E], hT[:, b, :], w_route[:], start=True, stop=True)
                mm.then_inc(s["logits_made"], 1)
                for i, m in enumerate((mask, wmask)):
                    pe.wait_ge(s["masks_ready"], i + 1)
                    for k in range(4):
                        tr = pe.transpose(ps[:, 1 + i, k * N:(k + 1) * N], m[:, 8 * k:8 * k + 8].rearrange("p t e k -> p (t e k)"),
                                          ident[0:N, 0:N])
                    tr.then_inc(s["turned_made"], 1)

            @block.scalar
            def _(act):
                act.wait_ge(s["gap_ready"], 1)
                act.activation(ratio[:], ratio[:], ACT.Exp).then_inc(s["ratio_ready"], 1)
                for i in range(2):
                    act.wait_ge(s["turned_made"], i + 1)
                    act.activation(turned[:, i], ps[:, 1 + i, 0:4 * N].rearrange("p (k n) -> p k n", k=4), ACT.Copy).then_inc(s["turned_ready"], 1)

            @block.vector
            def _(dve):
                steps = Steps(dve, s["dve_step"])
                dve.wait_ge(s["consts_in"], 48)
                dve.wait_ge(s["logits_made"], 1)
                steps.done(dve.tensor_tensor(logit[:], ps[0:N, 0, 0:T * E].rearrange("p (t e) -> p t e", e=E),
                                             b_route[:].unsqueeze(1).broadcast_to(wide), ALU.add))
                for k in range(K):
                    chosen = mask[:, :, :, k]
                    steps.done(dve.tensor_reduce(best[:, k, :], logit[:], AX_X, ALU.max))
                    steps.done(dve.tensor_tensor(pick[:], logit[:], best[:, k, :].unsqueeze(2).broadcast_to(wide), ALU.is_equal))
                    steps.done(dve.tensor_tensor(pick[:], pick[:], order[:].unsqueeze(1).broadcast_to(wide), ALU.mult))
                    steps.done(dve.tensor_reduce(late[:], pick[:], AX_X, ALU.max))
                    steps.done(dve.tensor_tensor(chosen, pick[:], late[:].unsqueeze(2).broadcast_to(wide), ALU.is_equal))
                    if k == 0:
                        steps.done(dve.tensor_scalar(pick[:], chosen, -1e38, None, ALU.mult))
                        steps.done(dve.tensor_tensor(logit[:], logit[:], pick[:], ALU.add))
                dve.tensor_tensor(ratio[:], best[:, 1, :], best[:, 0, :], ALU.subtract).then_inc(s["gap_ready"], 1)
                dve.wait_ge(s["ratio_ready"], 1)
                steps.done(dve.tensor_scalar(late[:], ratio[:], 1.0, None, ALU.add))
                steps.done(dve.reciprocal(weight[:, 0, :], late[:]))
                signal(dve, dve.tensor_tensor(weight[:, 1, :], ratio[:], weight[:, 0, :], ALU.mult), s["masks_ready"], 1)
                for k in range(K):
                    w = dve.tensor_tensor(wmask[:, :, :, k], mask[:, :, :, k], weight[:, k, :].unsqueeze(2).broadcast_to(wide), ALU.mult)
                    if k == 1:
                        w.then_inc(s["masks_ready"], 1)

    with Phase(nc, "ls") as ph:
        sb = ph.sb
        w_in, w_rec = sb("w_in", [D, E, 4, D]), sb("w_rec", [D, E, 4, D])
        bias = sb("bias", [D, E, 4])
        w_out, b_out = sb("w_out", [D, E, D]), sb("b_out", [E * K, D])
        m_all, w_all = sb("m_all", [D, 2, E, C]), sb("w_all", [D, 2, E, C])
        w_row = sb("w_row", [E * K, 2, N])
        xm = sb("xm", [D, 2, E, C])
        state, cell = sb("state", [D, E, C]), sb("cell", [D, E, C])
        gates = sb("gates", [D, 4, 4, C])
        part, fresh, tc = sb("part", [D, C]), sb("fresh", [D, C]), sb("tc", [D, 2, C])
        wh, hc = sb("wh", [D, 2, C]), sb("hc", [D, E, N])
        names = ("consts_in masks_in0 masks_in1 zero_set xm_ready gates_made gates_ready cell_ready tc_ready "
                 "state_ready hc_ready y_made y_added dve_step pool_step").split()
        s = {n: ph.sem(n) for n in names}
        masks_in = (s["masks_in0"], s["masks_in1"])

        def steps_of(engine, step):
            step(0, 0)
            step(1, 1)
            with engine.Fori(2, T - 1, 2) as t:
                step(t, 0)
                step(t + 1, 1)

        def since(t, n):
            return not isinstance(t, int) or t >= n

        with ph.block() as block:
            @block.sync
            def _(sp):
                for tile, name in ((w_in, "ls_w_in"), (w_rec, "ls_w_rec"), (bias, "ls_bias"), (w_out, "ls_w_out"), (b_out, "ls_b_out")):
                    sp.dma_start(tile[:], dram[name]).then_inc(s["consts_in"], 16)
                for t in range(T):
                    k = t % 2
                    if t >= 2:
                        sp.wait_ge(s["xm_ready"], t - 1)
                        sp.wait_ge(s["hc_ready"], E * (t - 1))
                        sp.wait_ge(s["y_made"], t - 1)
                    rows = slice(t * E * K, (t + 1) * E * K)
                    sp.dma_start(m_all[:, k].rearrange("p e c -> p (e c)"),
                                 m_dram[rows, :].rearrange("r n -> (r n)").partition_broadcast(D)).then_inc(masks_in[k], 16)
                    sp.dma_start(w_all[:, k].rearrange("p e c -> p (e c)"),
                                 w_dram[rows, :].rearrange("r n -> (r n)").partition_broadcast(D)).then_inc(masks_in[k], 16)
                    sp.dma_start(w_row[:, k], w_dram[rows, :]).then_inc(masks_in[k], 16)

            @block.gpsimd
            def _(pool):
                def mask_inputs(t, k):
                    pool.wait_ge(masks_in[k], 24 * t - 24 * k + 48)
                    if since(t, 2):
                        pool.wait_ge(s["gates_made"], E * t - E)
                    pool.tensor_tensor(xm[:, k].rearrange("p e (k n) -> p (e k) n", k=K),
                                       hT[:, t, :].unsqueeze(1).broadcast_to([D, E * K, N]),
                                       m_all[:, k].rearrange("p e (k n) -> p (e k) n", k=K), ALU.mult).then_inc(s["xm_ready"], 1)

                def combine(t, k):
                    if since(t, 1):
                        pool.wait_ge(s["y_made"], t)
                    for e in range(E):
                        pool.wait_ge(s["state_ready"], E * t + e + 1)
                        signal(pool, pool.tensor_tensor(wh[:, e % 2], state[:, e], w_all[:, k, e], ALU.mult), s["pool_step"], E * t + e + 1)
                        pool.tensor_tensor(hc[:, e], wh[:, e % 2, 0:N], wh[:, e % 2, N:C], ALU.add).then_inc(s["hc_ready"], 1)

                mask_inputs(0, 0)
                mask_inputs(1, 1)
                combine(0, 0)
                with pool.Fori(1, T - 2, 2) as t:
                    mask_inputs(t + 1, 0)
                    combine(t, 1)
                    mask_inputs(t + 2, 1)
                    combine(t + 1, 0)
                combine(T - 1, 1)

            @block.tensor
            def _(pe):
                def outputs(t, k):
                    pe.wait_ge(s["hc_ready"], E * t + E)
                    if since(t, 1):
                        pe.wait_ge(s["y_added"], t)
                    for e in range(E):
                        pe.matmul(ps[0:N, 7, 0:D], hc[:, e], w_out[:, e, :], start=(e == 0), stop=False)
                    pe.matmul(ps[0:N, 7, 0:D], w_row[:, k], b_out[:], start=False, stop=True).then_inc(s["y_made"], 1)

                def step(t, k):
                    pe.wait_ge(s["xm_ready"], t + 1)
                    for e in range(E):
                        if e >= 3:
                            pe.wait_ge(s["gates_ready"], E * t + e - 2)
                        elif since(t, 1):
                            pe.wait_ge(s["gates_ready"], E * t if e < 2 else E * t - 2)
                        if since(t, 1):
                            pe.wait_ge(s["state_ready"], E * t - E + e + 1)
                        bank = e % 3 * 2
                        for j in range(4):
                            out = ps[:, bank + j // 2, j % 2 * 256:j % 2 * 256 + C]
                            pe.matmul(out, w_in[:, e, j, :], xm[:, k, e], start=True, stop=False)
                            mm = pe.matmul(out, w_rec[:, e, j, :], state[:, e], start=False, stop=True)
                        mm.then_inc(s["gates_made"], 1)
                        if e == 3 and since(t, 1):
                            outputs(t - 1, 1 - k)

                pe.wait_ge(s["consts_in"], 80)
                pe.wait_ge(s["zero_set"], 2)
                steps_of(pe, step)
                outputs(T - 1, 1)

            @block.scalar
            def _(act):
                def cell_tanh(t, e):
                    act.wait_ge(s["cell_ready"], E * t + e + 1)
                    act.activation(tc[:, e % 2], cell[:, e], ACT.Tanh).then_inc(s["tc_ready"], 1)

                def step(t, k):
                    for e in range(E):
                        act.wait_ge(s["gates_made"], E * t + e + 1)
                        if e >= 4 or since(t, 1):
                            act.wait_ge(s["state_ready"], E * t + e - 3)
                        bank = e % 3 * 2
                        view = ps[:, bank:bank + 2, :].rearrange("p k (j c) -> p (k j) c", j=2)
                        for j in range(4):
                            g = act.activation(gates[:, e % 4, j], view[:, j, 0:C], ACT.Tanh if j == 3 else ACT.Sigmoid,
                                               bias=bias[:, e, j:j + 1])
                        g.then_inc(s["gates_ready"], 1)
                        if e:
                            cell_tanh(t, e - 1)
                    cell_tanh(t, E - 1)

                act.wait_ge(s["consts_in"], 80)
                steps_of(act, step)

            @block.vector
            def _(dve):
                def new_state(t, e):
                    dve.wait_ge(s["tc_ready"], E * t + e + 1)
                    if since(t, 1):
                        dve.wait_ge(s["hc_ready"], E * t - E + e + 1)
                    dve.tensor_tensor(state[:, e], gates[:, e % 4, 2], tc[:, e % 2], ALU.mult).then_inc(s["state_ready"], 1)

                def add_outputs(t):
                    dve.wait_ge(s["y_made"], t + 1)
                    dve.tensor_tensor(h[:, t, :], ps[0:N, 7, 0:D], h[:, t, :], ALU.add).then_inc(s["y_added"], 1)

                def step(t, k):
                    for e in range(E):
                        n = 2 * E * t + 2 * e
                        dve.wait_ge(s["gates_ready"], E * t + e + 1)
                        g = gates[:, e % 4]
                        signal(dve, dve.tensor_tensor(part[:], g[:, 1], cell[:, e], ALU.mult), s["dve_step"], n + 1)
                        signal(dve, dve.tensor_tensor(fresh[:], g[:, 0], g[:, 3], ALU.mult), s["dve_step"], n + 2)
                        signal(dve, dve.tensor_tensor(cell[:, e], part[:], fresh[:], ALU.add), s["cell_ready"], E * t + e + 1)
                        if e:
                            new_state(t, e - 1)
                        if e == 5 and since(t, 1):
                            add_outputs(t - 1)
                    new_state(t, E - 1)

                signal(dve, dve.memset(state[:], 0.0), s["zero_set"], 1)
                signal(dve, dve.memset(cell[:], 0.0), s["zero_set"], 2)
                steps_of(dve, step)
                add_outputs(T - 1)



def build(nc, dram, out):
    with ExitStack() as ctx:
        def sb(name, shape):
            return ctx.enter_context(nc.sbuf_tensor(name, shape, F32))

        h = sb("h", [N, B, D])
        hT = sb("hT", [D, B, N])
        ident = sb("ident", [128, 128])
        eps = sb("eps", [128, 1])
        ps = ctx.enter_context(nc.psum_tensor("ps", [128, 8, BANK], F32))
        const_in = ctx.enter_context(nc.semaphore("const_in"))
        eps_set = ctx.enter_context(nc.semaphore("eps_set"))
        with nc.Block() as block:
            @block.sync
            def _(sp):
                sp.dma_start(ident[:], dram["ident"]).then_inc(const_in, 16)
                sp.wait_ge(const_in, 16)

            @block.vector
            def _(dve):
                dve.memset(eps[:], LN_EPS).then_inc(eps_set, 1)
                dve.wait_ge(eps_set, 1)

        tokenize(nc, h, ps, ident, eps, dram)
        norm_and_turn(nc, "la_norm", h, hT, ps, ident, eps)
        logic_attention(nc, h, hT, ps, ident, dram)
        norm_and_turn(nc, "ec_norm", h, hT, ps, ident, eps)
        expert_choice(nc, h, hT, ps, ident, dram)
        norm_and_turn(nc, "ra_norm", h, hT, ps, ident, eps)
        relative_attention(nc, h, hT, ps, ident, dram)
        norm_and_turn(nc, "ls_norm", h, hT, ps, ident, eps)
        lstm_experts(nc, h, hT, ps, ident, dram)
        out_done = ctx.enter_context(nc.semaphore("out_done"))
        with nc.Block() as block:
            @block.sync
            def _(sp):
                sp.dma_start(out.rearrange("b t d -> t b d"), h[:]).then_inc(out_done, 16)
                sp.wait_ge(out_done, 16)


def host_layout(a):
    P = {}
    x = a["x"]
    cells = x.reshape(B, 3, 6, 2, 8, 12, 8)
    v = cells.transpose(3, 4, 6, 1, 0, 2, 5).reshape(128, 3, B * 6, 12)
    P["x_v"] = np.pad(v, ((0, 0), (0, 0), (0, 0), (1, 1)))
    cells = x.reshape(B, 3, 12, 8, 6, 2, 8)
    v = cells.transpose(5, 3, 6, 1, 0, 2, 4).reshape(128, 3, B, 12, 6)
    P["x_h"] = np.pad(v, ((0, 0), (0, 0), (0, 0), (1, 1), (0, 0)))
    wm = a["L0_tok_W_main"].reshape(64, 3, 2, 8, 2, 8)
    wx = a["L0_tok_W_sx"].reshape(16, 3, 2, 8, 2, 8)
    wy = a["L0_tok_W_sy"].reshape(16, 3, 2, 8, 2, 8)
    wv = np.zeros((128, 4, 3, D), np.float32)
    wh = np.zeros((128, 4, 3, D), np.float32)
    for half in range(2):
        vert = lambda w: w[:, :, :, :, half, :].transpose(2, 3, 4, 1, 0).reshape(128, 3, -1)
        horz = lambda w: w[:, :, half].transpose(3, 2, 4, 1, 0).reshape(128, 3, -1)
        wv[:, 1 + half, :, 0:64] = vert(wm)
        wv[:, 2 + half, :, 64:80] = vert(wx)
        wv[:, 0 + half, :, 80:96] = vert(wx)
        wh[:, 2 + half, :, 96:112] = horz(wy)
        wh[:, 0 + half, :, 112:128] = horz(wy)
    P["tok_wv"], P["tok_wh"] = wv, wh
    bx, by = a["L0_tok_b_sx"], a["L0_tok_b_sy"]
    P["tok_bias"] = np.concatenate([a["L0_tok_b_main"], bx, bx, by, by]).reshape(D, 1)
    P["tok_gain"], P["tok_shift"] = a["L0_tok_ln_g"], a["L0_tok_ln_b"]
    P["txt"] = a["txt"]
    P["ident"] = np.eye(128, dtype=np.float32)
    q1, k1, v1 = np.split(a["L0_attn_qkv1_w"], 3, axis=1)
    q2, k2, v2 = np.split(a["L0_attn_qkv2_w"], 3, axis=1)
    stack = lambda *w: np.stack([m.reshape(D, 2, 4, DK) for m in w], axis=3).reshape(D, 2, 128)
    P["la_w_m"], P["la_w_n"] = stack(k1, k2), stack(q1, q2)
    P["la_w_v"] = np.concatenate([v1, v2], axis=1)
    P["la_w_out"] = a["L0_attn_proj_w"]
    row = np.arange(128)
    which, head = row % 32 // DK, row // 32
    P["la_n_mask"] = np.stack([(which == i) & (head == q) for i in range(2) for q in range(4)], 1) * np.float32(DK ** -0.5)
    in_row = np.arange(96)
    P["la_key_hot"] = (in_row[:, None] % 8 == np.arange(8)).astype(np.float32)
    P["la_w1_rows"] = a["L0_attn_conv1_w"].T[in_row // 8 % 6]
    P["la_g_hot"] = (row[:, None] // 16 == np.arange(8)).astype(np.float32)
    P["la_w2_rows"] = a["L0_attn_conv2_w"].T[row % 16]
    P["la_b1"] = a["L0_attn_conv1_b"][row % 16].reshape(128, 1)
    P["la_b2"] = np.tile(a["L0_attn_conv2_b"], (2, 1))
    P["la_chain"] = a["L0_attn_chain_logit"].reshape(1)
    P["ec_w_gate"] = a["L0_ffn_Wg"]
    P["ec_w1"] = a["L0_ffn_W1"].transpose(1, 0, 2)
    P["ec_b1"] = a["L0_ffn_b1"].reshape(8, 2, 128).transpose(2, 0, 1)
    P["ec_w2"] = a["L0_ffn_W2"].reshape(8, 2, 128, D).transpose(2, 0, 1, 3)
    b2 = np.zeros((16, 8, 16, D), np.float32)
    b2[np.arange(16), :, np.arange(16), :] = a["L0_ffn_b2"]
    P["ec_b2"] = b2.reshape(128, 16, D)
    for n, w in (("q", "Wq"), ("k", "Wk"), ("v", "Wv"), ("out", "Wo")):
        P["ra_w_" + n] = a["L1_attn_" + w]
    P["ra_b_q"], P["ra_b_k"] = a["L1_attn_bq"].reshape(D, 1), a["L1_attn_bk"].reshape(D, 1)
    P["ra_b_v"], P["ra_b_out"] = a["L1_attn_bv"], a["L1_attn_bo"]
    far = a["L1_attn_rel_k"].shape[0] // 2
    place = np.clip(np.arange(2 * N - 1) - (N - 1), -far, far) + far
    P["ra_rel_k"] = np.tile(a["L1_attn_rel_k"][place].T, (H, 1))
    rel_v = np.zeros((2 * N, DK), np.float32)
    rel_v[:2 * N - 1] = a["L1_attn_rel_v"][place]
    P["ra_rel_v"] = rel_v.reshape(2, N, DK).transpose(1, 0, 2)
    P["ra_head_mask"] = (np.arange(D)[:, None] // DK == np.arange(H)).astype(np.float32)
    P["ls_w_route"], P["ls_b_route"] = a["L1_ffn_router_w"], a["L1_ffn_router_b"]
    P["ls_order"] = np.arange(8, 0, -1).astype(np.float32)
    gate = [0, 1, 3, 2]
    for n, w in (("in", "Wi"), ("rec", "Wh")):
        P["ls_w_" + n] = a["L1_ffn_" + w].reshape(8, D, 4, D)[:, :, gate].transpose(1, 0, 2, 3)
    P["ls_bias"] = a["L1_ffn_b"].reshape(8, 4, D)[:, gate].transpose(2, 0, 1)
    P["ls_w_out"] = a["L1_ffn_Wo"].transpose(1, 0, 2)
    P["ls_b_out"] = np.repeat(a["L1_ffn_bo"], 2, axis=0)
    return {k: np.ascontiguousarray(v) for k, v in P.items()}


def kernel(**inputs):
    import concourse.bacc as bacc
    from concourse.bass_utils import run_bass_kernel_spmd

    nc = bacc.Bacc("TRN2", target_bir_lowering=False, num_devices=1)
    arrays = host_layout({k: np.asarray(v) for k, v in inputs.items()})
    dram = {k: nc.dram_tensor("in_" + k, v.shape, F32, kind="ExternalInput").ap() for k, v in arrays.items()}
    out = nc.dram_tensor("out_dram", (B, N, D), F32, kind="ExternalOutput").ap()
    build(nc, dram, out)
    r = run_bass_kernel_spmd(nc, [{"in_" + k: v for k, v in arrays.items()}], core_ids=[0])
    return r.results[0]["out_dram"]
```

```python
from contextlib import ExitStack, contextmanager

import numpy as np
import concourse.bass as bass
from concourse import mybir

F32 = mybir.dt.float32
F16 = mybir.dt.float16
ALU = mybir.AluOpType
ACT = mybir.ActivationFunctionType
AX_X = mybir.AxisListType.X

B = 32
NT = 36
TX = 77
N = NT + TX
D = 128
H = 8
DK = D // H
LN_EPS = 1e-5
BANK = 512
HB = 4


class Steps:

    def __init__(self, engine, sem, loop=0, per=0):
        self.engine, self.sem, self.base, self.per, self.n = engine, sem, loop * per, per, 0

    def done(self, instruction):
        instruction.then_inc(self.sem, 1)
        self.n += 1
        self.engine.wait_ge(self.sem, self.base + self.n)

    def close(self):
        assert self.n == self.per, (self.n, self.per)


class Phase:

    def __init__(self, nc, name):
        self.nc, self.name, self.ctx, self.sems = nc, name, ExitStack(), []

    def __enter__(self):
        return self

    def __exit__(self, *args):
        self.nc.clear_and_free_semaphores(self.sems)
        self.nc.all_engine_barrier()
        self.ctx.close()

    def sb(self, name, shape, dtype=F32):
        return self.ctx.enter_context(self.nc.sbuf_tensor(f"{self.name}_{name}", shape, dtype))

    def sem(self, name):
        self.sems.append(self.nc.alloc_semaphore(f"{self.name}_{name}"))
        return self.sems[-1]

    def block(self):
        return self.nc.Block()


def over_banks(ps, bank, banks, parts, width):
    return ps[0:parts, bank:bank + banks, 0:HB * width].rearrange("p k (h n) -> p k h n", h=HB)


def mean_and_rstd(ph, tag, parts):
    return dict(
        stats=ph.sb(f"{tag}_stats", [parts, B, 6]), mean=ph.sb(f"{tag}_mean", [parts, B]),
        diff=ph.sb(f"{tag}_diff", [parts, B]), var=ph.sb(f"{tag}_var", [parts, B]),
        std=ph.sb(f"{tag}_std", [parts, B]), rstd=ph.sb(f"{tag}_rstd", [parts, B]))


def ln_statistics(dve, steps, x, parts, t, var_ready, std_ready, stats_done):
    with dve.Fori(0, B) as b:
        dve.bn_stats(t["stats"][:, b, :], x[0:parts, b, :]).then_inc(stats_done, 1)
    dve.wait_ge(stats_done, B)
    st = t["stats"]
    steps.done(dve.tensor_tensor(t["mean"][:], st[:, :, 1], st[:, :, 4], ALU.add))
    steps.done(dve.tensor_tensor(t["diff"][:], st[:, :, 1], st[:, :, 4], ALU.subtract))
    steps.done(dve.tensor_tensor(t["var"][:], st[:, :, 2], st[:, :, 5], ALU.add))
    steps.done(dve.tensor_tensor(t["diff"][:], t["diff"][:], t["diff"][:], ALU.mult))
    steps.done(dve.tensor_scalar(t["mean"][:], t["mean"][:], 0.5, None, ALU.mult))
    steps.done(dve.tensor_scalar(t["var"][:], t["var"][:], 1.0 / D, None, ALU.mult))
    dve.scalar_tensor_tensor(t["var"][:], t["diff"][:], 0.25, t["var"][:], ALU.mult, ALU.add).then_inc(var_ready, 1)
    dve.wait_ge(std_ready, 1)
    steps.done(dve.reciprocal(t["rstd"][:], t["std"][:]))


def tokenize(nc, h, ps, ident, eps, dram):
    CW = 14
    with Phase(nc, "tok") as ph:
        xv = ph.sb("xv", [128, 3, B * 6, CW])
        xh = ph.sb("xh", [128, 3, B, CW, 6])
        wv = ph.sb("wv", [128, 4, 3, D])
        wh = ph.sb("wh", [128, 4, 3, D])
        bias = ph.sb("bias", [D, 1])
        gain = ph.sb("gain", [NT, D])
        shift = ph.sb("shift", [NT, D])
        tokT = ph.sb("tokT", [D, B * NT])
        tok = ph.sb("tok", [NT, B, D])
        t = mean_and_rstd(ph, "ln", NT)
        loads, txt_in, out_ready, tokT_ready, rows_ready = (ph.sem(s) for s in (
            "loads", "txt_in", "out_ready", "tokT_ready", "rows_ready"))
        var_ready, std_ready, stats_done, dve_step = (ph.sem(s) for s in (
            "var_ready", "std_ready", "stats_done", "dve_step"))
        weights_in = ph.sem("weights_in")
        IB = [11, 11, 10]

        with ph.block() as block:
            @block.sync
            def _(sp):
                sp.dma_start(wv[:], dram["tok_wv"]).then_inc(weights_in, 16)
                sp.dma_start(xv[:], dram["x_v"]).then_inc(loads, 16)
                sp.dma_start(wh[:], dram["tok_wh"]).then_inc(weights_in, 16)
                sp.dma_start(xh[:], dram["x_h"]).then_inc(loads, 16)
                sp.dma_start(bias[:], dram["tok_bias"]).then_inc(weights_in, 16)
                sp.dma_start(gain[:], dram["tok_gain"].partition_broadcast(NT)).then_inc(weights_in, 16)
                sp.dma_start(shift[:], dram["tok_shift"].partition_broadcast(NT)).then_inc(weights_in, 16)
                sp.dma_start(h[NT:N, :, :], dram["txt"].rearrange("b t d -> t b d")).then_inc(txt_in, 16)
                sp.wait_ge(txt_in, 16)

            @block.tensor
            def _(pe):
                pe.wait_ge(weights_in, 80)
                pe.wait_ge(loads, 32)
                b0 = 0
                for k, nb in enumerate(IB):
                    out = ps[:, k, 0:nb * NT]
                    for p in range(4):
                        for c in range(3):
                            pe.matmul(out, wv[:, p, c, :], xv[:, c, 6 * b0:6 * (b0 + nb), p:p + 11:2],
                                      start=(p == 0 and c == 0), stop=False)
                    for p in range(4):
                        for c in range(3):
                            last = pe.matmul(out, wh[:, p, c, :], xh[:, c, b0:b0 + nb, p:p + 11:2, :],
                                             start=False, stop=(p == 3 and c == 2))
                    last.then_inc(out_ready, 1)
                    b0 += nb
                pe.wait_ge(tokT_ready, 3)
                for b in range(B):
                    tr = pe.transpose(ps[0:NT, b // 4, (b % 4) * D:(b % 4 + 1) * D], tokT[:, b * NT:(b + 1) * NT], ident[:])
                    if b % 4 == 3:
                        tr.then_inc(rows_ready, 1)

            @block.scalar
            def _(act):
                b0 = 0
                for k, nb in enumerate(IB):
                    act.wait_ge(out_ready, k + 1)
                    act.activation(tokT[:, b0 * NT:(b0 + nb) * NT], ps[:, k, 0:nb * NT], ACT.Identity,
                                   bias=bias[:]).then_inc(tokT_ready, 1)
                    b0 += nb
                act.wait_ge(var_ready, 1)
                act.activation(t["std"][:], t["var"][:], ACT.Sqrt, bias=eps[0:NT]).then_inc(std_ready, 1)

            @block.vector
            def _(dve):
                steps = Steps(dve, dve_step)
                for k in range(8):
                    dve.wait_ge(rows_ready, k + 1)
                    steps.done(dve.tensor_copy(tok[:, 4 * k:4 * k + 4, :],
                                               ps[0:NT, k, :].rearrange("p (b d) -> p b d", d=D)))
                ln_statistics(dve, steps, tok, NT, t, var_ready, std_ready, stats_done)
                wide = [NT, B, D]
                steps.done(dve.tensor_tensor(tok[:], tok[:], t["mean"][:].unsqueeze(2).broadcast_to(wide), ALU.subtract))
                steps.done(dve.tensor_tensor(tok[:], tok[:], t["rstd"][:].unsqueeze(2).broadcast_to(wide), ALU.mult))
                steps.done(dve.tensor_tensor(tok[:], tok[:], gain[:].unsqueeze(1).broadcast_to(wide), ALU.mult))
                steps.done(dve.tensor_tensor(h[0:NT, :, :], tok[:], shift[:].unsqueeze(1).broadcast_to(wide), ALU.add))


def norm_and_turn(nc, name, h, hT, ps, ident, eps):
    with Phase(nc, name) as ph:
        hn = ph.sb("hn", [N, B, D])
        t = mean_and_rstd(ph, "ln", N)
        var_ready, std_ready, stats_done, dve_step, rows_ready, turned, moved = (ph.sem(s) for s in (
            "var_ready", "std_ready", "stats_done", "dve_step", "rows_ready", "turned", "moved"))
        with ph.block() as block:
            @block.vector
            def _(dve):
                steps = Steps(dve, dve_step)
                ln_statistics(dve, steps, h, N, t, var_ready, std_ready, stats_done)
                for b in range(B):
                    dve.tensor_scalar(hn[:, b, :], h[:, b, :], t["mean"][:, b:b + 1], t["rstd"][:, b:b + 1],
                                      ALU.subtract, ALU.mult).then_inc(rows_ready, 1)

            @block.tensor
            def _(pe):
                for b in range(B):
                    pe.wait_ge(rows_ready, b + 1)
                    tr = pe.transpose(ps[:, b // 4, (b % 4) * N:(b % 4 + 1) * N], hn[:, b, :], ident[0:N, 0:N])
                    if b % 4 == 3:
                        tr.then_inc(turned, 1)

            @block.scalar
            def _(act):
                act.wait_ge(var_ready, 1)
                act.activation(t["std"][:], t["var"][:], ACT.Sqrt, bias=eps[0:N]).then_inc(std_ready, 1)
                for k in range(B // 4):
                    act.wait_ge(turned, k + 1)
                    act.activation(hT[:, 4 * k:4 * k + 4, :], ps[:, k, 0:4 * N].rearrange("p (b n) -> p b n", n=N),
                                   ACT.Copy).then_inc(moved, 1)
                act.wait_ge(moved, B // 4)



def signal(engine, instruction, sem, count):
    instruction.then_inc(sem, 1)
    engine.wait_ge(sem, count)


def logic_attention(nc, h, hT, ps, ident, dram):
    W = H * N
    G = 8
    GROUPS = -(-N // G)
    MP = GROUPS * G
    MAPS, UNITS_H = 6, 16
    ROWS = 2 * MAPS * G
    HALVES = 2 * GROUPS
    UNITS, GATES, X, Y = 0, 2, 4, 6
    IN_ALL = 2 * MAPS * 16
    HT = 4

    with Phase(nc, "la") as ph:
        sb = ph.sb
        w_m, w_n = sb("w_m", [D, 2, 128]), sb("w_n", [D, 2, 128])
        w_v, w_out = sb("w_v", [D, 2 * D]), sb("w_out", [D, D])
        n_mask = sb("n_mask", [128, 2 * HT])
        key_hot, w1_rows = sb("key_hot", [ROWS, G]), sb("w1_rows", [ROWS, UNITS_H])
        g_hot, w2_rows, b1 = sb("g_hot", [128, G]), sb("w2_rows", [128, 4]), sb("b1", [128, 1])
        b2, w_chain = sb("b2", [N, 4]), sb("w_chain", [N, 1])
        one, tiny, zero = (sb(n, [128, 1]) for n in ("one", "tiny", "zero"))
        w1_full = sb("w1_full", [ROWS, G, UNITS_H])
        w1 = sb("w1", [ROWS, 2, G * UNITS_H], F16)
        w2_full = sb("w2_full", [128, G, 4])
        w2 = sb("w2", [128, 2, G, 4], F16)

        xT = sb("xT", [D, N])
        m_side = sb("m_side", [128, 2, N])
        n_side = sb("n_side", [128, 2, N])
        n_map = sb("n_map", [128, 2, HT, 2, N])
        V = sb("V", [N, 2, 2 * D])
        S = [sb(f"S{i}", [N, 2, W]) for i in (1, 2)]
        P = [sb(f"P{i}", [N, W]) for i in (1, 2)]
        PT = [sb(f"PT{i}", [N, W]) for i in (1, 2)]
        top, total, inv = sb("top", [N, 3 * H]), sb("total", [N, 3 * H]), sb("inv", [N, 3 * H])
        Cr, soft = sb("Cr", [N, 2, W]), sb("soft", [N, 2, W])
        absd = sb("absd", [N, W])
        maps = sb("maps", [MP, MAPS, 2, W], F16)
        pairs_in = sb("pairs_in", [ROWS, 2, GROUPS, W], F16)
        hid = sb("hid", [128, 3, HB, N])
        hid_parts = sb("hid_parts", [128, 3, 2, HB, N], F16)
        gate = sb("gate", [N, H, MP, 4])
        mixA, mixB, mixC = sb("mixA", [N, W]), sb("mixB", [N, W]), sb("mixC", [N, W])
        logT = mixA, mixB
        ET, transport, chain = mixC, sb("transport", [N, D]), sb("chain", [N, 2, D])
        y, yT = sb("y", [N, D]), sb("yT", [D, N])

        names = ("consts_in setup act_setup dve_setup xT_ready mn_made m_ready n_ready n_map_ready S1_made S2_made "
                 "S1_ready S2_ready v_made V_ready top_step shifted diff_ready raised norm_step P_ready ST_made "
                 "ST_high PT_made PT_ready CrT_made ClT_made Cr_made Cr_out logT_ready Cr_ready log_step abs_made "
                 "abs_step abs_ready pool_step gate_step transport_made transport_ready chain_made chain_ready pairs_in "
                 "hid_made hid_ready hid_high hid_split gate_made gate_in gate_ready mix_step mix_shifted mix_raised mixT_made ET_ready "
                 "inv_step base_made y_step y_ready yT_made yT_ready out_made added").split()
        s = {n: ph.sem(n) for n in names}
        map_ready = [ph.sem(f"map{c}_ready") for c in range(MAPS)]
        loads = [(w_m, "la_w_m"), (w_n, "la_w_n"), (w_v, "la_w_v"), (w_out, "la_w_out"), (n_mask, "la_n_mask"),
                 (key_hot, "la_key_hot"), (w1_rows, "la_w1_rows"), (g_hot, "la_g_hot"), (w2_rows, "la_w2_rows"),
                 (b1, "la_b1")]
        ALL_IN = 16 * (len(loads) + 2)

        def col(i):
            return slice(i * N, (i + 1) * N)

        def banks(bank, parts=N):
            return ps[0:parts, bank:bank + 2, 0:HB * N]

        def at(bank, hd):
            return ps[0:N, bank + hd // HB, col(hd % HB)]

        def two(tile):
            return tile.rearrange("p (k c) -> p k c", k=2)

        def by_head(tile):
            return tile.rearrange("p (h n) -> p h n", h=H)

        def per_head(stat, width=N):
            return stat.unsqueeze(2).broadcast_to([N, H, width])

        def since(b, n):
            return not isinstance(b, int) or b >= n

        def pipeline(beside, pair_step, last_step):
            def image(b, k, more, before):
                for t in range(HALVES):
                    pair_step(b, k, t)
                    beside(b, k, t, more, before)
                last_step(b)

            for t in range(HALVES):
                beside(-1, 1, t, True, False)
            image(0, 0, True, False)
            return image

        def no_step(*args):
            pass

        def gates_of(g):
            return ps[0:N, GATES + g % 2, :].rearrange("p (h i m c) -> p h i m c", h=H, i=2, m=G)

        with ph.block() as block:
            @block.sync
            def _(sp):
                for tile, name in loads:
                    sp.dma_start(tile[:], dram[name]).then_inc(s["consts_in"], 16)
                sp.dma_start(b2[:], dram["la_b2"].partition_broadcast(N)).then_inc(s["consts_in"], 16)
                sp.dma_start(w_chain[:], dram["la_chain"].partition_broadcast(N)).then_inc(s["consts_in"], 16)
                for b in range(B):
                    if b >= 2:
                        sp.wait_ge(s["hid_made"], HALVES * (b - 1))
                    for c in (2, 3, 0, 1, 4, 5):
                        sp.wait_ge(map_ready[c], b + 1)
                        for part in range(2):
                            row = (part * MAPS + c) * G
                            sp.dma_start(pairs_in[row:row + G, b % 2], maps[:, c, part, :]).then_inc(s["pairs_in"], 16)

            @block.gpsimd
            def _(pool):
                pool.memset(zero[:], 0.0).then_inc(s["setup"], 1)
                pool.memset(maps[:], 0.0).then_inc(s["setup"], 1)
                pool.wait_ge(s["setup"], 2)
                pool.wait_ge(s["consts_in"], ALL_IN)

                def copy(out, x):
                    rows, cols = x.shape
                    return pool.tensor_tensor(out, x, zero[0:rows].broadcast_to([rows, cols]), ALU.add)

                def split(b, k, i):
                    pool.wait_ge(s[f"S{i + 1}_ready"], b + 1)
                    signal(pool, copy(maps[0:N, 2 + i, 0, :], S[i][:, k, :]), s["pool_step"], 2 * b + i + 1)
                    pool.tensor_tensor(maps[0:N, 2 + i, 1, :], S[i][:, k, :], maps[0:N, 2 + i, 0, :],
                                       ALU.subtract).then_inc(map_ready[2 + i], 1)

                def beside(b, k, t, more, before):
                    new, par = b + 1, 1 - k
                    if more and t == 0:
                        if since(new, 1):
                            pool.wait_ge(s["v_made"], new)
                        copy(xT[:], hT[:, new, :]).then_inc(s["xT_ready"], 1)
                    if more and t == 1:
                        pool.wait_ge(s["n_ready"], new + 1)
                        wide = [128, 2 * HT, 2 * N]
                        pool.tensor_tensor(n_map[:].rearrange("p i q t n -> p (i q) (t n)"),
                                           n_side[:].rearrange("p t n -> p (t n)").unsqueeze(1).broadcast_to(wide),
                                           n_mask[:].unsqueeze(2).broadcast_to(wide), ALU.mult).then_inc(s["n_map_ready"], 1)
                    if more and t == 7:
                        if since(new, 1):
                            pool.wait_ge(s["pairs_in"], IN_ALL * new)
                        split(new, par, 0)
                    if more and t == 9:
                        split(new, par, 1)

                def pair_step(b, k, t):
                    pool.wait_ge(s["hid_high"], HALVES * b + t + 1)
                    pool.tensor_tensor(hid_parts[:, t % 3, 1], hid[:, t % 3], hid_parts[:, t % 3, 0],
                                       ALU.subtract).then_inc(s["hid_split"], 1)

                image = pipeline(beside, pair_step, no_step)
                with pool.Fori(1, B - 2, 2) as b:
                    image(b, 1, True, True)
                    image(b + 1, 0, True, True)
                image(B - 1, 1, False, True)

            @block.tensor
            def _(pe):
                def project(b):
                    if since(b, 1):
                        pe.wait_ge(s["Cr_out"], b)
                    for bank, w in ((X, w_m), (X + 1, w_n)):
                        for t in range(2):
                            mm = pe.matmul(ps[:, bank, col(t)], w[:, t, :], hT[:, b, :], start=True, stop=True)
                    mm.then_inc(s["mn_made"], 1)

                def score(b, i):
                    if i == 0:
                        pe.wait_ge(s["m_ready"], b + 1)
                        pe.wait_ge(s["n_map_ready"], b + 1)
                    elif since(b, 1):
                        pe.wait_ge(s["chain_ready"], b)
                    for hd in range(H):
                        mm = pe.matmul(at((X, Y)[i], hd), n_map[:, i, hd % HT, hd // HT, :], m_side[:, hd // HT, :],
                                       start=True, stop=True)
                    mm.then_inc(s[f"S{i + 1}_made"], 1)

                def turn_scores(b, k, i):
                    if i == 0:
                        pe.wait_ge(s["S1_ready"], b + 1)
                    else:
                        pe.wait_ge(s["S2_ready"], b + 1)
                        pe.wait_ge(map_ready[0], b + 1)
                    for hd in range(H):
                        tr = pe.transpose(at(X, hd), S[i][:, k, col(hd)], ident[0:N, 0:N])
                    tr.then_inc(s["ST_made"], 1)

                def turn_softmax(b, i):
                    pe.wait_ge(s["P_ready"], 2 * b + i + 1)
                    if i == 0:
                        pe.wait_ge(map_ready[1], b + 1)
                    else:
                        pe.wait_ge(s["PT_ready"], 2 * b + 1)
                    for hd in range(H):
                        tr = pe.transpose(at(X, hd), P[i][:, col(hd)], ident[0:N, 0:N])
                    tr.then_inc(s["PT_made"], 1)

                def values(b):
                    pe.wait_ge(s["xT_ready"], b + 1)
                    pe.matmul(ps[0:N, Y + 1, 0:2 * D], xT[:], w_v[:], start=True, stop=True).then_inc(s["v_made"], 1)

                def product(bank, left, right, made):
                    for hd in range(H):
                        mm = pe.matmul(at(bank, hd), left[:, col(hd)], right[:, col(hd)], start=True, stop=True)
                    mm.then_inc(s[made], 1)

                def transport_values(b, k):
                    pe.wait_ge(s["logT_ready"], 2 * b + 2)
                    for hd in range(H):
                        mm = pe.matmul(ps[0:N, Y, hd * DK:(hd + 1) * DK], PT[1][:, col(hd)],
                                       V[:, k, D + hd * DK:D + (hd + 1) * DK], start=True, stop=True)
                    mm.then_inc(s["transport_made"], 1)

                def chain_values(b):
                    pe.wait_ge(s["transport_ready"], b + 1)
                    for hd in range(H):
                        mm = pe.matmul(ps[0:N, Y + 1, hd * DK:(hd + 1) * DK], PT[0][:, col(hd)],
                                       transport[:, hd * DK:(hd + 1) * DK], start=True, stop=True)
                    mm.then_inc(s["chain_made"], 1)

                def turn_mix(b):
                    pe.wait_ge(s["mix_raised"], b + 1)
                    for hd in range(H):
                        tr = pe.transpose(at(Y, hd), mixB[:, col(hd)], ident[0:N, 0:N])
                    tr.then_inc(s["mixT_made"], 1)

                def base_values(b, k):
                    pe.wait_ge(s["ET_ready"], b + 1)
                    for hd in range(H):
                        mm = pe.matmul(ps[0:N, Y, hd * DK:(hd + 1) * DK], ET[:, col(hd)],
                                       V[:, k, hd * DK:(hd + 1) * DK], start=True, stop=True)
                    mm.then_inc(s["base_made"], 1)

                def turn_output(b):
                    pe.wait_ge(s["y_ready"], b + 1)
                    pe.transpose(ps[0:D, Y + 1, 0:N], y[:], ident[0:N, 0:N]).then_inc(s["yT_made"], 1)

                def project_output(b):
                    pe.wait_ge(s["yT_ready"], b + 1)
                    pe.matmul(ps[0:N, Y, 256:256 + D], yT[:], w_out[:], start=True, stop=True).then_inc(s["out_made"], 1)

                def beside(b, k, t, more, before):
                    new, old, par = b + 1, b - 1, 1 - k
                    if more:
                        if t == 1:
                            project(new)
                        if t == 4:
                            score(new, 0)
                        if t == 5:
                            score(new, 1)
                        if t == 7:
                            turn_scores(new, par, 0)
                        if t == 10:
                            turn_scores(new, par, 1)
                    if before:
                        if t == 11:
                            if more:
                                pe.wait_ge(s["S2_ready"], new + 1)
                            turn_mix(old)
                        if t == 13:
                            base_values(old, par)
                        if t == 17:
                            turn_output(old)
                        if t == 19:
                            project_output(old)
                    if more:
                        if t == 14:
                            turn_softmax(new, 0)
                        if t == 16:
                            turn_softmax(new, 1)
                        if t == 20:
                            values(new)
                        if t == 18:
                            pe.wait_ge(s["PT_ready"], 2 * new + 2)
                            product(X, P[1], PT[0], "CrT_made")
                        if t == 22:
                            pe.wait_ge(s["V_ready"], new + 1)
                            if before:
                                pe.wait_ge(s["added"], old + 1)
                            product(Y, P[0], PT[1], "ClT_made")
                        if t == 25:
                            pe.wait_ge(s["logT_ready"], 2 * new + 1)
                            product(X, PT[0], P[1], "Cr_made")
                        if t == 25:
                            transport_values(new, par)
                        if t == 27:
                            chain_values(new)

                def gates(b, t):
                    g, half = t // 2, t % 2
                    pe.wait_ge(s["hid_split"], HALVES * b + t + 1)
                    if half == 0 and (g >= 2 or since(b, 1)):
                        pe.wait_ge(s["gate_in"], GROUPS * b + g - 1)
                    for q in range(HB):
                        for part in range(2):
                            mm = pe.matmul(gates_of(g)[:, half * HB + q], hid_parts[:, t % 3, part, q, :], w2[:],
                                           start=(part == 0), stop=(part == 1))
                    mm.then_inc(s["gate_made"], 1)

                def pair_step(b, k, t):
                    g, half = t // 2, t % 2
                    if t == 0:
                        pe.wait_ge(s["pairs_in"], IN_ALL * (b + 1))
                    if t >= 2:
                        pe.wait_ge(s["hid_ready"], HALVES * b + t - 1)
                    for part in range(2):
                        mm = pe.matmul(ps[:, UNITS + half, 0:HB * N], w1[:, part, :],
                                       pairs_in[:, k, g, half * HB * N:(half + 1) * HB * N],
                                       start=(part == 0), stop=(part == 1))
                    mm.then_inc(s["hid_made"], 1)
                    if t >= 2:
                        gates(b, t - 2)

                def last_step(b):
                    gates(b, HALVES - 2)
                    gates(b, HALVES - 1)

                pe.wait_ge(s["consts_in"], ALL_IN)
                pe.wait_ge(s["dve_setup"], 10)
                image = pipeline(beside, pair_step, last_step)
                with pe.Fori(1, B - 2, 2) as b:
                    image(b, 1, True, True)
                    image(b + 1, 0, True, True)
                image(B - 1, 1, False, True)
                for t in range(HALVES):
                    beside(B, 0, t, False, True)

            @block.scalar
            def _(act):
                def keys_side(b):
                    act.wait_ge(s["mn_made"], b + 1)
                    act.activation(m_side[:], ps[:, X, 0:2 * N].rearrange("p (k n) -> p k n", k=2), ACT.Copy).then_inc(s["m_ready"], 1)

                def score(b, k, i):
                    act.wait_ge(s[f"S{i + 1}_made"], b + 1)
                    if i == 0 and since(b, 2):
                        act.wait_ge(s["mix_step"], 7 * (b - 2) + 3)
                    act.activation(two(S[i][:, k]), banks((X, Y)[i]), ACT.Copy).then_inc(s[f"S{i + 1}_ready"], 1)

                def values(b, k):
                    act.wait_ge(s["v_made"], b + 1)
                    act.activation(V[:, k], ps[0:N, Y + 1, 0:2 * D], ACT.Copy).then_inc(s["V_ready"], 1)

                def scores_high(b, i):
                    if i == 0 and since(b, 1):
                        act.wait_ge(s["pairs_in"], IN_ALL * b)
                    act.wait_ge(s["ST_made"], 2 * b + i + 1)
                    act.activation(two(maps[0:N, i, 0, :]), banks(X), ACT.Copy).then_inc(s["ST_high"], 1)

                def open_gates(b, c):
                    act.wait_ge(s["gate_in"], GROUPS * (b + 1))
                    part = gate[:, :, :, c]
                    act.activation(part, part, ACT.Tanh, bias=b2[:, c:c + 1], scale=0.5).then_inc(s["gate_ready"], 1)

                def raise_maps(b):
                    for i in range(2):
                        act.wait_ge(s["shifted"], 2 * b + i + 1)
                        act.activation(P[i][:], P[i][:], ACT.Exp).then_inc(s["raised"], 1)

                def raise_mix(b):
                    act.wait_ge(s["mix_shifted"], b + 1)
                    act.activation(mixB[:], mixA[:], ACT.Exp, scale=0.5).then_inc(s["mix_raised"], 1)

                def raise_difference(b):
                    act.wait_ge(s["abs_made"], b + 1)
                    act.activation(absd[:], absd[:], ACT.Exp, scale=-1.0).then_inc(s["abs_step"], 1)

                def softplus(b):
                    act.wait_ge(s["abs_step"], b + 1)
                    act.activation(absd[:], absd[:], ACT.Ln, bias=one[0:N]).then_inc(s["abs_ready"], 1)

                def log_product(b, k):
                    act.wait_ge(s["Cr_out"], b + 1)
                    act.activation(Cr[:, k], Cr[:, k], ACT.Ln, bias=tiny[0:N]).then_inc(s["Cr_ready"], 1)

                def log_turned(b):
                    for i, made in enumerate(("CrT_made", "ClT_made")):
                        act.wait_ge(s[made], b + 1)
                        act.activation(two(logT[i][:]), banks((X, Y)[i]), ACT.Ln, bias=tiny[0:N]).then_inc(s["logT_ready"], 1)

                def beside(b, k, t, more, before):
                    new, old, par = b + 1, b - 1, 1 - k
                    now = not isinstance(b, int) or 0 <= b < B
                    if before and t < 2:
                        for c in ((0, 2), (1, 3))[t]:
                            open_gates(old, c)
                    if more:
                        if t == 2:
                            keys_side(new)
                        if t == 5:
                            score(new, par, 0)
                        if t == 6:
                            score(new, par, 1)
                        if t == 8:
                            scores_high(new, 0)
                    if t == 10:
                        if more:
                            raise_maps(new)
                        if before:
                            raise_mix(old)
                        if now:
                            raise_difference(b)
                        if more:
                            scores_high(new, 1)
                    if before:
                        if t == 12:
                            act.wait_ge(s["mixT_made"], old + 1)
                            act.activation(two(ET[:]), banks(Y), ACT.Copy).then_inc(s["ET_ready"], 1)
                        if t == 18:
                            act.wait_ge(s["yT_made"], old + 1)
                            act.activation(yT[:], ps[0:D, Y + 1, 0:N], ACT.Copy).then_inc(s["yT_ready"], 1)
                    if more:
                        if t == 15:
                            act.wait_ge(s["PT_made"], 2 * new + 1)
                            act.activation(two(PT[0][:]), banks(X), ACT.Copy).then_inc(s["PT_ready"], 1)
                        if t == 21:
                            values(new, par)
                        if t == 23:
                            log_turned(new)
                    if t == 23 and now:
                        softplus(b)
                        log_product(b, k)

                def pair_step(b, k, t):
                    act.wait_ge(s["hid_made"], HALVES * b + t + 1)
                    if t >= 3 or since(b, 1):
                        act.wait_ge(s["hid_split"], HALVES * b + t - 2)
                    act.activation(hid[:, t % 3].rearrange("p h n -> p (h n)"), ps[:, UNITS + t % 2, 0:HB * N],
                                   ACT.Gelu_apprx_tanh, bias=b1[:]).then_inc(s["hid_ready"], 1)

                act.wait_ge(s["consts_in"], ALL_IN)
                signal(act, act.activation(w_chain[:], w_chain[:], ACT.Tanh, scale=0.5), s["act_setup"], 1)
                act.wait_ge(s["dve_setup"], 10)
                image = pipeline(beside, pair_step, no_step)
                with act.Fori(1, B - 2, 2) as b:
                    image(b, 1, True, True)
                    image(b + 1, 0, True, True)
                image(B - 1, 1, False, True)
                for t in range(HALVES):
                    beside(B, 0, t, False, True)

            @block.vector
            def _(dve):
                def queries_side(b):
                    dve.wait_ge(s["mn_made"], b + 1)
                    if since(b, 1):
                        dve.wait_ge(s["n_map_ready"], b)
                    dve.tensor_copy(n_side[:], ps[:, X + 1, 0:2 * N].rearrange("p (k n) -> p k n", k=2)).then_inc(s["n_ready"], 1)

                def largest(x, i):
                    return dve.tensor_reduce(top[:, H * i:H * i + H], by_head(x), AX_X, ALU.max)

                def shift(x, out, i):
                    return dve.tensor_tensor(by_head(out), by_head(x), per_head(top[:, H * i:H * i + H]), ALU.subtract)

                def score(b, k, i):
                    dve.wait_ge(s[f"S{i + 1}_ready"], b + 1)
                    signal(dve, largest(S[i][:, k], i), s["top_step"], 2 * b + i + 1)
                    shift(S[i][:, k], P[i][:], i).then_inc(s["shifted"], 1)

                def difference(b, k):
                    dve.tensor_tensor(soft[:, k], S[1][:, k], S[0][:, k], ALU.subtract).then_inc(s["diff_ready"], 1)

                def normalize(b, i):
                    dve.wait_ge(s["raised"], 2 * b + i + 1)
                    stat = slice(H * i, H * i + H)
                    signal(dve, dve.tensor_reduce(total[:, stat], by_head(P[i][:]), AX_X, ALU.add), s["norm_step"], 4 * b + 2 * i + 1)
                    signal(dve, dve.reciprocal(inv[:, stat], total[:, stat]), s["norm_step"], 4 * b + 2 * i + 2)
                    dve.tensor_tensor(by_head(P[i][:]), by_head(P[i][:]), per_head(inv[:, stat]), ALU.mult).then_inc(s["P_ready"], 1)

                def scores_low(b, i):
                    dve.wait_ge(s["ST_high"], 2 * b + i + 1)
                    dve.tensor_tensor(two(maps[0:N, i, 1, :]), banks(X), two(maps[0:N, i, 0, :]), ALU.subtract).then_inc(map_ready[i], 1)

                def log_split(b, i):
                    dve.wait_ge(s["logT_ready"], 2 * b + i + 1)
                    signal(dve, dve.tensor_copy(maps[0:N, 4 + i, 0, :], logT[i][:]), s["log_step"], 2 * b + i + 1)
                    dve.tensor_tensor(maps[0:N, 4 + i, 1, :], logT[i][:], maps[0:N, 4 + i, 0, :], ALU.subtract)\
                       .then_inc(map_ready[4 + i], 1)

                def mix(b, k, i):
                    t_and, t_or, t_not, t_chain = (gate[:, :, 0:N, c] for c in range(4))
                    A, Bm, C = (by_head(x[:]) for x in (mixA, mixB, mixC))
                    if i == 1:
                        dve.wait_ge(s["gate_ready"], 4 * b + 2)
                        done = dve.scalar_tensor_tensor(A, t_not, -0.5, t_and, ALU.mult, ALU.add)
                    elif i == 2:
                        done = dve.scalar_tensor_tensor(A, A, 0.5, by_head(S[1][:, k]), ALU.add, ALU.mult)
                    elif i == 3:
                        done = dve.scalar_tensor_tensor(mixA[:], S[0][:, k], 2.0, mixA[:], ALU.mult, ALU.add)
                    elif i == 4:
                        dve.wait_ge(s["gate_ready"], 4 * b + 4)
                        done = dve.scalar_tensor_tensor(Bm, t_or, 1.0, by_head(soft[:, k]), ALU.add, ALU.mult)
                    elif i == 5:
                        dve.wait_ge(s["Cr_ready"], b + 1)
                        done = dve.scalar_tensor_tensor(C, t_chain, 1.0, by_head(Cr[:, k]), ALU.add, ALU.mult)
                    elif i == 6:
                        done = dve.tensor_tensor(mixA[:], mixA[:], mixB[:], ALU.add)
                    else:
                        done = dve.tensor_tensor(mixA[:], mixA[:], mixC[:], ALU.add)
                    signal(dve, done, s["mix_step"], 7 * b + i)

                def mix_shift(b):
                    signal(dve, largest(mixA[:], 2), s["inv_step"], 3 * b + 1)
                    shift(mixA[:], mixA[:], 2).then_inc(s["mix_shifted"], 1)

                def mix_total(b):
                    stat = slice(2 * H, 3 * H)
                    dve.wait_ge(s["mix_raised"], b + 1)
                    signal(dve, dve.tensor_reduce(total[:, stat], by_head(mixB[:]), AX_X, ALU.add), s["inv_step"], 3 * b + 2)
                    signal(dve, dve.reciprocal(inv[:, stat], total[:, stat]), s["inv_step"], 3 * b + 3)

                def attended(b, k):
                    dve.wait_ge(s["base_made"], b + 1)
                    signal(dve, dve.tensor_tensor(y[:].rearrange("p (h d) -> p h d", h=H),
                                                  ps[0:N, Y, 0:D].rearrange("p (h d) -> p h d", h=H),
                                                  per_head(inv[:, 2 * H:3 * H], DK), ALU.mult), s["y_step"], b + 1)
                    dve.tensor_tensor(y[:], y[:], chain[:, k], ALU.add).then_inc(s["y_ready"], 1)

                def add_output(b):
                    dve.wait_ge(s["out_made"], b + 1)
                    dve.tensor_tensor(h[:, b, :], ps[0:N, Y, 256:256 + D], h[:, b, :], ALU.add).then_inc(s["added"], 1)

                def gates_in(b, g):
                    dve.wait_ge(s["gate_made"], HALVES * b + 2 * g + 2)
                    logit = gates_of(g)
                    dve.tensor_copy(gate[:].rearrange("p h (m g) c -> p g h m c", m=G)[:, g], logit[:, :, 0]).then_inc(s["gate_step"], 1)
                    dve.wait_ge(s["gate_step"], GROUPS * b + g + 1)
                    dve.tensor_tensor(gate[:].rearrange("p h (m g) c -> p g h m c", m=G)[:, g],
                                      gate[:].rearrange("p h (m g) c -> p g h m c", m=G)[:, g], logit[:, :, 1],
                                      ALU.add).then_inc(s["gate_in"], 1)

                def beside(b, k, t, more, before):
                    new, old, par = b + 1, b - 1, 1 - k
                    now = not isinstance(b, int) or 0 <= b < B
                    if t == 0 and more:
                        queries_side(new)
                    if t == 0 and now:
                        dve.wait_ge(s["diff_ready"], b + 1)
                        dve.scalar_tensor_tensor(absd[:], soft[:, k], -1.0, soft[:, k], ALU.mult, ALU.max).then_inc(s["abs_made"], 1)
                    if before and 1 <= t <= 4:
                        for i in (2 * t - 1, 2 * t):
                            if i <= 7:
                                mix(old, par, i)
                    if before:
                        if t == 5:
                            mix_shift(old)
                        if t == 14:
                            mix_total(old)
                        if t == 15:
                            attended(old, par)
                        if t == 20:
                            add_output(old)
                    if t == 27 and now:
                        dve.wait_ge(s["abs_ready"], b + 1)
                        dve.scalar_tensor_tensor(soft[:, k], soft[:, k], 0.0, absd[:], ALU.max, ALU.add)
                    if more:
                        if t == 6:
                            score(new, par, 0)
                        if t == 7:
                            score(new, par, 1)
                        if t == 8:
                            scores_low(new, 0)
                        if t == 9:
                            difference(new, par)
                        if t == 11:
                            normalize(new, 0)
                        if t == 12:
                            scores_low(new, 1)
                        if t == 13:
                            normalize(new, 1)
                        if t == 17:
                            dve.wait_ge(s["PT_made"], 2 * new + 2)
                            dve.tensor_copy(two(PT[1][:]), banks(X)).then_inc(s["PT_ready"], 1)
                        if t == 24:
                            log_split(new, 0)
                        if t == 25:
                            log_split(new, 1)
                        if t == 26:
                            dve.wait_ge(s["Cr_made"], new + 1)
                            dve.tensor_copy(two(Cr[:, par]), banks(X)).then_inc(s["Cr_out"], 1)
                            dve.wait_ge(s["transport_made"], new + 1)
                            dve.tensor_copy(transport[:], ps[0:N, Y, 0:D]).then_inc(s["transport_ready"], 1)
                        if t == 28:
                            dve.wait_ge(s["chain_made"], new + 1)
                            dve.tensor_scalar(chain[:, par], ps[0:N, Y + 1, 0:D], w_chain[:], None, ALU.mult).then_inc(s["chain_ready"], 1)

                def pair_step(b, k, t):
                    dve.wait_ge(s["hid_ready"], HALVES * b + t + 1)
                    if t >= 3 or since(b, 1):
                        dve.wait_ge(s["gate_made"], HALVES * b + t - 2)
                    dve.tensor_copy(hid_parts[:, t % 3, 0], hid[:, t % 3]).then_inc(s["hid_high"], 1)
                    if t >= 4 and t % 2 == 0:
                        gates_in(b, t // 2 - 2)

                def last_step(b):
                    gates_in(b, GROUPS - 2)
                    gates_in(b, GROUPS - 1)

                def setup(i, instruction):
                    signal(dve, instruction, s["dve_setup"], i)

                setup(1, dve.memset(one[:], 1.0))
                setup(2, dve.memset(tiny[:], 1e-6))
                dve.wait_ge(s["setup"], 2)
                dve.wait_ge(s["consts_in"], ALL_IN)
                wide = [ROWS, G, UNITS_H]
                setup(3, dve.tensor_tensor(w1_full[:], key_hot[:].unsqueeze(2).broadcast_to(wide),
                                           w1_rows[:].unsqueeze(1).broadcast_to(wide), ALU.mult))
                flat = w1_full[:].rearrange("p g o -> p (g o)")
                setup(4, dve.tensor_copy(w1[:, 0, :], flat))
                setup(5, dve.tensor_tensor(w1[:, 1, :], flat, w1[:, 0, :], ALU.subtract))
                wide = [128, G, 4]
                setup(6, dve.tensor_tensor(w2_full[:], g_hot[:].unsqueeze(2).broadcast_to(wide),
                                           w2_rows[:].unsqueeze(1).broadcast_to(wide), ALU.mult))
                dve.wait_ge(s["act_setup"], 1)
                setup(7, dve.tensor_scalar(w_chain[:], w_chain[:], 0.5, 0.5, ALU.mult, ALU.add))
                setup(8, dve.tensor_scalar(b2[:], b2[:], 0.5, None, ALU.mult))
                setup(9, dve.tensor_copy(w2[:, 0], w2_full[:]))
                setup(10, dve.tensor_tensor(w2[:, 1], w2_full[:], w2[:, 0], ALU.subtract))
                image = pipeline(beside, pair_step, last_step)
                with dve.Fori(1, B - 2, 2) as b:
                    image(b, 1, True, True)
                    image(b + 1, 0, True, True)
                image(B - 1, 1, False, True)
                for t in range(HALVES):
                    beside(B, 0, t, False, True)


def expert_choice(nc, h, hT, ps, ident, dram):
    E, F, TOP = 8, 256, 2 * N // 8
    HALF = B // 2
    Q = 4
    with Phase(nc, "ec") as ph:
        sb = ph.sb
        w_gate = sb("w_gate", [D, E])
        w1, b1 = sb("w1", [D, E, F]), sb("b1", [128, E, 2])
        w2 = sb("w2", [128, E, 2, D])
        b2 = sb("b2", [128, HALF, D])
        gate = sb("gate", [N, B, E])
        peak, total, inv = sb("peak", [N, B]), sb("total", [N, B]), sb("inv", [N, B])
        rows = sb("rows", [128, 2, N])
        left, best = sb("left", [128, 2, N]), sb("best", [128, 2, 4, 8])
        above, equal, rank = sb("above", [128, 2, N]), sb("equal", [128, 2, N]), sb("rank", [128, 2, N])
        room, ones = sb("room", [128, 2]), sb("ones", [128, N])
        hid = sb("hid", [128, 2, 2, Q * N])
        names = ("consts_in scores_made shifted raised gate_ready rows_made rows_ready chosen turned_back "
                 "bias_made hid_made hid_ready out_made added dve_step").split()
        s = {n: ph.sem(n) for n in names}
        wide = [N, B, E]

        with ph.block() as block:
            @block.sync
            def _(sp):
                for tile, name in ((w_gate, "ec_w_gate"), (w1, "ec_w1"), (b1, "ec_b1"), (w2, "ec_w2"), (b2, "ec_b2")):
                    sp.dma_start(tile[:], dram[name]).then_inc(s["consts_in"], 16)

            @block.tensor
            def _(pe):
                pe.wait_ge(s["consts_in"], 80)
                for b in range(B):
                    mm = pe.matmul(ps[0:N, 0, b * E:(b + 1) * E], hT[:, b, :], w_gate[:], start=True, stop=True)
                mm.then_inc(s["scores_made"], 1)
                pe.wait_ge(s["gate_ready"], 1)
                for k in range(2):
                    tr = pe.transpose(ps[:, 1, k * N:(k + 1) * N], gate[:, k * HALF:(k + 1) * HALF, :].rearrange("p b e -> p (b e)"),
                                      ident[0:N, 0:N])
                tr.then_inc(s["rows_made"], 1)
                pe.wait_ge(s["chosen"], 1)
                for k in range(2):
                    tr = pe.transpose(ps[0:N, 0, k * 128:(k + 1) * 128], rows[:, k, :], ident[:])
                tr.then_inc(s["turned_back"], 1)
                for j in range(8):
                    lo = j % 4 * Q
                    if j >= 4:
                        pe.wait_ge(s["added"], j - 3)
                    pe.matmul(ps[0:N, 1 + j % 4, :], rows[:, j // 4, :], b2[:, lo:lo + Q, :].rearrange("p b d -> p (b d)"),
                              start=True, stop=True).then_inc(s["bias_made"], 1)
                pe.wait_ge(s["added"], 8)
                with pe.Fori(0, B // Q) as g:
                    def second(e):
                        pe.wait_ge(s["hid_ready"], 2 * E * g + 2 * e + 2)
                        pe.wait_ge(s["added"], 8 + E * g + e - 1)
                        for i in range(Q):
                            for c in range(2):
                                mm = pe.matmul(ps[0:N, 6 + e % 2, i * D:(i + 1) * D], hid[:, e % 2, c, i * N:(i + 1) * N],
                                               w2[:, e, c, :], start=(c == 0), stop=(c == 1))
                        mm.then_inc(s["out_made"], 1)

                    for e in range(E):
                        for c in range(2):
                            if e >= 2:
                                pe.wait_ge(s["hid_ready"], 2 * E * g + 2 * e + c - 3)
                            pe.matmul(ps[:, 2 + (2 * e + c) % 4, 0:Q * N], w1[:, e, c * 128:(c + 1) * 128],
                                      hT[:, bass.ds(g * Q, Q), :].rearrange("p b n -> p (b n)"),
                                      start=True, stop=True).then_inc(s["hid_made"], 1)
                        if e:
                            second(e - 1)
                    second(E - 1)

            @block.scalar
            def _(act):
                act.wait_ge(s["shifted"], 1)
                act.activation(gate[:], gate[:], ACT.Exp).then_inc(s["raised"], 1)
                with act.Fori(0, B // Q) as g:
                    for e in range(E):
                        for c in range(2):
                            act.wait_ge(s["hid_made"], 2 * E * g + 2 * e + c + 1)
                            if e >= 2:
                                act.wait_ge(s["out_made"], E * g + e - 1)
                            act.activation(hid[:, e % 2, c, :], ps[:, 2 + (2 * e + c) % 4, 0:Q * N], ACT.Gelu,
                                           bias=b1[:, e, c:c + 1]).then_inc(s["hid_ready"], 1)

            @block.vector
            def _(dve):
                steps = Steps(dve, s["dve_step"])
                steps.done(dve.memset(ones[:], 1.0))
                dve.wait_ge(s["scores_made"], 1)
                scores = ps[0:N, 0, 0:B * E].rearrange("p (b e) -> p b e", e=E)
                steps.done(dve.tensor_reduce(peak[:], scores, AX_X, ALU.max))
                dve.tensor_tensor(gate[:], scores, peak[:].unsqueeze(2).broadcast_to(wide), ALU.subtract).then_inc(s["shifted"], 1)
                dve.wait_ge(s["raised"], 1)
                steps.done(dve.tensor_reduce(total[:], gate[:], AX_X, ALU.add))
                steps.done(dve.reciprocal(inv[:], total[:]))
                dve.tensor_tensor(gate[:], gate[:], inv[:].unsqueeze(2).broadcast_to(wide), ALU.mult).then_inc(s["gate_ready"], 1)
                dve.wait_ge(s["rows_made"], 1)
                steps.done(dve.tensor_copy(rows[:], ps[:, 1, 0:2 * N].rearrange("p (k n) -> p k n", k=2)))
                steps.done(dve.tensor_copy(left[:], rows[:]))
                for k in range(2):
                    for r in range(TOP // 8):
                        steps.done(dve.max(best[:, k, r, :], left[:, k, :]))
                        steps.done(dve.match_replace(left[:, k, :], best[:, k, r, :], left[:, k, :], -1.0))
                    steps.done(dve.max(best[:, k, TOP // 8, :], left[:, k, :]))
                    last = best[:, k, TOP // 8, TOP % 8 - 1:TOP % 8]
                    steps.done(dve.tensor_scalar(above[:, k, :], rows[:, k, :], last, None, ALU.is_gt))
                    steps.done(dve.tensor_scalar(equal[:, k, :], rows[:, k, :], last, None, ALU.is_equal))
                    steps.done(dve.tensor_reduce(room[:, k:k + 1], above[:, k, :], AX_X, ALU.add))
                    steps.done(dve.tensor_scalar(room[:, k:k + 1], room[:, k:k + 1], -1.0, float(TOP), ALU.mult, ALU.add))
                    steps.done(dve.tensor_tensor_scan(rank[:, k, :], ones[:], equal[:, k, :], 0.0, ALU.mult, ALU.add))
                    steps.done(dve.scalar_tensor_tensor(equal[:, k, :], rank[:, k, :], room[:, k:k + 1], equal[:, k, :],
                                                        ALU.is_le, ALU.mult))
                    steps.done(dve.tensor_tensor(above[:, k, :], above[:, k, :], equal[:, k, :], ALU.add))
                dve.tensor_tensor(rows[:], rows[:], above[:], ALU.mult).then_inc(s["chosen"], 1)
                dve.wait_ge(s["turned_back"], 1)
                steps.done(dve.tensor_copy(gate[:], ps[0:N, 0, 0:B * E].rearrange("p (b e) -> p b e", e=E)))
                for j in range(8):
                    dve.wait_ge(s["bias_made"], j + 1)
                    part = h[:, Q * j:Q * j + Q, :]
                    signal(dve, dve.tensor_tensor(part, ps[0:N, 1 + j % 4, :].rearrange("p (b d) -> p b d", d=D), part,
                                                  ALU.add), s["added"], j + 1)
                with dve.Fori(0, B // Q) as g:
                    for e in range(E):
                        dve.wait_ge(s["out_made"], E * g + e + 1)
                        for i in range(Q):
                            row = h[:, g * Q + i, :]
                            one = dve.scalar_tensor_tensor(row, ps[0:N, 6 + e % 2, i * D:(i + 1) * D], gate[:, g * Q + i, e:e + 1],
                                                           row, ALU.mult, ALU.add)
                        signal(dve, one, s["added"], 8 + E * g + e + 1)


def relative_attention(nc, h, hT, ps, ident, dram):
    J = 2 * N - 1
    W = H * N
    SCALE = D ** -0.5
    r_dram = nc.dram_tensor("ra_shift_scores", (B, N, H * J), F32, kind="Internal").ap()
    e_dram = nc.dram_tensor("ra_shift_probs", (2, N, H * J), F32, kind="Internal").ap()

    def skewed(dram_ap, i):
        return bass.AP(dram_ap.tensor, i * (N * H * J) + N - 1, [[H * J - 1, N], [J, H], [1, N]])

    with Phase(nc, "ra") as outer:
        scores = outer.sb("scores", [N, B, W])
        V = outer.sb("V", [N, B, D])
        with Phase(nc, "rp") as ph:
            sb = ph.sb
            w_q, w_k, w_v = sb("w_q", [D, D]), sb("w_k", [D, D]), sb("w_v", [D, D])
            b_q, b_k, b_v = sb("b_q", [D, 1]), sb("b_k", [D, 1]), sb("b_v", [N, D])
            rel_k, head_mask = sb("rel_k", [D, J]), sb("head_mask", [D, H])
            b_out = sb("b_out", [N, D])
            xT, qT, kT = sb("xT", [D, N]), sb("qT", [D, N]), sb("kT", [D, N])
            q_head = sb("q_head", [D, H, N])
            shift = sb("shift", [N, 2, 4, 2 * J])
            names = ("consts_in xT_ready q_made k_made qT_ready kT_ready q_head_ready V_ready scores_made "
                     "scores_ready shift_made shift_dve shift_act shift_out0 shift_out1 bias_added").split()
            s = {n: ph.sem(n) for n in names}
            shift_out = (s["shift_out0"], s["shift_out1"])
            loads = [(w_q, "ra_w_q"), (w_k, "ra_w_k"), (w_v, "ra_w_v"), (b_q, "ra_b_q"), (b_k, "ra_b_k"),
                     (rel_k, "ra_rel_k"), (head_mask, "ra_head_mask")]
            rows = [(b_v, "ra_b_v"), (b_out, "ra_b_out")]
            ALL_IN = 16 * (len(loads) + len(rows))
            with ph.block() as block:
                @block.sync
                def _(sp):
                    for tile, name in loads:
                        sp.dma_start(tile[:], dram[name]).then_inc(s["consts_in"], 16)
                    for tile, name in rows:
                        sp.dma_start(tile[:], dram[name].partition_broadcast(N)).then_inc(s["consts_in"], 16)
                    for k in range(2):
                        sp.wait_ge(shift_out[k], 16 * (B // 2))

                @block.gpsimd
                def _(pool):
                    pool.wait_ge(s["consts_in"], ALL_IN)
                    pool.tensor_tensor(h[:], h[:], b_out[:].unsqueeze(1).broadcast_to([N, B, D]), ALU.add).then_inc(s["bias_added"], 1)
                    pool.tensor_copy(xT[:], hT[:, 0, :]).then_inc(s["xT_ready"], 1)
                    with pool.Fori(1, B) as b:
                        pool.wait_ge(s["q_made"], b)
                        pool.tensor_copy(xT[:], hT[:, b, :]).then_inc(s["xT_ready"], 1)

                @block.tensor
                def _(pe):
                    def image(b, first):
                        if not first:
                            pe.wait_ge(s["kT_ready"], b)
                            pe.wait_ge(s["V_ready"], b)
                        pe.matmul(ps[:, 7, 0:N], w_k[:], hT[:, b, :], start=True, stop=True).then_inc(s["k_made"], 1)
                        pe.matmul(ps[:, 0, 0:N], w_q[:], hT[:, b, :], start=True, stop=True)
                        pe.wait_ge(s["xT_ready"], b + 1)
                        pe.matmul(ps[0:N, 0, 128:128 + D], xT[:], w_v[:], start=True, stop=True).then_inc(s["q_made"], 1)
                        pe.wait_ge(s["kT_ready"], b + 1)
                        pe.wait_ge(s["q_head_ready"], b + 1)
                        if not first:
                            pe.wait_ge(s["scores_ready"], b)
                        for hd in range(H):
                            mm = pe.matmul(ps[0:N, 1 + hd // HB, hd % HB * N:(hd % HB + 1) * N], q_head[:, hd, :], kT[:],
                                           start=True, stop=True)
                        mm.then_inc(s["scores_made"], 1)
                        if not first:
                            pe.wait_ge(s["shift_dve"], b)
                            pe.wait_ge(s["shift_act"], b)
                        for hd in range(H):
                            mm = pe.matmul(ps[0:N, 3 + hd // 2, hd % 2 * J:(hd % 2 + 1) * J], q_head[:, hd, :], rel_k[:],
                                           start=True, stop=True)
                            if hd % 4 == 3:
                                mm.then_inc(s["shift_made"], 1)

                    pe.wait_ge(s["consts_in"], ALL_IN)
                    image(0, True)
                    with pe.Fori(1, B) as b:
                        image(b, False)

                @block.scalar
                def _(act):
                    def image(b, k, early):
                        act.wait_ge(s["k_made"], b + 1)
                        if not early or k:
                            act.wait_ge(s["shift_made"], 2 * b)
                        act.activation(kT[:], ps[:, 7, 0:N], ACT.Identity, bias=b_k[:]).then_inc(s["kT_ready"], 1)
                        act.wait_ge(s["scores_made"], b + 1)
                        act.activation(scores[:, b, :].rearrange("p (k c) -> p k c", k=2), ps[0:N, 1:3, 0:HB * N],
                                       ACT.Copy).then_inc(s["scores_ready"], 1)
                        act.wait_ge(s["shift_made"], 2 * b + 2)
                        if not early:
                            act.wait_ge(shift_out[k], 8 * b - 8 * k)
                        act.activation(shift[:, k, 2:4, :], ps[0:N, 5:7, 0:2 * J], ACT.Copy).then_inc(s["shift_act"], 1)
                        act.wait_ge(s["shift_dve"], b + 1)
                        act.wait_ge(s["shift_act"], b + 1)
                        act.dma_start(r_dram[b, :, :], shift[:, k].rearrange("p a c -> p (a c)")).then_inc(shift_out[k], 16)

                    act.wait_ge(s["consts_in"], ALL_IN)
                    image(0, 0, True)
                    image(1, 1, True)
                    with act.Fori(2, B - 1, 2) as b:
                        image(b, 0, False)
                        image(b + 1, 1, False)

                @block.vector
                def _(dve):
                    def image(b, k, early):
                        dve.wait_ge(s["q_made"], b + 1)
                        signal(dve, dve.tensor_scalar(qT[:], ps[:, 0, 0:N], b_q[:], SCALE, ALU.add, ALU.mult), s["qT_ready"], b + 1)
                        if not early or k:
                            dve.wait_ge(s["shift_made"], 2 * b)
                        dve.tensor_tensor(q_head[:], qT[:].unsqueeze(1).broadcast_to([D, H, N]),
                                          head_mask[:].unsqueeze(2).broadcast_to([D, H, N]), ALU.mult).then_inc(s["q_head_ready"], 1)
                        dve.tensor_tensor(V[:, b, :], ps[0:N, 0, 128:128 + D], b_v[:], ALU.add).then_inc(s["V_ready"], 1)
                        dve.wait_ge(s["shift_made"], 2 * b + 1)
                        if not early:
                            dve.wait_ge(shift_out[k], 8 * b - 8 * k)
                        dve.tensor_copy(shift[:, k, 0:2, :], ps[0:N, 3:5, 0:2 * J]).then_inc(s["shift_dve"], 1)

                    dve.wait_ge(s["consts_in"], ALL_IN)
                    image(0, 0, True)
                    image(1, 1, True)
                    with dve.Fori(2, B - 1, 2) as b:
                        image(b, 0, False)
                        image(b + 1, 1, False)

        with Phase(nc, "rv") as ph:
            sb = ph.sb
            w_out, rel_v = sb("w_out", [D, D]), sb("rel_v", [N, 2, DK])
            zero = hT[0:N].rearrange("p b n -> p (b n)")[:, 0:H * J]
            bent = sb("bent", [N, 2, W])
            z = sb("z", [N, W])
            E = sb("E", [N, 2, W])
            Ej = sb("Ej", [N, 2, H * J])
            top, total, inv = sb("top", [N, H]), sb("total", [N, H]), sb("inv", [N, 2, H])
            ET, EjT = sb("ET", [N, W]), sb("EjT", [N, 2, W])
            y, yT = sb("y", [N, D]), sb("yT", [D, N])
            names = ("consts_in zeroed bent_in0 bent_in1 summed shifted raised inv_ready E_out0 E_out1 Ej_in0 Ej_in1 "
                     "ET_made ET_ready EjT_made0 EjT_made1 EjT_ready0 EjT_ready1 y_made y_ready yT_made yT_ready out_made "
                     "added zero_set dve_step").split()
            s = {n: ph.sem(n) for n in names}
            bent_in, E_out, Ej_in = ([s[f"{n}{k}"] for k in range(2)] for n in ("bent_in", "E_out", "Ej_in"))

            def lagged(engine, front, back):
                front(0, 0, True)
                front(1, 1, True)
                back(0, 0, True)
                front(2, 0, False)
                back(1, 1, True)
                with engine.Fori(3, B - 4, 2) as b:
                    front(b, 1, False)
                    back(b - 1, 0, False)
                    front(b + 1, 0, False)
                    back(b, 1, False)
                for b in (B - 3, B - 2, B - 1):
                    front(b, b % 2, False)
                    back(b - 1, 1 - b % 2, False)
                back(B - 1, 1, False)

            def turn(b, k):
                return 8 * b - 8 * k + 16

            with ph.block() as block:
                @block.sync
                def _(sp):
                    sp.dma_start(w_out[:], dram["ra_w_out"]).then_inc(s["consts_in"], 16)
                    sp.dma_start(rel_v[:], dram["ra_rel_v"]).then_inc(s["consts_in"], 16)
                    sp.wait_ge(s["zero_set"], 1)
                    for k in range(2):
                        sp.dma_start(e_dram[k, :, :], zero).then_inc(s["zeroed"], 16)
                    sp.wait_ge(s["zeroed"], 32)

                    def store_and_reload(b, k, early):
                        sp.wait_ge(s["raised"], b + 1)
                        if not early:
                            sp.wait_ge(Ej_in[k], turn(b, k) - 16)
                        sp.dma_start(skewed(e_dram, k), E[:, k, :].rearrange("p (h n) -> p h n", h=H)).then_inc(E_out[k], 16)
                        sp.wait_ge(E_out[k], turn(b, k))
                        if not early:
                            sp.wait_ge(s["EjT_made1"], b - 1)
                        sp.dma_start(Ej[:, k, :], e_dram[k, :, :]).then_inc(Ej_in[k], 16)

                    for b in range(B):
                        store_and_reload(b, b % 2, b < 2)

                @block.tensor
                def _(pe):
                    pe.wait_ge(s["consts_in"], 32)

                    def image(b, k, first):
                        pe.wait_ge(s["raised"], b + 1)
                        for hd in range(H):
                            tr = pe.transpose(ps[0:N, hd // HB, hd % HB * N:(hd % HB + 1) * N], E[:, k, hd * N:(hd + 1) * N],
                                              ident[0:N, 0:N])
                        tr.then_inc(s["ET_made"], 1)
                        pe.wait_ge(Ej_in[k], turn(b, k))
                        for c, lo, hi in ((0, 0, N), (1, N, J)):
                            for hd in range(H):
                                tr = pe.transpose(ps[0:hi - lo, 3 + 2 * c + hd // HB, hd % HB * N:(hd % HB + 1) * N],
                                                  Ej[:, k, hd * J + lo:hd * J + hi], ident[0:N, 0:N])
                            tr.then_inc(s[f"EjT_made{c}"], 1)
                        pe.wait_ge(s["ET_ready"], b + 1)
                        pe.wait_ge(s["EjT_ready0"], b + 1)
                        pe.wait_ge(s["EjT_ready1"], b + 1)
                        for hd in range(H):
                            out = ps[0:N, 2, hd * DK:(hd + 1) * DK]
                            c = slice(hd * N, (hd + 1) * N)
                            pe.matmul(out, ET[:, c], V[:, b, hd * DK:(hd + 1) * DK], start=True, stop=False)
                            pe.matmul(out, EjT[:, 0, c], rel_v[:, 0, :], start=False, stop=False)
                            mm = pe.matmul(out, EjT[0:J - N, 1, c], rel_v[0:J - N, 1, :], start=False, stop=True)
                        mm.then_inc(s["y_made"], 1)
                        pe.wait_ge(s["y_ready"], b + 1)
                        pe.transpose(ps[0:D, 7, 0:N], y[:], ident[0:N, 0:N]).then_inc(s["yT_made"], 1)
                        pe.wait_ge(s["yT_ready"], b + 1)
                        pe.matmul(ps[0:N, 7, 128:128 + D], yT[:], w_out[:], start=True, stop=True).then_inc(s["out_made"], 1)

                    image(0, 0, True)
                    image(1, 1, False)
                    with pe.Fori(2, B - 1, 2) as b:
                        image(b, 0, False)
                        image(b + 1, 1, False)

                @block.scalar
                def _(act):
                    def load_bent(b, k):
                        act.dma_start(bent[:, k, :].rearrange("p (h n) -> p h n", h=H), skewed(r_dram, b)).then_inc(bent_in[k], 16)

                    def front(b, k, early):
                        act.wait_ge(s["shifted"], b + 1)
                        if not early:
                            act.wait_ge(s["ET_made"], b - 1)
                            act.wait_ge(E_out[k], turn(b, k) - 16)
                        act.activation(E[:, k, :], z[:], ACT.Exp).then_inc(s["raised"], 1)
                        if not isinstance(b, int) or b + 2 < B:
                            load_bent(b + 2, k)

                    def back(b, k, early):
                        act.wait_ge(s["ET_made"], b + 1)
                        act.activation(ET[:].rearrange("p (k c) -> p k c", k=2), ps[0:N, 0:2, 0:HB * N], ACT.Copy).then_inc(s["ET_ready"], 1)
                        act.wait_ge(s["EjT_made1"], b + 1)
                        act.activation(EjT[0:J - N, 1, :].rearrange("p (k c) -> p k c", k=2), ps[0:J - N, 5:7, 0:HB * N],
                                       ACT.Copy).then_inc(s["EjT_ready1"], 1)
                        act.wait_ge(s["yT_made"], b + 1)
                        act.activation(yT[:], ps[0:D, 7, 0:N], ACT.Copy).then_inc(s["yT_ready"], 1)

                    load_bent(0, 0)
                    load_bent(1, 1)
                    lagged(act, front, back)

                @block.vector
                def _(dve):
                    dve.memset(zero, 0.0).then_inc(s["zero_set"], 1)

                    def front(b, k, early):
                        def chain(i, instruction):
                            signal(dve, instruction, s["dve_step"], 3 * b + i)

                        z3 = z[:].rearrange("p (h n) -> p h n", h=H)
                        dve.wait_ge(bent_in[k], turn(b, k))
                        if not (early and k == 0):
                            dve.wait_ge(s["raised"], b)
                        signal(dve, dve.tensor_tensor(z[:], scores[:, b, :], bent[:, k, :], ALU.add), s["summed"], b + 1)
                        chain(1, dve.tensor_reduce(top[:], z3, AX_X, ALU.max))
                        dve.tensor_tensor(z3, z3, top[:].unsqueeze(2).broadcast_to([N, H, N]), ALU.subtract).then_inc(s["shifted"], 1)
                        dve.wait_ge(s["raised"], b + 1)
                        chain(2, dve.tensor_reduce(total[:], E[:, k, :].rearrange("p (h n) -> p h n", h=H), AX_X, ALU.add))
                        chain(3, dve.reciprocal(inv[:, k, :], total[:]))

                    def back(b, k, early):
                        dve.wait_ge(s["EjT_made0"], b + 1)
                        dve.tensor_copy(EjT[:, 0, :].rearrange("p (k c) -> p k c", k=2), ps[0:N, 3:5, 0:HB * N]).then_inc(s["EjT_ready0"], 1)
                        dve.wait_ge(s["y_made"], b + 1)
                        dve.tensor_tensor(y[:].rearrange("p (h d) -> p h d", h=H), ps[0:N, 2, 0:D].rearrange("p (h d) -> p h d", h=H),
                                          inv[:, k, :].unsqueeze(2).broadcast_to([N, H, DK]), ALU.mult).then_inc(s["y_ready"], 1)
                        dve.wait_ge(s["out_made"], b + 1)
                        signal(dve, dve.tensor_tensor(h[:, b, :], ps[0:N, 7, 128:128 + D], h[:, b, :], ALU.add), s["added"], b + 1)

                    lagged(dve, front, back)


def lstm_experts(nc, h, hT, ps, ident, dram):
    E, K, T = 8, 2, B
    C = K * N
    PASSES = ((0, 0), (0, 1), (1, 0))
    m_dram = nc.dram_tensor("ls_masks", (T * E * K, N), F32, kind="Internal").ap()
    w_dram = nc.dram_tensor("ls_weights", (T * E * K, N), F32, kind="Internal").ap()

    with Phase(nc, "lr") as ph:
        sb = ph.sb
        w_route, b_route, order = sb("w_route", [D, E]), sb("b_route", [N, E]), sb("order", [N, E])
        logit, pick = sb("logit", [N, T, E]), sb("pick", [N, T, E])
        best, late = sb("best", [N, K, T]), sb("late", [N, T])
        ratio, weight = sb("ratio", [N, T]), sb("weight", [N, K, T])
        mask, wmask = sb("mask", [N, T, E, K]), sb("wmask", [N, T, E, K])
        turned = sb("turned", [128, 2, 4, N])
        names = "consts_in logits_made gap_ready ratio_ready masks_ready turned_made turned_ready stored dve_step".split()
        s = {n: ph.sem(n) for n in names}
        wide = [N, T, E]
        with ph.block() as block:
            @block.sync
            def _(sp):
                sp.dma_start(w_route[:], dram["ls_w_route"]).then_inc(s["consts_in"], 16)
                sp.dma_start(b_route[:], dram["ls_b_route"].partition_broadcast(N)).then_inc(s["consts_in"], 16)
                sp.dma_start(order[:], dram["ls_order"].partition_broadcast(N)).then_inc(s["consts_in"], 16)
                for i, out in enumerate((m_dram, w_dram)):
                    sp.wait_ge(s["turned_ready"], i + 1)
                    sp.dma_start(out.rearrange("(k p) n -> p k n", p=128), turned[:, i]).then_inc(s["stored"], 16)
                sp.wait_ge(s["stored"], 32)

            @block.tensor
            def _(pe):
                pe.wait_ge(s["consts_in"], 48)
                for b in range(T):
                    mm = pe.matmul(ps[0:N, 0, b * E:(b + 1) * E], hT[:, b, :], w_route[:], start=True, stop=True)
                mm.then_inc(s["logits_made"], 1)
                for i, m in enumerate((mask, wmask)):
                    pe.wait_ge(s["masks_ready"], i + 1)
                    for k in range(4):
                        tr = pe.transpose(ps[:, 1 + i, k * N:(k + 1) * N], m[:, 8 * k:8 * k + 8].rearrange("p t e k -> p (t e k)"),
                                          ident[0:N, 0:N])
                    tr.then_inc(s["turned_made"], 1)

            @block.scalar
            def _(act):
                act.wait_ge(s["gap_ready"], 1)
                act.activation(ratio[:], ratio[:], ACT.Exp).then_inc(s["ratio_ready"], 1)
                for i in range(2):
                    act.wait_ge(s["turned_made"], i + 1)
                    act.activation(turned[:, i], ps[:, 1 + i, 0:4 * N].rearrange("p (k n) -> p k n", k=4), ACT.Copy).then_inc(s["turned_ready"], 1)

            @block.vector
            def _(dve):
                steps = Steps(dve, s["dve_step"])
                dve.wait_ge(s["consts_in"], 48)
                dve.wait_ge(s["logits_made"], 1)
                steps.done(dve.tensor_tensor(logit[:], ps[0:N, 0, 0:T * E].rearrange("p (t e) -> p t e", e=E),
                                             b_route[:].unsqueeze(1).broadcast_to(wide), ALU.add))
                for k in range(K):
                    chosen = mask[:, :, :, k]
                    steps.done(dve.tensor_reduce(best[:, k, :], logit[:], AX_X, ALU.max))
                    steps.done(dve.tensor_tensor(pick[:], logit[:], best[:, k, :].unsqueeze(2).broadcast_to(wide), ALU.is_equal))
                    steps.done(dve.tensor_tensor(pick[:], pick[:], order[:].unsqueeze(1).broadcast_to(wide), ALU.mult))
                    steps.done(dve.tensor_reduce(late[:], pick[:], AX_X, ALU.max))
                    steps.done(dve.tensor_tensor(chosen, pick[:], late[:].unsqueeze(2).broadcast_to(wide), ALU.is_equal))
                    if k == 0:
                        steps.done(dve.tensor_scalar(pick[:], chosen, -1e38, None, ALU.mult))
                        steps.done(dve.tensor_tensor(logit[:], logit[:], pick[:], ALU.add))
                dve.tensor_tensor(ratio[:], best[:, 1, :], best[:, 0, :], ALU.subtract).then_inc(s["gap_ready"], 1)
                dve.wait_ge(s["ratio_ready"], 1)
                steps.done(dve.tensor_scalar(late[:], ratio[:], 1.0, None, ALU.add))
                steps.done(dve.reciprocal(weight[:, 0, :], late[:]))
                signal(dve, dve.tensor_tensor(weight[:, 1, :], ratio[:], weight[:, 0, :], ALU.mult), s["masks_ready"], 1)
                for k in range(K):
                    w = dve.tensor_tensor(wmask[:, :, :, k], mask[:, :, :, k], weight[:, k, :].unsqueeze(2).broadcast_to(wide), ALU.mult)
                    if k == 1:
                        w.then_inc(s["masks_ready"], 1)

    with Phase(nc, "ls") as ph:
        sb = ph.sb
        w_in, w_rec = sb("w_in", [D, E, 4, D]), sb("w_rec", [D, E, 4, D])
        bias = sb("bias", [D, E, 4])
        w_out, b_out = sb("w_out", [D, E, D]), sb("b_out", [E * K, D])
        m_all, w_all = sb("m_all", [D, 2, E, C]), sb("w_all", [D, 2, E, C])
        w_row = sb("w_row", [E * K, 2, N])
        w_in_parts, w_rec_parts = sb("w_in_parts", [D, 2, E, 4, D], F16), sb("w_rec_parts", [D, 2, E, 4, D], F16)
        hT_parts = sb("hT_parts", [D, B, 2, N], F16)
        xm = sb("xm", [D, 2, E, K, 2, N], F16)
        state, cell = sb("state", [D, E, C]), sb("cell", [D, E, C])
        state_parts = sb("state_parts", [D, 2, E, C], F16)
        gates = sb("gates", [D, 4, 4, C])
        part, fresh, tc = sb("part", [D, C]), sb("fresh", [D, C]), sb("tc", [D, 2, C])
        wh, hc = sb("wh", [D, 2, C]), sb("hc", [D, E, N])
        names = ("consts_in split_in split_rec high_step state_split choices_in0 choices_in1 weights_in0 weights_in1 zero_set xm_ready gates_made gates_ready cell_ready tc_ready "
                 "state_ready hc_ready y_made y_added dve_step pool_step").split()
        s = {n: ph.sem(n) for n in names}
        choices_in, weights_in = ([s[f"{n}_in{k}"] for k in range(2)] for n in ("choices", "weights"))

        def steps_of(engine, step):
            step(0, 0)
            step(1, 1)
            with engine.Fori(2, T - 1, 2) as t:
                step(t, 0)
                step(t + 1, 1)

        def since(t, n):
            return not isinstance(t, int) or t >= n

        with ph.block() as block:
            @block.sync
            def _(sp):
                for tile, name in ((w_in, "ls_w_in"), (w_rec, "ls_w_rec"), (bias, "ls_bias"), (w_out, "ls_w_out"), (b_out, "ls_b_out")):
                    sp.dma_start(tile[:], dram[name]).then_inc(s["consts_in"], 16)
                for t in range(T):
                    k = t % 2
                    rows = slice(t * E * K, (t + 1) * E * K)
                    if t >= 2:
                        sp.wait_ge(s["xm_ready"], 2 * (t - 1))
                    sp.dma_start(m_all[:, k].rearrange("p e c -> p (e c)"),
                                 m_dram[rows, :].rearrange("r n -> (r n)").partition_broadcast(D)).then_inc(choices_in[k], 16)
                    if t >= 2:
                        sp.wait_ge(s["hc_ready"], E * (t - 1))
                        sp.wait_ge(s["y_made"], t - 1)
                    sp.dma_start(w_all[:, k].rearrange("p e c -> p (e c)"),
                                 w_dram[rows, :].rearrange("r n -> (r n)").partition_broadcast(D)).then_inc(weights_in[k], 16)
                    sp.dma_start(w_row[:, k], w_dram[rows, :]).then_inc(weights_in[k], 16)

            @block.gpsimd
            def _(pool):
                def mask_inputs(t, k):
                    pool.wait_ge(choices_in[k], 8 * t - 8 * k + 16)
                    if since(t, 2):
                        pool.wait_ge(s["gates_made"], E * t - E)
                    mask = m_all[:, k].rearrange("p e (k n) -> p (e k) n", k=K)
                    for part in range(2):
                        pool.tensor_tensor(xm[:, k, :, :, part, :].rearrange("p e k n -> p (e k) n"),
                                           hT_parts[:, t, part, :].unsqueeze(1).broadcast_to([D, E * K, N]),
                                           mask, ALU.mult).then_inc(s["xm_ready"], 1)

                def combine(t, k):
                    if since(t, 1):
                        pool.wait_ge(s["y_made"], t)
                    pool.wait_ge(weights_in[k], 16 * t - 16 * k + 32)
                    for e in range(E):
                        pool.wait_ge(s["state_ready"], E * t + e + 1)
                        signal(pool, pool.tensor_tensor(wh[:, e % 2], state[:, e], w_all[:, k, e], ALU.mult), s["pool_step"], E * t + e + 1)
                        pool.tensor_tensor(hc[:, e], wh[:, e % 2, 0:N], wh[:, e % 2, N:C], ALU.add).then_inc(s["hc_ready"], 1)

                pool.wait_ge(s["consts_in"], 80)
                signal(pool, pool.tensor_copy(w_rec_parts[:, 0], w_rec[:]), s["split_rec"], 1)
                pool.tensor_tensor(w_rec_parts[:, 1], w_rec[:], w_rec_parts[:, 0], ALU.subtract).then_inc(s["split_rec"], 1)
                pool.wait_ge(s["split_in"], 2)
                mask_inputs(0, 0)
                mask_inputs(1, 1)
                combine(0, 0)
                with pool.Fori(1, T - 2, 2) as t:
                    mask_inputs(t + 1, 0)
                    combine(t, 1)
                    mask_inputs(t + 2, 1)
                    combine(t + 1, 0)
                combine(T - 1, 1)

            @block.tensor
            def _(pe):
                def outputs(t, k):
                    pe.wait_ge(s["hc_ready"], E * t + E)
                    if since(t, 1):
                        pe.wait_ge(s["y_added"], t)
                    for e in range(E):
                        pe.matmul(ps[0:N, 7, 0:D], hc[:, e], w_out[:, e, :], start=(e == 0), stop=False)
                    pe.matmul(ps[0:N, 7, 0:D], w_row[:, k], b_out[:], start=False, stop=True).then_inc(s["y_made"], 1)

                def step(t, k):
                    pe.wait_ge(s["xm_ready"], 2 * t + 2)
                    for e in range(E):
                        if e >= 3:
                            pe.wait_ge(s["gates_ready"], E * t + e - 2)
                        elif since(t, 1):
                            pe.wait_ge(s["gates_ready"], E * t if e < 2 else E * t - 2)
                        if since(t, 1):
                            pe.wait_ge(s["state_split"], E * t - E + e + 1)
                        bank = e % 3 * 2
                        for j in range(4):
                            out = ps[:, bank + j // 2, j % 2 * 256:j % 2 * 256 + C]
                            for w, x in PASSES:
                                pe.matmul(out, w_in_parts[:, w, e, j, :], xm[:, k, e, :, x, :], start=((w, x) == PASSES[0]), stop=False)
                            for w, x in PASSES:
                                mm = pe.matmul(out, w_rec_parts[:, w, e, j, :], state_parts[:, x, e], start=False,
                                               stop=((w, x) == PASSES[-1]))
                        mm.then_inc(s["gates_made"], 1)
                        if e == 3 and since(t, 1):
                            outputs(t - 1, 1 - k)

                pe.wait_ge(s["consts_in"], 80)
                pe.wait_ge(s["zero_set"], 3)
                pe.wait_ge(s["split_in"], 4)
                pe.wait_ge(s["split_rec"], 2)
                steps_of(pe, step)
                outputs(T - 1, 1)

            @block.scalar
            def _(act):
                def cell_tanh(t, e):
                    act.wait_ge(s["cell_ready"], E * t + e + 1)
                    act.activation(tc[:, e % 2], cell[:, e], ACT.Tanh).then_inc(s["tc_ready"], 1)

                def step(t, k):
                    for e in range(E):
                        act.wait_ge(s["gates_made"], E * t + e + 1)
                        if e >= 4 or since(t, 1):
                            act.wait_ge(s["state_ready"], E * t + e - 3)
                        bank = e % 3 * 2
                        view = ps[:, bank:bank + 2, :].rearrange("p k (j c) -> p (k j) c", j=2)
                        for j in range(4):
                            g = act.activation(gates[:, e % 4, j], view[:, j, 0:C], ACT.Tanh if j == 3 else ACT.Sigmoid,
                                               bias=bias[:, e, j:j + 1])
                        g.then_inc(s["gates_ready"], 1)
                        if e:
                            cell_tanh(t, e - 1)
                    cell_tanh(t, E - 1)

                act.wait_ge(s["consts_in"], 80)
                steps_of(act, step)

            @block.vector
            def _(dve):
                def new_state(t, e):
                    dve.wait_ge(s["tc_ready"], E * t + e + 1)
                    if since(t, 1):
                        dve.wait_ge(s["hc_ready"], E * t - E + e + 1)
                    signal(dve, dve.tensor_tensor(state[:, e], gates[:, e % 4, 2], tc[:, e % 2], ALU.mult), s["state_ready"], E * t + e + 1)
                    signal(dve, dve.tensor_copy(state_parts[:, 0, e], state[:, e]), s["high_step"], E * t + e + 1)
                    dve.tensor_tensor(state_parts[:, 1, e], state[:, e], state_parts[:, 0, e], ALU.subtract).then_inc(s["state_split"], 1)

                def add_outputs(t):
                    dve.wait_ge(s["y_made"], t + 1)
                    dve.tensor_tensor(h[:, t, :], ps[0:N, 7, 0:D], h[:, t, :], ALU.add).then_inc(s["y_added"], 1)

                def step(t, k):
                    for e in range(E):
                        n = 2 * E * t + 2 * e
                        dve.wait_ge(s["gates_ready"], E * t + e + 1)
                        g = gates[:, e % 4]
                        signal(dve, dve.tensor_tensor(part[:], g[:, 1], cell[:, e], ALU.mult), s["dve_step"], n + 1)
                        signal(dve, dve.tensor_tensor(fresh[:], g[:, 0], g[:, 3], ALU.mult), s["dve_step"], n + 2)
                        signal(dve, dve.tensor_tensor(cell[:, e], part[:], fresh[:], ALU.add), s["cell_ready"], E * t + e + 1)
                        if e:
                            new_state(t, e - 1)
                        if e == 5 and since(t, 1):
                            add_outputs(t - 1)
                    new_state(t, E - 1)

                signal(dve, dve.memset(state[:], 0.0), s["zero_set"], 1)
                signal(dve, dve.memset(cell[:], 0.0), s["zero_set"], 2)
                signal(dve, dve.memset(state_parts[:], 0.0), s["zero_set"], 3)
                by_part = hT_parts[:].rearrange("p b i n -> p i b n")
                signal(dve, dve.tensor_copy(by_part[:, 0], hT[:]), s["split_in"], 1)
                signal(dve, dve.tensor_tensor(by_part[:, 1], hT[:], by_part[:, 0], ALU.subtract), s["split_in"], 2)
                dve.wait_ge(s["consts_in"], 80)
                signal(dve, dve.tensor_copy(w_in_parts[:, 0], w_in[:]), s["split_in"], 3)
                signal(dve, dve.tensor_tensor(w_in_parts[:, 1], w_in[:], w_in_parts[:, 0], ALU.subtract), s["split_in"], 4)
                steps_of(dve, step)
                add_outputs(T - 1)



def build(nc, dram, out):
    with ExitStack() as ctx:
        def sb(name, shape):
            return ctx.enter_context(nc.sbuf_tensor(name, shape, F32))

        h = sb("h", [N, B, D])
        hT = sb("hT", [D, B, N])
        ident = sb("ident", [128, 128])
        eps = sb("eps", [128, 1])
        ps = ctx.enter_context(nc.psum_tensor("ps", [128, 8, BANK], F32))
        const_in = ctx.enter_context(nc.semaphore("const_in"))
        eps_set = ctx.enter_context(nc.semaphore("eps_set"))
        with nc.Block() as block:
            @block.sync
            def _(sp):
                sp.dma_start(ident[:], dram["ident"]).then_inc(const_in, 16)
                sp.wait_ge(const_in, 16)

            @block.vector
            def _(dve):
                dve.memset(eps[:], LN_EPS).then_inc(eps_set, 1)
                dve.wait_ge(eps_set, 1)

        tokenize(nc, h, ps, ident, eps, dram)
        norm_and_turn(nc, "la_norm", h, hT, ps, ident, eps)
        logic_attention(nc, h, hT, ps, ident, dram)
        norm_and_turn(nc, "ec_norm", h, hT, ps, ident, eps)
        expert_choice(nc, h, hT, ps, ident, dram)
        norm_and_turn(nc, "ra_norm", h, hT, ps, ident, eps)
        relative_attention(nc, h, hT, ps, ident, dram)
        norm_and_turn(nc, "ls_norm", h, hT, ps, ident, eps)
        lstm_experts(nc, h, hT, ps, ident, dram)
        out_done = ctx.enter_context(nc.semaphore("out_done"))
        with nc.Block() as block:
            @block.sync
            def _(sp):
                sp.dma_start(out.rearrange("b t d -> t b d"), h[:]).then_inc(out_done, 16)
                sp.wait_ge(out_done, 16)


def host_layout(a):
    P = {}
    x = a["x"]
    cells = x.reshape(B, 3, 6, 2, 8, 12, 8)
    v = cells.transpose(3, 4, 6, 1, 0, 2, 5).reshape(128, 3, B * 6, 12)
    P["x_v"] = np.pad(v, ((0, 0), (0, 0), (0, 0), (1, 1)))
    cells = x.reshape(B, 3, 12, 8, 6, 2, 8)
    v = cells.transpose(5, 3, 6, 1, 0, 2, 4).reshape(128, 3, B, 12, 6)
    P["x_h"] = np.pad(v, ((0, 0), (0, 0), (0, 0), (1, 1), (0, 0)))
    wm = a["L0_tok_W_main"].reshape(64, 3, 2, 8, 2, 8)
    wx = a["L0_tok_W_sx"].reshape(16, 3, 2, 8, 2, 8)
    wy = a["L0_tok_W_sy"].reshape(16, 3, 2, 8, 2, 8)
    wv = np.zeros((128, 4, 3, D), np.float32)
    wh = np.zeros((128, 4, 3, D), np.float32)
    for half in range(2):
        vert = lambda w: w[:, :, :, :, half, :].transpose(2, 3, 4, 1, 0).reshape(128, 3, -1)
        horz = lambda w: w[:, :, half].transpose(3, 2, 4, 1, 0).reshape(128, 3, -1)
        wv[:, 1 + half, :, 0:64] = vert(wm)
        wv[:, 2 + half, :, 64:80] = vert(wx)
        wv[:, 0 + half, :, 80:96] = vert(wx)
        wh[:, 2 + half, :, 96:112] = horz(wy)
        wh[:, 0 + half, :, 112:128] = horz(wy)
    P["tok_wv"], P["tok_wh"] = wv, wh
    bx, by = a["L0_tok_b_sx"], a["L0_tok_b_sy"]
    P["tok_bias"] = np.concatenate([a["L0_tok_b_main"], bx, bx, by, by]).reshape(D, 1)
    P["tok_gain"], P["tok_shift"] = a["L0_tok_ln_g"], a["L0_tok_ln_b"]
    P["txt"] = a["txt"]
    P["ident"] = np.eye(128, dtype=np.float32)
    q1, k1, v1 = np.split(a["L0_attn_qkv1_w"], 3, axis=1)
    q2, k2, v2 = np.split(a["L0_attn_qkv2_w"], 3, axis=1)
    stack = lambda *w: np.stack([m.reshape(D, 2, 4, DK) for m in w], axis=3).reshape(D, 2, 128)
    P["la_w_m"], P["la_w_n"] = stack(k1, k2), stack(q1, q2)
    P["la_w_v"] = np.concatenate([v1, v2], axis=1)
    P["la_w_out"] = a["L0_attn_proj_w"]
    row = np.arange(128)
    which, head = row % 32 // DK, row // 32
    P["la_n_mask"] = np.stack([(which == i) & (head == q) for i in range(2) for q in range(4)], 1) * np.float32(DK ** -0.5)
    in_row = np.arange(96)
    P["la_key_hot"] = (in_row[:, None] % 8 == np.arange(8)).astype(np.float32)
    P["la_w1_rows"] = a["L0_attn_conv1_w"].T[in_row // 8 % 6]
    P["la_g_hot"] = (row[:, None] // 16 == np.arange(8)).astype(np.float32)
    P["la_w2_rows"] = a["L0_attn_conv2_w"].T[row % 16]
    P["la_b1"] = a["L0_attn_conv1_b"][row % 16].reshape(128, 1)
    P["la_b2"] = a["L0_attn_conv2_b"]
    P["la_chain"] = a["L0_attn_chain_logit"].reshape(1)
    P["ec_w_gate"] = a["L0_ffn_Wg"]
    P["ec_w1"] = a["L0_ffn_W1"].transpose(1, 0, 2)
    P["ec_b1"] = a["L0_ffn_b1"].reshape(8, 2, 128).transpose(2, 0, 1)
    P["ec_w2"] = a["L0_ffn_W2"].reshape(8, 2, 128, D).transpose(2, 0, 1, 3)
    b2 = np.zeros((16, 8, 16, D), np.float32)
    b2[np.arange(16), :, np.arange(16), :] = a["L0_ffn_b2"]
    P["ec_b2"] = b2.reshape(128, 16, D)
    for n, w in (("q", "Wq"), ("k", "Wk"), ("v", "Wv"), ("out", "Wo")):
        P["ra_w_" + n] = a["L1_attn_" + w]
    P["ra_b_q"], P["ra_b_k"] = a["L1_attn_bq"].reshape(D, 1), a["L1_attn_bk"].reshape(D, 1)
    P["ra_b_v"], P["ra_b_out"] = a["L1_attn_bv"], a["L1_attn_bo"]
    far = a["L1_attn_rel_k"].shape[0] // 2
    place = np.clip(np.arange(2 * N - 1) - (N - 1), -far, far) + far
    P["ra_rel_k"] = np.tile(a["L1_attn_rel_k"][place].T, (H, 1))
    rel_v = np.zeros((2 * N, DK), np.float32)
    rel_v[:2 * N - 1] = a["L1_attn_rel_v"][place]
    P["ra_rel_v"] = rel_v.reshape(2, N, DK).transpose(1, 0, 2)
    P["ra_head_mask"] = (np.arange(D)[:, None] // DK == np.arange(H)).astype(np.float32)
    P["ls_w_route"], P["ls_b_route"] = a["L1_ffn_router_w"], a["L1_ffn_router_b"]
    P["ls_order"] = np.arange(8, 0, -1).astype(np.float32)
    gate = [0, 1, 3, 2]
    for n, w in (("in", "Wi"), ("rec", "Wh")):
        P["ls_w_" + n] = a["L1_ffn_" + w].reshape(8, D, 4, D)[:, :, gate].transpose(1, 0, 2, 3)
    P["ls_bias"] = a["L1_ffn_b"].reshape(8, 4, D)[:, gate].transpose(2, 0, 1)
    P["ls_w_out"] = a["L1_ffn_Wo"].transpose(1, 0, 2)
    P["ls_b_out"] = np.repeat(a["L1_ffn_bo"], 2, axis=0)
    return {k: np.ascontiguousarray(v) for k, v in P.items()}


def kernel(**inputs):
    import concourse.bacc as bacc
    from concourse.bass_utils import run_bass_kernel_spmd

    nc = bacc.Bacc("TRN2", target_bir_lowering=False, num_devices=1)
    arrays = host_layout({k: np.asarray(v) for k, v in inputs.items()})
    dram = {k: nc.dram_tensor("in_" + k, v.shape, F32, kind="ExternalInput").ap() for k, v in arrays.items()}
    out = nc.dram_tensor("out_dram", (B, N, D), F32, kind="ExternalOutput").ap()
    build(nc, dram, out)
    r = run_bass_kernel_spmd(nc, [{"in_" + k: v for k, v in arrays.items()}], core_ids=[0])
    return r.results[0]["out_dram"]
```
